# Optimizing a Trainium2 kernel written in Bass

```python
import numpy as np
import jax
import jax.numpy as jnp

def _softmax(x, axis=-1):
    return jax.nn.softmax(x, axis=axis)

def _gelu(x):
    return jax.nn.gelu(x, approximate=True)

def _silu(x):
    return jax.nn.silu(x)

def _sigmoid(x):
    return jax.nn.sigmoid(x)

def _layernorm(x, axis=-1, eps=1e-05):
    m = jnp.mean(x, axis=axis, keepdims=True)
    v = jnp.var(x, axis=axis, keepdims=True)
    return (x - m) / jnp.sqrt(v + eps)

def _scatter_add(tgt, idx, src, axis=0):
    return tgt.at[idx].add(src)

def _segment_sum(src, seg, n):
    return jax.ops.segment_sum(src, seg, n)
kernel_name = 'mk_gnn_preln_d4_gnn_r32_599a65'

def setup_inputs(seed: int=0):
    np.random.seed(seed)
    _w = jnp.asarray

    def _rec_inputs():
        import jax
        import jax.numpy as jnp
        _gk = jax.random.key(seed)
        x = -0.000202 + 1 * jax.random.normal(jax.random.fold_in(_gk, 1), (3125, 128), jnp.float32)
        src = jax.random.randint(jax.random.fold_in(_gk, 2), (50000,), 0, 3125, jnp.int32)
        dst = jax.random.randint(jax.random.fold_in(_gk, 3), (50000,), 0, 3125, jnp.int32)
        _o = jnp.argsort(dst, stable=True)
        src = src[_o]
        dst = dst[_o]
        edge_attr_16 = 0.000254156 + 0.999948 * jax.random.normal(jax.random.fold_in(_gk, 13), (50000, 16), jnp.float32)
        edge_attr_20 = 2.32446e-05 + 1 * jax.random.normal(jax.random.fold_in(_gk, 14), (50000, 20), jnp.float32)
        edge_attr_32 = -5.3897e-05 + 0.999841 * jax.random.normal(jax.random.fold_in(_gk, 15), (50000, 32), jnp.float32)
        edge_weight1 = -0.0026448 + 0.998911 * jax.random.normal(jax.random.fold_in(_gk, 17), (50000, 1), jnp.float32)
        return (x, src, dst, edge_attr_16, edge_attr_20, edge_attr_32, edge_weight1)
    x, src, dst, edge_attr_16, edge_attr_20, edge_attr_32, edge_weight1 = _rec_inputs()

    def _L0_gnn_setup():
        import jax, jax.numpy as jnp
        import numpy as np
        N, E, D, SD, SH, EA, FC, H = (50000, 25000, 128, 64, 16, 32, 128, 8)
        EPS = 1e-05
        key = jax.random.key(seed)
        ks = jax.random.split(key, 20)
        rn = lambda k, shp, fan: jax.random.normal(k, shp, jnp.float32) / np.sqrt(fan).astype(np.float32)
        return {'node_features': jax.random.normal(ks[0], (N, D), jnp.float32), 'edge_attr': jax.random.normal(ks[1], (E, EA), jnp.float32), 'edge_sh': jax.random.normal(ks[2], (E, SH), jnp.float32), 'W_node': rn(ks[3], (D, D), D), 'fc1': rn(ks[4], (EA, FC), EA), 'b1': jnp.zeros((FC,), jnp.float32), 'fc2': rn(ks[5], (FC, FC), FC), 'b2': jnp.zeros((FC,), jnp.float32), 'fc3': rn(ks[6], (FC, D), FC), 'b3': jnp.zeros((D,), jnp.float32), 'W_sh': rn(ks[7], (SH, D), SH), 'aW1': rn(ks[8], (2 * SD + EA, FC), 2 * SD + EA), 'ab1': jnp.zeros((FC,), jnp.float32), 'aW2': rn(ks[9], (FC, FC), FC), 'ab2': jnp.zeros((FC,), jnp.float32), 'aW3': rn(ks[10], (FC, H), FC), 'ab3': jnp.zeros((H,), jnp.float32), 'W_out': rn(ks[11], (D, D), D), 'edge_index': jax.random.randint(ks[12], (2, E), 0, N, jnp.int32), 'batch': jnp.zeros((N,), jnp.int32)}
    _L0_gnn_all = _L0_gnn_setup()
    _L0_gnn_in = {k: v for k, v in _L0_gnn_all.items() if k in ('W_node', 'fc1', 'b1', 'fc2', 'b2', 'fc3', 'b3', 'W_sh', 'aW1', 'ab1', 'aW2', 'ab2', 'aW3', 'ab3', 'W_out')}
    del _L0_gnn_all

    def _L1_gnn_setup():
        import jax, jax.numpy as jnp
        import numpy as np
        N = 50000
        E = 12500
        D = 128
        GEO = 20
        H = 3
        C = 128
        NUM_LAYERS = 3

        def _lin_init(key, fan_in, fan_out, extra=()):
            s = 1.0 / np.sqrt(fan_in)
            return jax.random.uniform(key, extra + (fan_in, fan_out), jnp.float32, -s, s)

        def _transformer_conv(x, src, dst, e_attr, Wq, bq, Wk, bk, Wv, bv, We, be, Ws, bs):
            n = x.shape[0]
            q = (x @ Wq + bq).reshape(n, H, C)
            k = (x @ Wk + bk).reshape(n, H, C)
            v = (x @ Wv + bv).reshape(n, H, C)
            e = (e_attr @ We + be).reshape(-1, H, C)
            ke = k[src] + e
            alpha = (q[dst] * ke).sum(-1) / jnp.sqrt(jnp.asarray(C, x.dtype))
            amax = jax.ops.segment_max(alpha, dst, num_segments=n)
            amax = jnp.where(jnp.isfinite(amax), amax, 0.0)
            ex = jnp.exp(alpha - amax[dst])
            den = jax.ops.segment_sum(ex, dst, num_segments=n)
            w = ex / (den[dst] + 1e-16)
            msg = (v[src] + e) * w[:, :, None]
            out = jax.ops.segment_sum(msg.reshape(-1, H * C), dst, num_segments=n)
            out = out.reshape(n, H, C).mean(axis=1)
            return out + x @ Ws + bs
        key = jax.random.key(seed)
        ks = jax.random.split(key, 20)
        inp = {'h': jax.random.normal(ks[0], (N, D), jnp.float32), 'lower_adj_feat': jax.random.normal(ks[1], (E, GEO), jnp.float32), 'dir_w': jax.random.normal(ks[2], (E, 1), jnp.float32), 'src_idx': jax.random.randint(ks[3], (E,), 0, N), 'dst_idx': jax.random.randint(ks[4], (E,), 0, N), 'W_ee': _lin_init(ks[5], 2 * D + GEO + 1, D), 'b_ee': jnp.zeros((D,), jnp.float32), 'W_res': _lin_init(ks[6], D, D), 'b_res': jnp.zeros((D,), jnp.float32), 'Wq': _lin_init(ks[7], D, H * C, (NUM_LAYERS,)), 'bq': jnp.zeros((NUM_LAYERS, H * C), jnp.float32), 'Wk': _lin_init(ks[8], D, H * C, (NUM_LAYERS,)), 'bk': jnp.zeros((NUM_LAYERS, H * C), jnp.float32), 'Wv': _lin_init(ks[9], D, H * C, (NUM_LAYERS,)), 'bv': jnp.zeros((NUM_LAYERS, H * C), jnp.float32), 'We': _lin_init(ks[10], D, H * C, (NUM_LAYERS,)), 'be': jnp.zeros((NUM_LAYERS, H * C), jnp.float32), 'Ws': _lin_init(ks[11], D, C, (NUM_LAYERS,)), 'bs': jnp.zeros((NUM_LAYERS, C), jnp.float32), 'W_ctr': _lin_init(ks[12], 2 * D, D), 'b_ctr': jnp.zeros((D,), jnp.float32)}
        return inp
    _L1_gnn_all = _L1_gnn_setup()
    _L1_gnn_in = {k: v for k, v in _L1_gnn_all.items() if k in ('W_ee', 'b_ee', 'W_res', 'b_res', 'Wq', 'bq', 'Wk', 'bk', 'Wv', 'bv', 'We', 'be', 'Ws', 'bs', 'W_ctr', 'b_ctr')}
    del _L1_gnn_all

    def _L2_gnn_setup():
        import jax, jax.numpy as jnp
        import numpy as np
        N_NODES = 50000
        N_EDGES = 25000
        D_IN = 128
        D_HID = 128
        key = jax.random.key(seed)
        ks = jax.random.split(key, 9)
        s_in = 1.0 / np.sqrt(D_IN)
        s_hid = 1.0 / np.sqrt(D_HID)
        return {'x': jax.random.normal(ks[0], (N_NODES, D_IN), dtype=jnp.float32), 'W_self0': jax.random.normal(ks[1], (D_HID, D_IN), dtype=jnp.float32) * s_in, 'W_neigh0': jax.random.normal(ks[2], (D_HID, D_IN), dtype=jnp.float32) * s_in, 'b0': jnp.zeros((D_HID,), dtype=jnp.float32), 'W_self1': jax.random.normal(ks[3], (D_HID, D_HID), dtype=jnp.float32) * s_hid, 'W_neigh1': jax.random.normal(ks[4], (D_HID, D_HID), dtype=jnp.float32) * s_hid, 'b1': jnp.zeros((D_HID,), dtype=jnp.float32), 'edge_src': jax.random.randint(ks[5], (N_EDGES,), 0, N_NODES, dtype=jnp.int32), 'edge_dst': jax.random.randint(ks[6], (N_EDGES,), 0, N_NODES, dtype=jnp.int32)}
    _L2_gnn_all = _L2_gnn_setup()
    _L2_gnn_in = {k: v for k, v in _L2_gnn_all.items() if k in ('W_self0', 'W_neigh0', 'b0', 'W_self1', 'W_neigh1', 'b1')}
    del _L2_gnn_all

    def _L3_gnn_setup():
        import jax, jax.numpy as jnp
        import numpy as np
        N = 50000
        E = 25000
        DIN = 128
        H = 256
        DOUT = 128
        EPS = 1e-05

        def gcn_conv(x, W, b, src, dst):
            n = x.shape[0]
            h = x @ W
            loop = jnp.arange(n, dtype=src.dtype)
            src_f = jnp.concatenate([src, loop])
            dst_f = jnp.concatenate([dst, loop])
            deg = jax.ops.segment_sum(jnp.ones(src_f.shape[0], h.dtype), dst_f, num_segments=n)
            dinv = jnp.where(deg > 0, jax.lax.rsqrt(deg), 0.0)
            norm = dinv[src_f] * dinv[dst_f]
            out = jax.ops.segment_sum(h[src_f] * norm[:, None], dst_f, num_segments=n)
            return out + b

        def layer_norm(x, g, b):
            mu = jnp.mean(x, axis=-1, keepdims=True)
            xc = x - mu
            var = jnp.mean(xc * xc, axis=-1, keepdims=True)
            return xc * jax.lax.rsqrt(var + EPS) * g + b
        key = jax.random.key(seed)
        ks = jax.random.split(key, 8)
        x = jax.random.normal(ks[0], (N, DIN), jnp.float32)
        edge_index = jax.random.randint(ks[1], (2, E), 0, N, dtype=jnp.int32)

        def lin(k, fi, fo):
            s = 1.0 / np.sqrt(fi)
            return jax.random.uniform(k, (fi, fo), jnp.float32, -s, s)
        return {'x': x, 'edge_index': edge_index, 'W1': lin(ks[2], DIN, H), 'b1': jnp.zeros((H,), jnp.float32), 'g1': jnp.ones((H,), jnp.float32), 'be1': jnp.zeros((H,), jnp.float32), 'W2': lin(ks[3], H, H), 'b2': jnp.zeros((H,), jnp.float32), 'g2': jnp.ones((H,), jnp.float32), 'be2': jnp.zeros((H,), jnp.float32), 'W3': lin(ks[4], H, DOUT), 'b3': jnp.zeros((DOUT,), jnp.float32), 'g3': jnp.ones((DOUT,), jnp.float32), 'be3': jnp.zeros((DOUT,), jnp.float32)}
    _L3_gnn_all = _L3_gnn_setup()
    _L3_gnn_in = {k: v for k, v in _L3_gnn_all.items() if k in ('W1', 'b1', 'g1', 'be1', 'W2', 'b2', 'g2', 'be2', 'W3', 'b3', 'g3', 'be3')}
    del _L3_gnn_all
    return {'x': x, 'src': src, 'dst': dst, 'edge_attr_16': edge_attr_16, 'edge_attr_20': edge_attr_20, 'edge_attr_32': edge_attr_32, 'edge_weight1': edge_weight1, 'L0_gnn_W_node': _L0_gnn_in['W_node'], 'L0_gnn_fc1': _L0_gnn_in['fc1'], 'L0_gnn_b1': _L0_gnn_in['b1'], 'L0_gnn_fc2': _L0_gnn_in['fc2'], 'L0_gnn_b2': _L0_gnn_in['b2'], 'L0_gnn_fc3': _L0_gnn_in['fc3'], 'L0_gnn_b3': _L0_gnn_in['b3'], 'L0_gnn_W_sh': _L0_gnn_in['W_sh'], 'L0_gnn_aW1': _L0_gnn_in['aW1'], 'L0_gnn_ab1': _L0_gnn_in['ab1'], 'L0_gnn_aW2': _L0_gnn_in['aW2'], 'L0_gnn_ab2': _L0_gnn_in['ab2'], 'L0_gnn_aW3': _L0_gnn_in['aW3'], 'L0_gnn_ab3': _L0_gnn_in['ab3'], 'L0_gnn_W_out': _L0_gnn_in['W_out'], 'L1_gnn_W_ee': _L1_gnn_in['W_ee'], 'L1_gnn_b_ee': _L1_gnn_in['b_ee'], 'L1_gnn_W_res': _L1_gnn_in['W_res'], 'L1_gnn_b_res': _L1_gnn_in['b_res'], 'L1_gnn_Wq': _L1_gnn_in['Wq'], 'L1_gnn_bq': _L1_gnn_in['bq'], 'L1_gnn_Wk': _L1_gnn_in['Wk'], 'L1_gnn_bk': _L1_gnn_in['bk'], 'L1_gnn_Wv': _L1_gnn_in['Wv'], 'L1_gnn_bv': _L1_gnn_in['bv'], 'L1_gnn_We': _L1_gnn_in['We'], 'L1_gnn_be': _L1_gnn_in['be'], 'L1_gnn_Ws': _L1_gnn_in['Ws'], 'L1_gnn_bs': _L1_gnn_in['bs'], 'L1_gnn_W_ctr': _L1_gnn_in['W_ctr'], 'L1_gnn_b_ctr': _L1_gnn_in['b_ctr'], 'L2_gnn_W_self0': _L2_gnn_in['W_self0'], 'L2_gnn_W_neigh0': _L2_gnn_in['W_neigh0'], 'L2_gnn_b0': _L2_gnn_in['b0'], 'L2_gnn_W_self1': _L2_gnn_in['W_self1'], 'L2_gnn_W_neigh1': _L2_gnn_in['W_neigh1'], 'L2_gnn_b1': _L2_gnn_in['b1'], 'L3_gnn_W1': _L3_gnn_in['W1'], 'L3_gnn_b1': _L3_gnn_in['b1'], 'L3_gnn_g1': _L3_gnn_in['g1'], 'L3_gnn_be1': _L3_gnn_in['be1'], 'L3_gnn_W2': _L3_gnn_in['W2'], 'L3_gnn_b2': _L3_gnn_in['b2'], 'L3_gnn_g2': _L3_gnn_in['g2'], 'L3_gnn_be2': _L3_gnn_in['be2'], 'L3_gnn_W3': _L3_gnn_in['W3'], 'L3_gnn_b3': _L3_gnn_in['b3'], 'L3_gnn_g3': _L3_gnn_in['g3'], 'L3_gnn_be3': _L3_gnn_in['be3']}

def reference(x, src, dst, edge_attr_16, edge_attr_20, edge_attr_32, edge_weight1, L0_gnn_W_node, L0_gnn_fc1, L0_gnn_b1, L0_gnn_fc2, L0_gnn_b2, L0_gnn_fc3, L0_gnn_b3, L0_gnn_W_sh, L0_gnn_aW1, L0_gnn_ab1, L0_gnn_aW2, L0_gnn_ab2, L0_gnn_aW3, L0_gnn_ab3, L0_gnn_W_out, L1_gnn_W_ee, L1_gnn_b_ee, L1_gnn_W_res, L1_gnn_b_res, L1_gnn_Wq, L1_gnn_bq, L1_gnn_Wk, L1_gnn_bk, L1_gnn_Wv, L1_gnn_bv, L1_gnn_We, L1_gnn_be, L1_gnn_Ws, L1_gnn_bs, L1_gnn_W_ctr, L1_gnn_b_ctr, L2_gnn_W_self0, L2_gnn_W_neigh0, L2_gnn_b0, L2_gnn_W_self1, L2_gnn_W_neigh1, L2_gnn_b1, L3_gnn_W1, L3_gnn_b1, L3_gnn_g1, L3_gnn_be1, L3_gnn_W2, L3_gnn_b2, L3_gnn_g2, L3_gnn_be2, L3_gnn_W3, L3_gnn_b3, L3_gnn_g3, L3_gnn_be3):
    import jax
    import jax.numpy as jnp

    def _L0_gnn_ref(node_features, edge_attr, edge_sh, W_node, fc1, b1, fc2, b2, fc3, b3, W_sh, aW1, ab1, aW2, ab2, aW3, ab3, W_out, edge_index, batch):
        import jax, jax.numpy as jnp
        import numpy as np
        N, E, D, SD, SH, EA, FC, H = (50000, 25000, 128, 64, 16, 32, 128, 8)
        EPS = 1e-05
        src, dst = (edge_index[0], edge_index[1])
        x_src = node_features[src]
        h = jax.nn.silu(edge_attr @ fc1 + b1)
        h = jax.nn.silu(h @ fc2 + b2)
        scale = h @ fc3 + b3
        msg = jax.nn.silu(x_src @ W_node * scale + edge_sh @ W_sh)
        alpha_in = jnp.concatenate([x_src[:, :SD], node_features[dst, :SD], edge_attr], axis=-1)
        a = jax.nn.silu(alpha_in @ aW1 + ab1)
        a = jax.nn.silu(a @ aW2 + ab2)
        a = a @ aW3 + ab3
        alpha = jax.nn.softmax(a, axis=0)
        alpha_mean = alpha.mean(axis=1, keepdims=True)
        agg = jax.ops.segment_sum(msg * alpha_mean, dst, num_segments=node_features.shape[0])
        out = node_features + agg @ W_out
        mu = out.mean(axis=-1, keepdims=True)
        var = out.var(axis=-1, keepdims=True)
        return (out - mu) / jnp.sqrt(var + EPS)

    def _L1_gnn_ref(h, lower_adj_feat, dir_w, src_idx, dst_idx, W_ee, b_ee, W_res, b_res, Wq, bq, Wk, bk, Wv, bv, We, be, Ws, bs, W_ctr, b_ctr):
        import jax, jax.numpy as jnp
        import numpy as np
        N = 50000
        E = 12500
        D = 128
        GEO = 20
        H = 3
        C = 128
        NUM_LAYERS = 3

        def _lin_init(key, fan_in, fan_out, extra=()):
            s = 1.0 / np.sqrt(fan_in)
            return jax.random.uniform(key, extra + (fan_in, fan_out), jnp.float32, -s, s)

        def _transformer_conv(x, src, dst, e_attr, Wq, bq, Wk, bk, Wv, bv, We, be, Ws, bs):
            n = x.shape[0]
            q = (x @ Wq + bq).reshape(n, H, C)
            k = (x @ Wk + bk).reshape(n, H, C)
            v = (x @ Wv + bv).reshape(n, H, C)
            e = (e_attr @ We + be).reshape(-1, H, C)
            ke = k[src] + e
            alpha = (q[dst] * ke).sum(-1) / jnp.sqrt(jnp.asarray(C, x.dtype))
            amax = jax.ops.segment_max(alpha, dst, num_segments=n)
            amax = jnp.where(jnp.isfinite(amax), amax, 0.0)
            ex = jnp.exp(alpha - amax[dst])
            den = jax.ops.segment_sum(ex, dst, num_segments=n)
            w = ex / (den[dst] + 1e-16)
            msg = (v[src] + e) * w[:, :, None]
            out = jax.ops.segment_sum(msg.reshape(-1, H * C), dst, num_segments=n)
            out = out.reshape(n, H, C).mean(axis=1)
            return out + x @ Ws + bs
        edge_features = jnp.concatenate([h[dst_idx], h[src_idx] * dir_w, dir_w, lower_adj_feat], axis=-1)
        edge_attr = edge_features @ W_ee + b_ee
        h_cur = h
        for i in range(NUM_LAYERS):
            residual = h_cur @ W_res + b_res if i == 0 else h_cur
            h_t = _transformer_conv(h_cur, src_idx, dst_idx, edge_attr, Wq[i], bq[i], Wk[i], bk[i], Wv[i], bv[i], We[i], be[i], Ws[i], bs[i])
            h_cur = jax.nn.relu(h_t + residual)
        return jnp.concatenate([h, h_cur], axis=-1) @ W_ctr + b_ctr

    def _L2_gnn_ref(x, W_self0, W_neigh0, b0, W_self1, W_neigh1, b1, edge_src, edge_dst):
        import jax, jax.numpy as jnp
        import numpy as np
        N_NODES = 50000
        N_EDGES = 25000
        D_IN = 128
        D_HID = 128
        N = x.shape[0]
        deg = jax.ops.segment_sum(jnp.ones(edge_dst.shape, dtype=x.dtype), edge_dst, num_segments=N)
        inv_deg = (1.0 / jnp.maximum(deg, 1.0))[:, None]

        def sage_conv(h, W_self, W_neigh, b):
            agg = jax.ops.segment_sum(h[edge_src], edge_dst, num_segments=N) * inv_deg
            return h @ W_self.T + agg @ W_neigh.T + b
        h = jax.nn.relu(sage_conv(x, W_self0, W_neigh0, b0))
        h = sage_conv(h, W_self1, W_neigh1, b1)
        return h

    def _L3_gnn_ref(x, edge_index, W1, b1, g1, be1, W2, b2, g2, be2, W3, b3, g3, be3):
        import jax, jax.numpy as jnp
        import numpy as np
        N = 50000
        E = 25000
        DIN = 128
        H = 256
        DOUT = 128
        EPS = 1e-05

        def gcn_conv(x, W, b, src, dst):
            n = x.shape[0]
            h = x @ W
            loop = jnp.arange(n, dtype=src.dtype)
            src_f = jnp.concatenate([src, loop])
            dst_f = jnp.concatenate([dst, loop])
            deg = jax.ops.segment_sum(jnp.ones(src_f.shape[0], h.dtype), dst_f, num_segments=n)
            dinv = jnp.where(deg > 0, jax.lax.rsqrt(deg), 0.0)
            norm = dinv[src_f] * dinv[dst_f]
            out = jax.ops.segment_sum(h[src_f] * norm[:, None], dst_f, num_segments=n)
            return out + b

        def layer_norm(x, g, b):
            mu = jnp.mean(x, axis=-1, keepdims=True)
            xc = x - mu
            var = jnp.mean(xc * xc, axis=-1, keepdims=True)
            return xc * jax.lax.rsqrt(var + EPS) * g + b
        src, dst = (edge_index[0], edge_index[1])
        h = layer_norm(jax.nn.relu(gcn_conv(x, W1, b1, src, dst)), g1, be1)
        h = layer_norm(jax.nn.relu(gcn_conv(h, W2, b2, src, dst)), g2, be2)
        h = layer_norm(jax.nn.relu(gcn_conv(h, W3, b3, src, dst)), g3, be3)
        return h
    edge_index = jnp.stack([src, dst])
    batch0 = jnp.zeros((3125,), jnp.int32)
    h = jnp.maximum(_layernorm(x, axis=-1), 0.0)
    x = x + _L0_gnn_ref(h, edge_attr_32, edge_attr_16, L0_gnn_W_node, L0_gnn_fc1, L0_gnn_b1, L0_gnn_fc2, L0_gnn_b2, L0_gnn_fc3, L0_gnn_b3, L0_gnn_W_sh, L0_gnn_aW1, L0_gnn_ab1, L0_gnn_aW2, L0_gnn_ab2, L0_gnn_aW3, L0_gnn_ab3, L0_gnn_W_out, edge_index, batch0)
    h = jnp.maximum(_layernorm(x, axis=-1), 0.0)
    x = x + _L1_gnn_ref(h, edge_attr_20, edge_weight1, src, dst, L1_gnn_W_ee, L1_gnn_b_ee, L1_gnn_W_res, L1_gnn_b_res, L1_gnn_Wq, L1_gnn_bq, L1_gnn_Wk, L1_gnn_bk, L1_gnn_Wv, L1_gnn_bv, L1_gnn_We, L1_gnn_be, L1_gnn_Ws, L1_gnn_bs, L1_gnn_W_ctr, L1_gnn_b_ctr)
    h = jnp.maximum(_layernorm(x, axis=-1), 0.0)
    x = x + _L2_gnn_ref(h, L2_gnn_W_self0, L2_gnn_W_neigh0, L2_gnn_b0, L2_gnn_W_self1, L2_gnn_W_neigh1, L2_gnn_b1, src, dst)
    h = jnp.maximum(_layernorm(x, axis=-1), 0.0)
    x = x + _L3_gnn_ref(h, edge_index, L3_gnn_W1, L3_gnn_b1, L3_gnn_g1, L3_gnn_be1, L3_gnn_W2, L3_gnn_b2, L3_gnn_g2, L3_gnn_be2, L3_gnn_W3, L3_gnn_b3, L3_gnn_g3, L3_gnn_be3)
    return x

_drawn_inputs = setup_inputs


def setup_inputs(seed=0):
    import zlib

    import numpy as np

    out = dict(_drawn_inputs(seed))
    spreads = {'L0_gnn_b1': (0.0, 0.8),
     'L0_gnn_b2': (0.0, 0.8),
     'L0_gnn_b3': (0.0, 0.8),
     'L0_gnn_ab1': (0.0, 0.8),
     'L0_gnn_ab2': (0.0, 0.8),
     'L0_gnn_ab3': (0.0, 0.8),
     'L1_gnn_b_ee': (0.0, 0.757),
     'L1_gnn_b_res': (0.0, 0.431),
     'L1_gnn_bq': (0.0, 0.8),
     'L1_gnn_bk': (0.0, 0.8),
     'L1_gnn_bv': (0.0, 0.498),
     'L1_gnn_be': (0.0, 0.507),
     'L1_gnn_bs': (0.0, 0.1),
     'L1_gnn_b_ctr': (0.0, 0.1),
     'L2_gnn_b0': (0.0, 0.1),
     'L2_gnn_b1': (0.0, 0.1),
     'L3_gnn_b1': (0.0, 0.1),
     'L3_gnn_g1': (1.0, 0.2),
     'L3_gnn_be1': (0.0, 0.1),
     'L3_gnn_b2': (0.0, 0.1),
     'L3_gnn_g2': (1.0, 0.2),
     'L3_gnn_be2': (0.0, 0.1),
     'L3_gnn_b3': (0.0, 0.1),
     'L3_gnn_g3': (1.0, 0.2),
     'L3_gnn_be3': (0.0, 0.1)}
    factors = {'edge_attr_16': 8.0,
     'edge_attr_20': 8.0,
     'edge_attr_32': 8.0,
     'edge_weight1': 8.0,
     'L0_gnn_W_node': 8.0,
     'L0_gnn_fc1': 8.0,
     'L0_gnn_fc2': 8.0,
     'L0_gnn_fc3': 8.0,
     'L0_gnn_W_sh': 8.0,
     'L0_gnn_aW1': 8.0,
     'L0_gnn_aW2': 8.0,
     'L0_gnn_aW3': 8.0,
     'L0_gnn_W_out': 8.0,
     'L1_gnn_Wq': 8.0,
     'L1_gnn_Wk': 8.0}
    for name, (base, spread) in spreads.items():
        noise = np.random.default_rng([zlib.crc32(name.encode()), seed]).standard_normal(out[name].shape)
        drawn = base * np.exp(spread * noise) if base else spread * noise
        out[name] = jnp.asarray(drawn.astype(out[name].dtype))
    for name, factor in factors.items():
        out[name] = (out[name] * factor).astype(out[name].dtype)
    return out
```

```python
from contextlib import ExitStack, contextmanager

import concourse.bass as bass
from concourse import mybir

F32 = mybir.dt.float32
BF16 = mybir.dt.bfloat16
I32 = mybir.dt.int32
I16 = mybir.dt.int16
ALU = mybir.AluOpType
ACT = mybir.ActivationFunctionType
AX = mybir.AxisListType
RMAX = bass.bass_isa.ReduceOp.max
RADD = bass.bass_isa.ReduceOp.add

N, E, D, H = 3125, 50000, 128, 3
EA, SH, GEO, AH = 32, 16, 20, 8
WN = 42
NW = -(-N // WN)
NP = NW * WN
WH = WN * H
T = 6
S = 128 * T
BM, NB = 3 * WN, NW // 3
CE = 512
NC = -(-E // CE)
EP = NC * CE
EW = E + S + 256
NCOL, NCH = 450, 7
WC, NWC = 5, 15
CW = WC * WN
GK = GEO + 2
AW = 12
KEY0 = 8192
EPS = 1e-5
FAR = float(2.0 ** 100)
FLOOR = -float(2.0 ** 90)


class Steps:

    def __init__(self, sem, names, ahead=0):
        self.sem, self.per, self.ahead = sem, len(names), ahead
        self.at = {n: k + 1 for k, n in enumerate(names)}

    def of(self, turn, name):
        return (turn + self.ahead) * self.per + self.at[name]

    def prime(self, eng):
        eng.sem_inc(self.sem, self.ahead * self.per)


class Kit:

    def __init__(self, nc, dram, ctx):
        self.nc, self.dram, self.ctx = nc, dram, ctx
        self.old = []
        self.rows_in = [ctx.enter_context(nc.semaphore(f"rows_in{u}")) for u in range(3)]
        self.rows_base = [0] * 3
        self.ps = ctx.enter_context(nc.psum_tensor("ps", [128, 8, 512], F32))

    def keep(self, name, shape, dt=F32):
        return self.ctx.enter_context(self.nc.sbuf_tensor(name, shape, dt))

    @contextmanager
    def phase(self, name):
        nc = self.nc
        sems = ExitStack()
        used = []

        def sem(what):
            used.append(sems.enter_context(nc.semaphore(f"{name}_{what}")))
            return used[-1]

        with ExitStack() as bufs:
            def sb(what, shape, dt=F32):
                return bufs.enter_context(nc.sbuf_tensor(f"{name}_{what}", shape, dt))

            hop = {e: sem(f"hop_{e}") for e in ("pool", "act")}
            with nc.Block() as block:
                yield sb, sem, block, hop
        if self.old:
            self.old[-1].close()
        self.old = [used, sems]

    def clear_old(self, sp):
        for s in (self.old[0] if self.old else []):
            sp.sem_clear(s)


def bc(ap, shape):
    return ap.to_broadcast(shape)


def prepare(k):
    nc, d = k.nc, k.dram
    k.ident = k.keep("ident", [128, 128])
    k.far = k.keep("far", [128, 128], BF16)
    k.mean = k.keep("mean", [128, 128])
    k.ones = k.keep("ones", [128, 128])
    k.iota_wn = k.keep("iota_wn", [128, WN])
    k.eps = k.keep("eps", [128, 1])
    k.xT = k.keep("xT", [128, NP])
    k.starts = k.keep("starts", [1, NW], I32)
    k.fits = k.keep("fits", [1, 1], I32)
    PC = EP // 128
    with k.phase("prep") as (sb, sem, block, hop):
        dsts = sb("dsts", [128, PC], I32)
        nexts = sb("nexts", [128, PC], I32)
        dstf = sb("dstf", [128, PC])
        nextf = sb("nextf", [128, PC])
        junk = sb("junk", [128, PC], BF16)
        cnt = sb("cnt", [128, NW + 2])
        row = sb("row", [1, NW + 2])
        gap = sb("gap", [1, NW])
        most = sb("most", [1, 1])
        is_sorted = sb("is_sorted", [1, 1])
        PAD = EW - EP
        zero = sb("zero", [128, PAD // 106 * D])
        pads_out = sem("pads_out")
        x_in, dst_in, made, pe_sums, dve = (sem(n) for n in ("x_in", "dst_in", "made", "pe_sums", "dve"))

        @block.sync
        def _(sp):
            sp.dma_start(dsts[:, :], d["dst"][0:EP].rearrange("(p c) -> p c", c=PC)).then_inc(dst_in, 16)
            sp.dma_start(nexts[:, :], d["dst"][1:EP + 1].rearrange("(p c) -> p c", c=PC)).then_inc(dst_in, 16)
            sp.dma_start(k.xT[:, :], d["xT"]).then_inc(x_in, 16)
            sp.wait_ge(made, 1)
            sp.dma_start(d["am"][EP:EW].rearrange("(p j) -> p j", p=106), zero[0:106, 0:PAD // 106]).then_inc(pads_out, 16)
            sp.dma_start(d["msg"][EP:EW, :].rearrange("(p j) f -> p (j f)", p=106), zero[0:106, :]).then_inc(pads_out, 16)
            sp.wait_ge(x_in, 16)
            sp.wait_ge(pads_out, 32)

        @block.gpsimd
        def _(pool):
            pool.memset(zero[:, :], 0.0).then_inc(made, 1)
            pool.memset(k.mean[:, :], 1.0 / D).then_inc(made, 1)
            pool.memset(k.ones[:, :], 1.0).then_inc(made, 1)
            pool.memset(k.eps[:, :], EPS).then_inc(made, 1)
            pool.iota(k.iota_wn[:, :], pattern=[[1, WN]], base=0, channel_multiplier=0,
                      allow_small_or_imprecise_dtypes=True).then_inc(made, 1)
            pool.wait_ge(made, 1)
            for m, fill in ((k.ident, 1.0), (k.far, FAR)):
                pool.affine_select(out=m[:, :], in_=zero[:, 0:128], compare_op=ALU.not_equal, fill=fill,
                                   base=0, pattern=[[-1, 128]], channel_multiplier=1).then_inc(made, 1)
            pool.wait_ge(made, 7)

        @block.vector
        def _(dve_):
            dve_.wait_ge(dst_in, 32)
            nc.vector.tensor_copy(dstf[:, :], dsts[:, :]).then_inc(dve, 1)
            nc.vector.tensor_copy(nextf[:, :], nexts[:, :]).then_inc(dve, 1)
            dve_.wait_ge(dve, 2)
            for w in range(NW + 1):
                if w:
                    dve_.wait_ge(dve, 2 + w)
                nc.vector.tensor_scalar(junk[:, :], dstf[:, :], float(min(w * WN, N)), 0.0, ALU.is_lt, ALU.add,
                                        accum_out=cnt[:, w:w + 1]).then_inc(dve, 1)
            dve_.wait_ge(dve, NW + 3)
            nc.vector.tensor_tensor(dstf[:, :], dstf[:, :], nextf[:, :], ALU.is_gt).then_inc(dve, 1)
            dve_.wait_ge(dve, NW + 4)
            nc.vector.reduce_sum(cnt[:, NW + 1:NW + 2], dstf[:, :], AX.X).then_inc(dve, 1)
            dve_.wait_ge(pe_sums, 1)
            nc.vector.tensor_copy(row[:, :], k.ps[0:1, 0, 0:NW + 2]).then_inc(dve, 1)
            dve_.wait_ge(dve, NW + 6)
            nc.vector.tensor_copy(k.starts[:, :], row[:, 0:NW]).then_inc(dve, 1)
            nc.vector.tensor_sub(gap[:, :], row[:, 1:NW + 1], row[:, 0:NW]).then_inc(dve, 1)
            nc.vector.tensor_scalar(is_sorted[:, :], row[:, NW + 1:NW + 2], 0.0, None, ALU.is_le).then_inc(dve, 1)
            dve_.wait_ge(dve, NW + 9)
            nc.vector.reduce_max(most[:, :], gap[:, :], AX.X).then_inc(dve, 1)
            dve_.wait_ge(dve, NW + 10)
            nc.vector.scalar_tensor_tensor(k.fits[:, :], most[:, :], float(S), is_sorted[:, :],
                                           ALU.is_le, ALU.mult).then_inc(dve, 1)
            dve_.wait_ge(dve, NW + 11)

        @block.tensor
        def _(pe):
            pe.wait_ge(made, 7)
            pe.wait_ge(dve, NW + 5)
            nc.tensor.matmul(k.ps[0:1, 0, 0:NW + 2], k.ones[:, 0:1], cnt[:, :], start=True, stop=True).then_inc(pe_sums, 1)


def layer_norm(k, name, src, out, parts=1, relu=False, gain=None, shift=None, add=False, inner_relu=False):
    nc = k.nc
    with k.phase(name) as (sb, sem, block, hop):
        xc = sb("xc", [128, 2, parts, NCOL])
        sq = sb("sq", [128, 2, parts, NCOL])
        std = sb("std", [128, 2, NCOL])
        rec = sb("rec", [128, 2, NCOL])
        y = sb("y", [128, 2, parts, NCOL])
        centred, squared, mean_ok, var_ok, std_ok, rec_ok, scaled, moved, stored = (
            sem(n) for n in ("centred", "squared", "mean_ok", "var_ok", "std_ok", "rec_ok", "scaled", "moved", "stored"))
        half = k.mean if parts == 1 else sb("half", [128, 128])
        half_ok = sem("half_ok")

        def cols(c):
            return slice(c * NCOL, (c + 1) * NCOL)

        @block.sync
        def _(sp):
            k.clear_old(sp)

        @block.gpsimd
        def _(pool):
            if parts > 1:
                pool.memset(half[:, :], 1.0 / (D * parts)).then_inc(half_ok, 1)

        @block.tensor
        def _(pe):
            def mean(c):
                if c >= 2:
                    pe.wait_ge(centred, c - 1)
                for p in range(parts):
                    m = nc.tensor.matmul(k.ps[:, c % 2, 0:NCOL], half[:, :], src[:, p, cols(c)],
                                         start=p == 0, stop=p == parts - 1)
                m.then_inc(mean_ok, 1)

            if parts > 1:
                pe.wait_ge(half_ok, 1)
            mean(0)
            for c in range(NCH):
                if c + 1 < NCH:
                    mean(c + 1)
                pe.wait_ge(squared, c + 1)
                if c >= 2:
                    pe.wait_ge(std_ok, c - 1)
                for p in range(parts):
                    m = nc.tensor.matmul(k.ps[:, 2 + c % 2, 0:NCOL], half[:, :], sq[:, c % 2, p, :],
                                         start=p == 0, stop=p == parts - 1)
                m.then_inc(var_ok, 1)

        @block.scalar
        def _(act):
            for c in range(NCH):
                act.wait_ge(var_ok, c + 1)
                if c >= 2:
                    act.wait_ge(rec_ok, c - 1)
                nc.scalar.activation(std[:, c % 2, :], k.ps[:, 2 + c % 2, 0:NCOL], ACT.Sqrt,
                                     bias=k.eps[:, 0:1]).then_inc(std_ok, 1)

        @block.vector
        def _(dve):
            def centre(c):
                dve.wait_ge(mean_ok, c + 1)
                if c >= 2:
                    dve.wait_ge(stored, c - 1)
                    dve.wait_ge(var_ok, c - 1)
                nc.vector.tensor_tensor(xc[:, c % 2, :, :], src[:, :, cols(c)],
                                        bc(k.ps[:, c % 2, 0:NCOL].unsqueeze(1), [128, parts, NCOL]),
                                        ALU.subtract).then_inc(centred, 1)
                dve.wait_ge(centred, c + 1)
                nc.vector.tensor_tensor(sq[:, c % 2, :, :], xc[:, c % 2, :, :], xc[:, c % 2, :, :],
                                        ALU.mult).then_inc(squared, 1)

            def finish(c):
                b = c % 2
                dve.wait_ge(std_ok, c + 1)
                nc.vector.reciprocal(rec[:, b, :], std[:, b, :]).then_inc(rec_ok, 1)
                dve.wait_ge(rec_ok, c + 1)
                recs = bc(rec[:, b, :].unsqueeze(1), [128, parts, NCOL])
                last = not (gain is not None or add)
                to = out[:, :, cols(c)] if last else y[:, b, :, :]
                if relu:
                    nc.vector.scalar_tensor_tensor(to, xc[:, b, :, :], 0.0, recs, ALU.max,
                                                   ALU.mult).then_inc(stored if last else scaled, 1)
                else:
                    nc.vector.tensor_tensor(to, xc[:, b, :, :], recs, ALU.mult).then_inc(stored if last else scaled, 1)
                if last:
                    return
                dve.wait_ge(scaled, c + 1)
                if gain is not None:
                    for p in range(parts):
                        to = y[:, b, p, :] if add else out[:, p, cols(c)]
                        nc.vector.tensor_scalar(to, y[:, b, p, :], gain[:, p:p + 1], shift[:, p:p + 1], ALU.mult,
                                                ALU.add).then_inc(moved if add or p < parts - 1 else stored, 1)
                    if not add:
                        return
                    dve.wait_ge(moved, parts * (c + 1))
                nc.vector.tensor_tensor(out[:, :, cols(c)], out[:, :, cols(c)], y[:, b, :, :],
                                        ALU.add).then_inc(stored, 1)

            for c in range(NCH + 1):
                if c < NCH:
                    centre(c)
                if c:
                    finish(c - 1)
            dve.wait_ge(stored, NCH)


def node_rows(k, name, srcT, weights, width, stores):
    nc = k.nc
    with k.phase(name) as (sb, sem, block, hop):
        rows = sb("rows", [BM, 4, width])
        w = None
        if weights is not None:
            w, w_in, w_zero = sb("w", [128, width]), sem("w_in"), sem("w_zero")
        made, copied = sem("made"), sem("copied")
        out = [sem(f"out{n}") for n in range(4)]
        ns = len(stores)

        @block.sync
        def _(sp):
            k.clear_old(sp)
            if w is not None:
                sp.wait_ge(w_zero, 1)
                for at, rows_, src in weights:
                    sp.dma_start(w[0:rows_, at:at + src.shape[1]], src).then_inc(w_in, 16)
            for b in range(NB):
                sp.wait_ge(copied, b + 1)
                for dst, at, n in stores:
                    sp.dma_start(dst[b * BM:(b + 1) * BM, :], rows[:, b % 4, at:at + n]).then_inc(out[b % 4], 16)
            for q in range(4):
                sp.wait_ge(out[q], 16 * ns * len(range(q, NB, 4)))

        @block.gpsimd
        def _(pool):
            if w is not None:
                pool.memset(w[:, :], 0.0).then_inc(w_zero, 1)

        @block.tensor
        def _(pe):
            if w is not None:
                pe.wait_ge(w_in, 16 * len(weights))
            for b in range(NB):
                if b >= 4:
                    pe.wait_ge(copied, b - 3)
                block_ = srcT[:, b * BM:(b + 1) * BM]
                if w is None:
                    m = nc.tensor.transpose(k.ps[0:BM, b % 4, 0:width], block_, k.ident[:, :])
                else:
                    m = nc.tensor.matmul(k.ps[0:BM, b % 4, 0:width], block_, w[:, :], start=True, stop=True)
                m.then_inc(made, 1)

        @block.scalar
        def _(act):
            for b in range(NB):
                act.wait_ge(made, b + 1)
                if b >= 4:
                    act.wait_ge(out[b % 4], 16 * ns * (b // 4))
                nc.scalar.activation(rows[:, b % 4, :], k.ps[0:BM, b % 4, 0:width], ACT.Copy).then_inc(copied, 1)


def edge_messages(k, a_all):
    nc, d = k.nc, k.dram
    with k.phase("em") as (sb, sem, block, hop):
        fc1, aw1e = sb("fc1", [EA, D]), sb("aw1e", [EA, D])
        fc2, fc3, aw2 = sb("fc2", [D, D]), sb("fc3", [D, D]), sb("aw2", [D, D])
        wsh, aw3 = sb("wsh", [SH, D]), sb("aw3", [D, AH])
        bias = sb("bias", [128, 4])
        b3 = sb("b3", [128, D])
        ab3 = sb("ab3", [128, AH])
        idx = sb("idx", [128, 2, 8], I32)
        ea = sb("ea", [EA, 2, CE])
        sh = sb("sh", [SH, 2, CE])
        gs = sb("gs", [128, 2, 4, 2 * D])
        gd = sb("gd", [128, 2, 4, D])
        ga = sb("ga", [128, 2, 4, D])
        h1, h2, a1, a2 = (sb(n, [128, 2, CE]) for n in ("h1", "h2", "a1", "a2"))
        t1 = sb("t1", [128, 2, 4, D])
        t2 = sb("t2", [128, 2, 4, D])
        t3 = sb("t3", [128, 2, 4, D])
        msg = sb("msg", [128, 2, 4, D])
        w_in = sem("w_in")
        idx_in, feat_in, msg_out = ([sem(f"{n}{u}") for u in range(2)] for n in ("idx_in", "feat_in", "msg_out"))
        rows_in, rows_base = k.rows_in, list(k.rows_base)
        pe_ = Steps(sem("pe"), ["FC1", "A1", "FC2", "A2", "SCALE", "SH", "A3"], 2)
        act_ = Steps(sem("act"), ["H1", "A1", "H2", "A2", "MSG"], 2)
        dve_ = Steps(sem("dve"), ["GA", "A3", "TB", "TG", "TS"], 2)
        loads = [(fc1[:, :], d["fc1"]), (aw1e[:, :], d["aW1"][D:D + EA, :]), (fc2[:, :], d["fc2"]), (fc3[:, :], d["fc3"]),
                 (aw2[:, :], d["aW2"]), (wsh[:, :], d["W_sh"]), (aw3[:, :], d["aW3"]), (bias[:, :], d["em_bias"]),
                 (b3[:, :], d["b3"].partition_broadcast(128)), (ab3[:, :], d["ab3"].partition_broadcast(128))]
        edges = d["sd"][0:EP, :].rearrange("(c p j) s -> c p (j s)", p=128, j=4)
        msgs = d["msg"][0:EP, :].rearrange("(c p j) f -> c p (j f)", p=128, j=4)

        @block.sync
        def _(sp):
            k.clear_old(sp)
            for to, src in loads:
                sp.dma_start(to, src).then_inc(w_in, 16)
            with sp.Fori(0, NC // 2) as i:
                for u in range(2):
                    c = 2 * i + u
                    sp.wait_ge(dve_.sem, dve_.of(c - 2, "GA"))
                    sp.dma_start(idx[:, u, :], edges[bass.ds(c, 1), :, :].rearrange("c p q -> (c p) q")).then_inc(idx_in[u], 16)
                    sp.wait_ge(pe_.sem, pe_.of(c - 2, "SH"))
                    sp.dma_start(ea[:, u, :], d["ea32"][bass.ds(c, 1), :, :].rearrange("c p q -> (c p) q")).then_inc(feat_in[u], 16)
                    sp.dma_start(sh[:, u, :], d["sh16"][bass.ds(c, 1), :, :].rearrange("c p q -> (c p) q")).then_inc(feat_in[u], 16)

        @block.gpsimd
        def _(pool):
            with pool.Fori(0, NC // 2) as i:
                for u in range(2):
                    c = 2 * i + u
                    pool.wait_ge(dve_.sem, dve_.of(c - 2, "TG"))
                    pool.sem_inc(hop["pool"], 1)
                    pool.wait_ge(idx_in[u], (i + 1) * 16)
                    pool.sem_inc(hop["pool"], 1)
                    for j in range(4):
                        pool.indirect_dma_start(out=gs[:, u, j, :], out_offset=None, in_=d["rows0"],
                                                in_offset=bass.IndirectOffsetOnAxis(ap=idx[:, u, 2 * j:2 * j + 1], axis=0)
                                                ).then_inc(rows_in[u], 16)
                        pool.indirect_dma_start(out=gd[:, u, j, :], out_offset=None, in_=d["rows0d"],
                                                in_offset=bass.IndirectOffsetOnAxis(ap=idx[:, u, 2 * j + 1:2 * j + 2], axis=0)
                                                ).then_inc(rows_in[u], 16)

        @block.tensor
        def _(pe):
            pe_.prime(pe)
            pe.wait_ge(w_in, 16 * len(loads))
            with pe.Fori(0, NC // 2) as i:
                cs = [2 * i, 2 * i + 1]
                for u, c in enumerate(cs):
                    pe.wait_ge(feat_in[u], (i + 1) * 32)
                    pe.wait_ge(act_.sem, act_.of(c - 2, "H2"))
                    nc.tensor.matmul(k.ps[:, u, :], fc1[:, :], ea[:, u, :], start=True, stop=True).then_inc(pe_.sem, 1)
                    pe.wait_ge(act_.sem, act_.of(c - 2, "A2"))
                    nc.tensor.matmul(k.ps[:, 2 + u, :], aw1e[:, :], ea[:, u, :], start=True, stop=False)
                    pe.wait_ge(dve_.sem, dve_.of(c, "GA"))
                    for j in range(4):
                        m = nc.tensor.matmul(k.ps[:, 2 + u, j * 128:(j + 1) * 128], ga[:, u, j, :], k.ident[:, :],
                                             start=False, stop=j == 3)
                    m.then_inc(pe_.sem, 1)
                    pe.wait_ge(act_.sem, act_.of(c, "H1"))
                    nc.tensor.matmul(k.ps[:, u, :], fc2[:, :], h1[:, u, :], start=True, stop=True).then_inc(pe_.sem, 1)
                    pe.wait_ge(act_.sem, act_.of(c, "A1"))
                    nc.tensor.matmul(k.ps[:, 2 + u, :], aw2[:, :], a1[:, u, :], start=True, stop=True).then_inc(pe_.sem, 1)
                    pe.wait_ge(act_.sem, act_.of(c, "H2"))
                    pe.wait_ge(dve_.sem, dve_.of(c - 2, "TB"))
                    for j in range(4):
                        m = nc.tensor.matmul(k.ps[:, 4 + u, j * 128:(j + 1) * 128], h2[:, u, j * 128:(j + 1) * 128], fc3[:, :],
                                             start=True, stop=True)
                    m.then_inc(pe_.sem, 1)
                    pe.wait_ge(dve_.sem, dve_.of(c - 1, "TS"))
                    for j in range(4):
                        m = nc.tensor.matmul(k.ps[:, 6, j * 128:(j + 1) * 128], sh[:, u, j * 128:(j + 1) * 128], wsh[:, :],
                                             start=True, stop=True)
                    m.then_inc(pe_.sem, 1)
                    pe.wait_ge(act_.sem, act_.of(c, "A2"))
                    pe.wait_ge(dve_.sem, dve_.of(c - 1, "A3"))
                    for j in range(4):
                        m = nc.tensor.matmul(k.ps[:, 7, j * AH:(j + 1) * AH], a2[:, u, j * 128:(j + 1) * 128], aw3[:, :],
                                             start=True, stop=True)
                    m.then_inc(pe_.sem, 1)

        @block.scalar
        def _(act):
            act_.prime(act)
            act.sem_inc(msg_out[0], 16)
            act.sem_inc(msg_out[1], 16)
            act.wait_ge(w_in, 16 * len(loads))
            with act.Fori(0, NC // 2) as i:
                for u in range(2):
                    c = 2 * i + u
                    act.wait_ge(pe_.sem, pe_.of(c, "FC1"))
                    nc.scalar.activation(h1[:, u, :], k.ps[:, u, :], ACT.Silu, bias=bias[:, 0:1]).then_inc(act_.sem, 1)
                    act.wait_ge(pe_.sem, pe_.of(c, "A1"))
                    nc.scalar.activation(a1[:, u, :], k.ps[:, 2 + u, :], ACT.Silu, bias=bias[:, 2:3]).then_inc(act_.sem, 1)
                    act.wait_ge(pe_.sem, pe_.of(c, "FC2"))
                    nc.scalar.activation(h2[:, u, :], k.ps[:, u, :], ACT.Silu, bias=bias[:, 1:2]).then_inc(act_.sem, 1)
                    act.wait_ge(pe_.sem, pe_.of(c, "A2"))
                    nc.scalar.activation(a2[:, u, :], k.ps[:, 2 + u, :], ACT.Silu, bias=bias[:, 3:4]).then_inc(act_.sem, 1)
                    act.wait_ge(dve_.sem, dve_.of(c, "TS"))
                    act.sem_inc(hop["act"], 1)
                    act.wait_ge(msg_out[u], (i + 1) * 16)
                    nc.scalar.activation(msg[:, u, :, :], t3[:, u, :, :], ACT.Silu).then_inc(act_.sem, 1)
                    act.wait_ge(act_.sem, act_.of(c, "MSG"))
                    act.sem_inc(hop["act"], 1)
                    act.dma_start(msgs[bass.ds(c, 1), :, :].rearrange("c p q -> (c p) q"),
                                  msg[:, u, :, :].rearrange("p j f -> p (j f)")).then_inc(msg_out[u], 16)
            for u in range(2):
                act.wait_ge(msg_out[u], 16 * (NC // 2 + 1))

        @block.vector
        def _(dve):
            dve_.prime(dve)
            dve.wait_ge(w_in, 16 * len(loads))
            with dve.Fori(0, NC // 2) as i:
                for u in range(2):
                    c = 2 * i + u
                    dve.wait_ge(rows_in[u], (i + 1) * 128 + rows_base[u])
                    dve.wait_ge(pe_.sem, pe_.of(c - 2, "A1"))
                    nc.vector.tensor_tensor(ga[:, u, :, :], gs[:, u, :, D:2 * D], gd[:, u, :, :], ALU.add).then_inc(dve_.sem, 1)
                    dve.wait_ge(pe_.sem, pe_.of(c, "A3"))
                    nc.vector.tensor_tensor(a_all[:, bass.ds(c, 1), :, :].rearrange("p c j h -> p (c j) h"),
                                            k.ps[:, 7, 0:4 * AH].rearrange("p (j h) -> p j h", h=AH),
                                            bc(ab3[:, :].unsqueeze(1), [128, 4, AH]), ALU.add).then_inc(dve_.sem, 1)
                    nc.vector.tensor_tensor(t1[:, u, :, :], k.ps[:, 4 + u, :].rearrange("p (j f) -> p j f", f=D),
                                            bc(b3[:, :].unsqueeze(1), [128, 4, D]), ALU.add).then_inc(dve_.sem, 1)
                    dve.wait_ge(dve_.sem, dve_.of(c, "TB"))
                    nc.vector.tensor_tensor(t2[:, u, :, :], t1[:, u, :, :], gs[:, u, :, 0:D], ALU.mult).then_inc(dve_.sem, 1)
                    dve.wait_ge(dve_.sem, dve_.of(c, "TG"))
                    dve.wait_ge(act_.sem, act_.of(c - 2, "MSG"))
                    nc.vector.tensor_tensor(t3[:, u, :, :], t2[:, u, :, :], k.ps[:, 6, :].rearrange("p (j f) -> p j f", f=D),
                                            ALU.add).then_inc(dve_.sem, 1)
        for u in range(2):
            k.rows_base[u] += NC // 2 * 128


def edge_softmax(k, a_all):
    nc, d = k.nc, k.dram
    ns = NC * 4
    with k.phase("es") as (sb, sem, block, hop):
        part, most, total, inv = (sb(n, [128, AH]) for n in ("part", "most", "total", "inv"))
        part2 = sb("part2", [128, AH])
        am = sb("am", [128, ns])
        masked, dve, pooled, exped, out = (sem(n) for n in ("masked", "dve", "pooled", "exped", "out"))
        flat = a_all[:, :, :, :].rearrange("p c j h -> p (c j) h")
        by_head = a_all[:, :, :, :].rearrange("p c j h -> p h (c j)")
        last = a_all[:, NC - 1, :, :].rearrange("p j h -> p (j h)")
        whole = bc

        @block.sync
        def _(sp):
            k.clear_old(sp)
            sp.wait_ge(dve, 7)
            sp.dma_start(d["am"][0:EP].rearrange("(c p j) -> p c j", p=128, j=4),
                         am[:, :].rearrange("p (c j) -> p c j", j=4)).then_inc(out, 16)
            sp.wait_ge(out, 16)

        @block.gpsimd
        def _(pool):
            pool.affine_select(out=last, in_=last, compare_op=ALU.is_ge, fill=-1e30,
                               base=(E - (NC - 1) * CE) // 4 - 1, pattern=[[0, 4 * AH]], channel_multiplier=-1).then_inc(masked, 1)
            pool.wait_ge(dve, 1)
            pool.partition_all_reduce(most[:, :], part[:, :], 128, RMAX).then_inc(pooled, 1)
            pool.wait_ge(dve, 3)
            pool.partition_all_reduce(total[:, :], part2[:, :], 128, RADD).then_inc(pooled, 1)

        @block.scalar
        def _(act):
            act.wait_ge(dve, 2)
            nc.scalar.activation(flat, flat, ACT.Exp).then_inc(exped, 1)

        @block.vector
        def _(v):
            v.wait_ge(masked, 1)
            nc.vector.tensor_reduce(part[:, :], by_head, AX.X, ALU.max).then_inc(dve, 1)
            v.wait_ge(pooled, 1)
            nc.vector.tensor_tensor(flat, flat, whole(most[:, :].unsqueeze(1), [128, ns, AH]), ALU.subtract).then_inc(dve, 1)
            v.wait_ge(exped, 1)
            nc.vector.tensor_reduce(part2[:, :], by_head, AX.X, ALU.add).then_inc(dve, 1)
            v.wait_ge(pooled, 2)
            nc.vector.reciprocal(inv[:, :], total[:, :]).then_inc(dve, 1)
            v.wait_ge(dve, 4)
            nc.vector.tensor_scalar(part[:, :], inv[:, :], 1.0 / AH, None, ALU.mult).then_inc(dve, 1)
            v.wait_ge(dve, 5)
            nc.vector.tensor_tensor(flat, flat, whole(part[:, :].unsqueeze(1), [128, ns, AH]), ALU.mult).then_inc(dve, 1)
            v.wait_ge(dve, 6)
            nc.vector.tensor_reduce(am[:, :], flat, AX.X, ALU.add).then_inc(dve, 1)


def window_sums(k, aggT):
    nc, d = k.nc, k.dram
    U = 3
    with k.phase("ws") as (sb, sem, block, hop):
        sd = sb("sd", [128, U, 2 * T], I32)
        am = sb("am", [128, U, T])
        msg = sb("msg", [128, U, T * D])
        base = sb("base", [128, 1])
        srcf, dl, blk, res, ok1, ok, key0, key = (sb(n, [128, U, T]) for n in
                                                  ("srcf", "dl", "blk", "res", "ok1", "ok", "key0", "key"))
        sel = sb("sel", [128, U, T, WN])
        wsel = sb("wsel", [128, U, T, WN])
        ge = sb("ge", [128, U, T, NB - 1])
        oh_res = sb("oh_res", [128, U, T, BM], BF16)
        oh_key = sb("oh_key", [128, U, T, NB * WN], BF16)
        bounds = sb("bounds", [128, NB - 1])
        iota_bm = sb("iota_bm", [128, BM])
        iota_key = sb("iota_key", [128, NB * WN], I16)
        adj = sb("adj", [BM, U, NB * WN], BF16)
        deg = sb("deg", [1, NP])
        made = sem("made")
        in_ = [sem(f"in{u}") for u in range(U)]
        adj_out = [sem(f"adj_out{u}") for u in range(U)]
        deg_out = sem("deg_out")
        dve_ = Steps(sem("dve"), ["SRC", "DL", "GE", "SEL", "OK1", "BLK", "WSEL", "OK", "RES", "KEY0", "KEY", "OH_RES"]
                     + [f"OH_KEY{j}" for j in range(T)] + ["BASE"], U)
        pe_ = Steps(sem("pe"), ["AGG", "DEG", "ADJ"], U)
        act_ = Steps(sem("act"), ["AGG", "DEG", "ADJ"], U)

        @block.sync
        def _(sp):
            k.clear_old(sp)
            with sp.If(sp.value_load(k.fits[0:1, 0:1], min_val=0, max_val=1) == 1):
                with sp.Fori(0, NW // U) as i:
                    for u in range(U):
                        w = U * i + u
                        at = sp.value_load(k.starts[0:1, bass.ds(w, 1)], min_val=0, max_val=E)
                        sp.wait_ge(pe_.sem, pe_.of(w - U, "ADJ"))
                        sp.dma_start(sd[:, u, :], d["sd"][bass.ds(at, S), :].rearrange("(p j) s -> p (j s)", j=T)).then_inc(in_[u], 16)
                        sp.dma_start(am[:, u, :], d["am"][bass.ds(at, S)].rearrange("(p j) -> p j", j=T)).then_inc(in_[u], 16)
                        sp.dma_start(msg[:, u, :], d["msg"][bass.ds(at, S), :].rearrange("(p j) f -> p (j f)", j=T)).then_inc(in_[u], 16)

        @block.gpsimd
        def _(pool):
            pool.iota(bounds[:, :], pattern=[[BM, NB - 1]], base=BM, channel_multiplier=0,
                      allow_small_or_imprecise_dtypes=True).then_inc(made, 1)
            pool.iota(iota_bm[:, :], pattern=[[1, BM]], base=0, channel_multiplier=0,
                      allow_small_or_imprecise_dtypes=True).then_inc(made, 1)
            pool.iota(iota_key[:, :], pattern=[[1, NB * WN]], base=-KEY0, channel_multiplier=0,
                      allow_small_or_imprecise_dtypes=True).then_inc(made, 1)
            pool.memset(base[:, :], 0.0).then_inc(made, 1)

        @block.vector
        def _(dve):
            with dve.If(dve.value_load(k.fits[0:1, 0:1], min_val=0, max_val=1) == 1):
                dve_.prime(dve)
                dve.wait_ge(made, 4)
                s = dve_.sem
                with dve.Fori(0, NW // U) as i:
                    for u in range(U):
                        w = U * i + u
                        sdv = sd[:, u, :].rearrange("p (j s) -> p s j", s=2)
                        dve.wait_ge(in_[u], (i + 1) * 48)
                        nc.vector.tensor_copy(srcf[:, u, :], sdv[:, 0, :]).then_inc(s, 1)
                        dve.wait_ge(s, dve_.of(w - 1, "BASE"))
                        nc.vector.tensor_scalar(dl[:, u, :], sdv[:, 1, :], base[:, 0:1], None, ALU.subtract).then_inc(s, 1)
                        dve.wait_ge(s, dve_.of(w, "SRC"))
                        nc.vector.tensor_tensor(ge[:, u, :, :], bc(srcf[:, u, :].unsqueeze(2), [128, T, NB - 1]),
                                                bc(bounds[:, :].unsqueeze(1), [128, T, NB - 1]), ALU.is_ge).then_inc(s, 1)
                        dve.wait_ge(s, dve_.of(w, "DL"))
                        dve.wait_ge(pe_.sem, pe_.of(w - U, "ADJ"))
                        nc.vector.tensor_tensor(sel[:, u, :, :], bc(k.iota_wn[:, :].unsqueeze(1), [128, T, WN]),
                                                bc(dl[:, u, :].unsqueeze(2), [128, T, WN]), ALU.is_equal).then_inc(s, 1)
                        nc.vector.tensor_scalar(ok1[:, u, :], dl[:, u, :], 0.0, None, ALU.is_ge).then_inc(s, 1)
                        dve.wait_ge(s, dve_.of(w, "GE"))
                        nc.vector.tensor_reduce(blk[:, u, :], ge[:, u, :, :], AX.X, ALU.add).then_inc(s, 1)
                        dve.wait_ge(s, dve_.of(w, "SEL"))
                        nc.vector.tensor_tensor(wsel[:, u, :, :], sel[:, u, :, :], bc(am[:, u, :].unsqueeze(2), [128, T, WN]),
                                                ALU.mult).then_inc(s, 1)
                        dve.wait_ge(s, dve_.of(w, "OK1"))
                        nc.vector.scalar_tensor_tensor(ok[:, u, :], dl[:, u, :], float(WN - 1), ok1[:, u, :], ALU.is_le,
                                                       ALU.mult).then_inc(s, 1)
                        dve.wait_ge(s, dve_.of(w, "BLK"))
                        nc.vector.scalar_tensor_tensor(res[:, u, :], blk[:, u, :], -float(BM), srcf[:, u, :], ALU.mult,
                                                       ALU.add).then_inc(s, 1)
                        nc.vector.scalar_tensor_tensor(key0[:, u, :], blk[:, u, :], float(WN), dl[:, u, :], ALU.mult,
                                                       ALU.add).then_inc(s, 1)
                        dve.wait_ge(s, dve_.of(w, "KEY0"))
                        nc.vector.scalar_tensor_tensor(key[:, u, :], ok[:, u, :], -float(KEY0), key0[:, u, :], ALU.mult,
                                                       ALU.add).then_inc(s, 1)
                        nc.vector.tensor_tensor(oh_res[:, u, :, :], bc(iota_bm[:, :].unsqueeze(1), [128, T, BM]),
                                                bc(res[:, u, :].unsqueeze(2), [128, T, BM]), ALU.is_equal).then_inc(s, 1)
                        dve.wait_ge(s, dve_.of(w, "KEY"))
                        for j in range(T):
                            nc.vector.tensor_scalar(oh_key[:, u, j, :], iota_key[:, :], key[:, u, j:j + 1], None,
                                                    ALU.is_equal).then_inc(s, 1)
                        nc.vector.tensor_scalar(base[:, :], base[:, :], float(WN), None, ALU.add).then_inc(s, 1)

        @block.tensor
        def _(pe):
            with pe.If(pe.value_load(k.fits[0:1, 0:1], min_val=0, max_val=1) == 1):
                pe_.prime(pe)
                with pe.Fori(0, NW // U) as i:
                    for u in range(U):
                        w = U * i + u
                        pe.wait_ge(in_[u], (i + 1) * 48)
                        pe.wait_ge(dve_.sem, dve_.of(w, "WSEL"))
                        pe.wait_ge(act_.sem, act_.of(w - 1, "DEG"))
                        for j in range(T):
                            m = nc.tensor.matmul(k.ps[:, 0, 0:WN], msg[:, u, j * D:(j + 1) * D], wsel[:, u, j, :],
                                                 start=j == 0, stop=j == T - 1)
                        m.then_inc(pe_.sem, 1)
                        for j in range(T):
                            m = nc.tensor.matmul(k.ps[0:1, 1, 0:WN], k.ones[:, 0:1], sel[:, u, j, :],
                                                 start=j == 0, stop=j == T - 1)
                        m.then_inc(pe_.sem, 1)
                        b = 2 + 3 * (u % 2)
                        pe.wait_ge(act_.sem, act_.of(w - (1 if u == 0 else 2), "ADJ"))
                        for j in range(T):
                            pe.wait_ge(dve_.sem, dve_.of(w, f"OH_KEY{j}"))
                            for q in range(3):
                                m = nc.tensor.matmul(k.ps[0:BM, b + q, 0:NB * WN // 3], oh_res[:, u, j, :],
                                                     oh_key[:, u, j, q * (NB * WN // 3):(q + 1) * (NB * WN // 3)],
                                                     start=j == 0, stop=j == T - 1)
                        m.then_inc(pe_.sem, 1)

        @block.scalar
        def _(act):
            with act.If(act.value_load(k.fits[0:1, 0:1], min_val=0, max_val=1) == 1):
                act_.prime(act)
                for u in range(U):
                    act.sem_inc(adj_out[u], 16)
                with act.Fori(0, NW // U) as i:
                    for u in range(U):
                        w = U * i + u
                        b = 2 + 3 * (u % 2)
                        act.wait_ge(pe_.sem, pe_.of(w, "AGG"))
                        act.sem_inc(hop["act"], 1)
                        nc.scalar.activation(aggT[:, bass.ds(w * WN, WN)], k.ps[:, 0, 0:WN], ACT.Copy).then_inc(act_.sem, 1)
                        act.wait_ge(pe_.sem, pe_.of(w, "DEG"))
                        act.sem_inc(hop["act"], 1)
                        nc.scalar.activation(deg[:, bass.ds(w * WN, WN)], k.ps[0:1, 1, 0:WN], ACT.Copy).then_inc(act_.sem, 1)
                        act.wait_ge(pe_.sem, pe_.of(w, "ADJ"))
                        act.sem_inc(hop["act"], 1)
                        act.wait_ge(adj_out[u], (i + 1) * 16)
                        nc.scalar.activation(adj[:, u, :].rearrange("p (q c) -> p q c", q=3), k.ps[0:BM, b:b + 3, 0:NB * WN // 3],
                                             ACT.Copy).then_inc(act_.sem, 1)
                        act.wait_ge(act_.sem, act_.of(w, "ADJ"))
                        act.sem_inc(hop["act"], 1)
                        act.dma_start(d["adj"][bass.ds(w, 1), :, :].rearrange("w p c -> (w p) c"), adj[:, u, :]).then_inc(adj_out[u], 16)
                act.dma_start(d["deg"].unsqueeze(0), deg[:, :]).then_inc(deg_out, 16)
                act.wait_ge(deg_out, 16)
                for u in range(U):
                    act.wait_ge(adj_out[u], 16 * (NW // U + 1))


def dense(k, name, outT, terms, bias=None, relu=False, add=None, parts=1):
    nc = k.nc
    with k.phase(name) as (sb, sem, block, hop):
        loads = []
        prog = []
        for p, ts in enumerate(terms):
            row = []
            for n, (src, feat) in enumerate(ts):
                w = sb(f"w{p}_{n}", [128, D])
                loads.append((w[:, :], src))
                row.append((w, feat))
            prog.append(row)
        bt = None
        if bias is not None:
            bt = sb("bt", [128, parts])
            loads.append((bt[:, :], bias))
        w_in, summed, moved, stored = (sem(n) for n in ("w_in", "summed", "moved", "stored"))
        tmp = sb("tmp", [128, 2, NCOL])

        @block.sync
        def _(sp):
            k.clear_old(sp)
            for to, src in loads:
                sp.dma_start(to, src).then_inc(w_in, 16)

        @block.tensor
        def _(pe):
            pe.wait_ge(w_in, 16 * len(loads))
            for n in range(NCH * parts):
                c, p = divmod(n, parts)
                if n >= 4:
                    pe.wait_ge(stored, n - 3)
                for q, (w, feat) in enumerate(prog[p]):
                    m = nc.tensor.matmul(k.ps[:, n % 4, 0:NCOL], w[:, :], feat[:, c * NCOL:(c + 1) * NCOL],
                                         start=q == 0, stop=q == len(prog[p]) - 1)
                m.then_inc(summed, 1)

        @block.vector
        def _(dve):
            dve.wait_ge(w_in, 16 * len(loads))
            for n in range(NCH * parts):
                c, p = divmod(n, parts)
                cols = slice(c * NCOL, (c + 1) * NCOL)
                dve.wait_ge(summed, n + 1)
                src = k.ps[:, n % 4, 0:NCOL]
                if bt is None:
                    if add is None:
                        nc.vector.tensor_copy(outT[:, p, cols], src).then_inc(stored, 1)
                    else:
                        nc.vector.tensor_tensor(outT[:, p, cols], add[:, cols], src, ALU.add).then_inc(stored, 1)
                elif add is not None:
                    nc.vector.scalar_tensor_tensor(outT[:, p, cols], src, bt[:, p:p + 1], add[:, cols], ALU.add,
                                                   ALU.add).then_inc(stored, 1)
                elif relu:
                    nc.vector.tensor_scalar(outT[:, p, cols], src, bt[:, p:p + 1], 0.0, ALU.add, ALU.max).then_inc(stored, 1)
                else:
                    nc.vector.tensor_scalar(outT[:, p, cols], src, bt[:, p:p + 1], None, ALU.add).then_inc(stored, 1)
            dve.wait_ge(stored, NCH * parts)


def attention_queries(k, l, h0, x):
    nc, d = k.nc, k.dram
    U = 3
    with k.phase(f"aq{l}") as (sb, sem, block, hop):
        wq = sb("wq", [D, H * D])
        wkT = sb("wkT", [D, H, D])
        we = sb("we", [D, H * D])
        w_eeT = sb("w_eeT", [D, 2 * D + GK])
        hb = sb("hb", [D, 4, H])
        keb = sb("keb", [D, H])
        eg = sb("eg", [D, H, D + GK])
        eh = sb("eh", [D, H * D])
        last = sb("last", [D, GK])
        q = sb("q", [D, U, H, CW])
        qk = sb("qk", [D, U, H, CW])
        qt = sb("qt", [D, U, WC, 2, H, WN])
        qg = sb("qg", [GK, U, WC, H, WN])
        w_in, made, mixed, mixed_c = sem("w_in"), sem("made"), sem("mixed"), sem("mixed_c")
        out = [sem(f"out{u}") for u in range(U)]
        q_ok = Steps(sem("q_ok"), ["Q"], U)
        kc_ok = Steps(sem("kc_ok"), ["KC"], U)
        both_ok = Steps(sem("both_ok"), [f"QK{h}" for h in range(H)], U)
        geo_ok = Steps(sem("geo_ok"), [f"G{h}" for h in range(H)], U)
        act_ = Steps(sem("act"), [f"Q{h}" for h in range(H)] + [f"QK{h}" for h in range(H)], U)
        dve_ = Steps(sem("dve"), [f"PROD{h}" for h in range(H)] + [f"G{h}" for h in range(H)], U)
        loads = [(wq[:, :], d["Wq"][l]), (wkT[:, :, :], d["WkT"][l].rearrange("(h c) i -> c h i", c=D)), (we[:, :], d["We"][l]),
                 (w_eeT[:, :], d["W_eeT"]), (hb[:, :, :], d["hb"][l])]

        @block.sync
        def _(sp):
            k.clear_old(sp)
            for to, src in loads:
                sp.dma_start(to, src).then_inc(w_in, 16)
            for u in range(U):
                sp.sem_inc(out[u], 32)
            with sp.Fori(0, NWC // U) as i:
                for u in range(U):
                    c = U * i + u
                    sp.wait_ge(act_.sem, act_.of(c, f"QK{H - 1}"))
                    sp.sem_inc(hop["pool"], 1)
                    sp.dma_start(d["qt"][bass.ds(c * WC, WC), :, :, :].rearrange("w k t n -> k w (t n)"),
                                 qt[:, u, :, :, :, :].rearrange("k w t h n -> k w (t h n)")).then_inc(out[u], 16)
                    sp.wait_ge(dve_.sem, dve_.of(c, f"G{H - 1}"))
                    sp.dma_start(d["qg"][bass.ds(c * WC, WC), :, :].rearrange("w k n -> k w n"),
                                 qg[:, u, :, :, :].rearrange("k w h n -> k w (h n)")).then_inc(out[u], 16)
            for u in range(U):
                sp.wait_ge(out[u], 32 * (NWC // U + 1))

        @block.gpsimd
        def _(pool):
            pool.memset(last[:, :], 0.0).then_inc(made, 1)
            pool.wait_ge(made, 1)
            pool.memset(last[:, GK - 1:GK], 1.0).then_inc(made, 1)

        @block.tensor
        def _(pe):
            pe.wait_ge(w_in, 16 * len(loads))
            pe.wait_ge(made, 2)
            for h in range(H):
                nc.tensor.matmul(k.ps[:, h, 0:D + GK], we[:, h * D:(h + 1) * D], w_eeT[:, D:2 * D + GK],
                                 start=True, stop=True).then_inc(mixed, 1)
            nc.tensor.matmul(k.ps[:, 3, 0:H * D], w_eeT[:, 0:D], we[:, :], start=True, stop=True).then_inc(mixed, 1)
            pe.wait_ge(mixed_c, 5)
            with pe.Fori(0, NWC // U) as i:
                def first(u):
                    c = U * i + u
                    cols = bass.ds(c * CW, CW)
                    pe.wait_ge(act_.sem, act_.of(c - 1, f"Q{H - 1}"))
                    for h in range(H):
                        m = nc.tensor.matmul(k.ps[:, h // 2, (h % 2) * CW:(h % 2 + 1) * CW], wq[:, h * D:(h + 1) * D],
                                             x[:, cols], start=True, stop=True)
                    m.then_inc(q_ok.sem, 1)
                    pe.wait_ge(dve_.sem, dve_.of(c - 1, f"PROD{H - 1}"))
                    for h in range(H):
                        m = nc.tensor.matmul(k.ps[:, 2 + h // 2, (h % 2) * CW:(h % 2 + 1) * CW], eh[:, h * D:(h + 1) * D],
                                             h0[:, cols], start=True, stop=True)
                    m.then_inc(kc_ok.sem, 1)

                def second(u):
                    c = U * i + u
                    for h in range(H):
                        pe.wait_ge(act_.sem, act_.of(c, f"Q{h}"))
                        if h < 2:
                            pe.wait_ge(act_.sem, act_.of(c - 1, f"QK{1 + h}"))
                        else:
                            pe.wait_ge(act_.sem, act_.of(c, "QK0"))
                        b = 4 + h % 2
                        nc.tensor.matmul(k.ps[:, b, 0:CW], wkT[:, h, :], q[:, u, h, :], start=True, stop=True)
                        nc.tensor.matmul(k.ps[:, b, CW:2 * CW], eg[:, h, 0:D], q[:, u, h, :], start=True, stop=True
                                         ).then_inc(both_ok.sem, 1)
                        pe.wait_ge(dve_.sem, dve_.of(c, f"PROD{h}"))
                        if h < 2:
                            pe.wait_ge(dve_.sem, dve_.of(c - 1, f"G{1 + h}"))
                        else:
                            pe.wait_ge(dve_.sem, dve_.of(c, "G0"))
                        b = 6 + h % 2
                        nc.tensor.matmul(k.ps[0:GK, b, 0:CW], eg[:, h, D:D + GK], q[:, u, h, :], start=True, stop=False)
                        nc.tensor.matmul(k.ps[0:GK, b, 0:CW], last[:, :], qk[:, u, h, :], start=False, stop=True
                                         ).then_inc(geo_ok.sem, 1)

                first(0)
                first(1)
                second(0)
                first(2)
                second(1)
                second(2)

        @block.scalar
        def _(act):
            act.wait_ge(w_in, 16 * len(loads))
            act_.prime(act)
            with act.Fori(0, NWC // U) as i:
                def queries(u):
                    c = U * i + u
                    act.wait_ge(q_ok.sem, c + 1)
                    for h in range(H):
                        nc.scalar.activation(q[:, u, h, :], k.ps[:, h // 2, (h % 2) * CW:(h % 2 + 1) * CW], ACT.Identity,
                                             bias=hb[:, 0, h:h + 1]).then_inc(act_.sem, 1)

                def keys(u):
                    c = U * i + u
                    act.wait_ge(out[u], (i + 1) * 32)
                    for h in range(H):
                        act.wait_ge(both_ok.sem, c * H + h + 1)
                        nc.scalar.activation(qt[:, u, :, :, h, :].rearrange("p w t n -> p t w n"),
                                             k.ps[:, 4 + h % 2, 0:2 * CW].rearrange("p (t w n) -> p t w n", t=2, n=WN),
                                             ACT.Copy).then_inc(act_.sem, 1)
                for u in range(U):
                    queries(u)
                    keys(u)

        @block.vector
        def _(dve):
            dve.wait_ge(w_in, 16 * len(loads))
            for h in range(H):
                dve.wait_ge(mixed, h + 1)
                nc.vector.tensor_copy(eg[:, h, :], k.ps[:, h, 0:D + GK]).then_inc(mixed_c, 1)
            dve.wait_ge(mixed, 4)
            nc.vector.tensor_copy(eh[:, :], k.ps[:, 3, 0:H * D]).then_inc(mixed_c, 1)
            nc.vector.tensor_tensor(keb[:, :], hb[:, 1, :], hb[:, 3, :], ALU.add).then_inc(mixed_c, 1)
            dve.wait_ge(mixed_c, 5)
            dve_.prime(dve)
            with dve.Fori(0, NWC // U) as i:
                for u in range(U):
                    c = U * i + u
                    dve.wait_ge(kc_ok.sem, c + 1)
                    for h in range(H):
                        dve.wait_ge(act_.sem, act_.of(c, f"Q{h}"))
                        nc.vector.scalar_tensor_tensor(qk[:, u, h, :], k.ps[:, 2 + h // 2, (h % 2) * CW:(h % 2 + 1) * CW],
                                                       keb[:, h:h + 1], q[:, u, h, :], ALU.add, ALU.mult).then_inc(dve_.sem, 1)
                    dve.wait_ge(out[u], (i + 1) * 32)
                    for h in range(H):
                        dve.wait_ge(geo_ok.sem, c * H + h + 1)
                        nc.vector.tensor_copy(qg[:, u, :, h, :], k.ps[0:GK, 6 + h % 2, 0:CW].rearrange("p (w n) -> p w n", n=WN)
                                              ).then_inc(dve_.sem, 1)


def attention_windows(k, l):
    nc, d = k.nc, k.dram
    U = 3
    W = D if l == 0 else 2 * D
    HS = S // 2
    JH = T // 2
    SCALE = float(D) ** -0.5
    table = d[f"lrows{l}"]
    with k.phase(f"aw{l}") as (sb, sem, block, hop):
        sd = sb("sd", [128, U, 2 * T], I32)
        geo = sb("geo", [128, U, T, GK])
        geoT = sb("geoT", [GK, U, S])
        qt = sb("qt", [D, U, 2, WH])
        qg = sb("qg", [GK, U, WH])
        g = sb("g", [128, U, T, W])
        dx = sb("dx", [128, U, T, D])
        base = sb("base", [128, 1])
        dl = sb("dl", [128, U, T])
        sel = sb("sel", [128, U, T, WN], BF16)
        off = sb("off", [128, U, T, H, WN], BF16)
        yT = sb("yT", [D, U, 2, S])
        p = sb("p", [WH, U, 2, HS])
        pT = sb("pT", [128, U, 2, JH * WH])
        mx, neg, den, den3, inv = (sb(n, [WH, U]) for n in ("mx", "neg", "den", "den3", "inv"))
        ag = sb("ag", [D, U, 2 * WH])
        agg = sb("agg", [GK, U, WH])
        base_ok = sem("base_ok")
        idx_in, in_, out = ([sem(f"{n}{u}") for u in range(U)] for n in ("idx_in", "in", "out"))
        rows_in, rows_base = k.rows_in, list(k.rows_base)
        turned = Steps(sem("turned"), ["T0", "T1", "T2"], U)
        scored = Steps(sem("scored"), ["S"], U)
        weights_turned = Steps(sem("weights_turned"), ["PT"], U)
        summed = Steps(sem("summed"), ["AG"], U)
        yT_ok = Steps(sem("yT_ok"), ["T0", "T1", "T2"], U)
        pT_ok = Steps(sem("pT_ok"), ["P0", "P1"], U)
        exped = Steps(sem("exped"), ["E"], U)
        ag_ok = Steps(sem("ag_ok"), ["X", "G"], U)
        ready = Steps(sem("ready"), ["DX", "DL", "SEL", "OFF", "BASE"], U)
        soft = Steps(sem("soft"), ["MAX", "NEG", "DEN", "INV", "P"], U)
        x0 = W - D

        @block.sync
        def _(sp):
            k.clear_old(sp)
            with sp.If(sp.value_load(k.fits[0:1, 0:1], min_val=0, max_val=1) == 1):
                with sp.Fori(0, NW // U) as i:
                    for u in range(U):
                        w = U * i + u
                        at = sp.value_load(k.starts[0:1, bass.ds(w, 1)], min_val=0, max_val=E)
                        sp.wait_ge(ready.sem, ready.of(w - U, "OFF"))
                        sp.dma_start(sd[:, u, :], d["sd"][bass.ds(at, S), :].rearrange("(p j) s -> p (j s)", j=T)).then_inc(idx_in[u], 16)
                        sp.wait_ge(summed.sem, summed.of(w - U, "AG"))
                        sp.dma_start(geo[:, u, :, :], d["geo"][bass.ds(at, S), :].rearrange("(p j) f -> p j f", j=T)).then_inc(in_[u], 16)
                        sp.dma_start(geoT[:, u, :], d["geoT"][:, bass.ds(at, S)]).then_inc(in_[u], 16)
                        sp.dma_start(qt[:, u, :, :], d["qt"][bass.ds(w, 1), :, :, :].rearrange("w k t n -> (w k) t n")).then_inc(in_[u], 16)
                        sp.dma_start(qg[:, u, :], d["qg"][bass.ds(w, 1), :, :].rearrange("w k n -> (w k) n")).then_inc(in_[u], 16)

        @block.gpsimd
        def _(pool):
            pool.memset(base[:, :], 0.0).then_inc(base_ok, 1)
            with pool.If(pool.value_load(k.fits[0:1, 0:1], min_val=0, max_val=1) == 1):
                with pool.Fori(0, NW // U) as i:
                    for u in range(U):
                        w = U * i + u
                        pool.wait_ge(summed.sem, summed.of(w - U, "AG"))
                        pool.sem_inc(hop["pool"], 1)
                        pool.wait_ge(idx_in[u], (i + 1) * 16)
                        pool.sem_inc(hop["pool"], 1)
                        for j in range(T):
                            pool.indirect_dma_start(out=g[:, u, j, :], out_offset=None, in_=table,
                                                    in_offset=bass.IndirectOffsetOnAxis(ap=sd[:, u, 2 * j:2 * j + 1], axis=0)
                                                    ).then_inc(rows_in[u], 16)

        @block.tensor
        def _(pe):
            def turn_features(w, u, i):
                pe.wait_ge(rows_in[u], (i + 1) * 16 * T + rows_base[u])
                pe.wait_ge(ready.sem, ready.of(w, "DX"))
                for n in range(3):
                    pe.wait_ge(yT_ok.sem, yT_ok.of(w - 1, f"T{n}"))
                    for q in range(4):
                        what, j = divmod(4 * n + q, T)
                        m = nc.tensor.transpose(k.ps[:, n, q * 128:(q + 1) * 128],
                                                dx[:, u, j, :] if what else g[:, u, j, 0:D], k.ident[:, :])
                    m.then_inc(turned.sem, 1)

            def scores(w, u, i):
                pe.wait_ge(in_[u], (i + 1) * 64)
                pe.wait_ge(ready.sem, ready.of(w, "OFF"))
                pe.wait_ge(exped.sem, exped.of(w - 1, "E"))
                for half in range(2):
                    to = k.ps[0:WH, 3 + half, 0:HS]
                    for j in range(JH):
                        nc.tensor.matmul(k.ps[0:WH, 3 + half, j * 128:(j + 1) * 128],
                                         off[:, u, half * JH + j, :, :].rearrange("p h n -> p (h n)"), k.far[:, :],
                                         start=j == 0, stop=False)
                    nc.tensor.matmul(to, qg[:, u, :], geoT[:, u, :].rearrange("f (p j) -> f j p", j=T)[:, half * JH:(half + 1) * JH, :],
                                     start=False, stop=False)
                    pe.wait_ge(yT_ok.sem, yT_ok.of(w, "T2"))
                    for t in range(2):
                        m = nc.tensor.matmul(to, qt[:, u, t, :], yT[:, u, t, half * HS:(half + 1) * HS], start=False, stop=t == 1)
                m.then_inc(scored.sem, 1)

            def turn_weights(w, u, i):
                pe.wait_ge(soft.sem, soft.of(w, "P"))
                pe.wait_ge(pT_ok.sem, pT_ok.of(w - 1, "P1"))
                for j in range(T):
                    m = nc.tensor.transpose(k.ps[:, 5 + j // JH, (j % JH) * WH:(j % JH + 1) * WH],
                                            p[:, u, j // JH, (j % JH) * 128:(j % JH + 1) * 128], k.ident[0:WH, 0:WH])
                m.then_inc(weights_turned.sem, 1)

            def sums(w, u, i):
                pe.wait_ge(pT_ok.sem, pT_ok.of(w, "P1"))
                pe.wait_ge(ag_ok.sem, ag_ok.of(w - 1, "G"))
                for t in range(3):
                    for j in range(T):
                        rows = (g[:, u, j, 0:D], dx[:, u, j, :], geo[:, u, j, :])[t]
                        m = nc.tensor.matmul(k.ps[0:rows.shape[1], 7, t * WH:(t + 1) * WH], rows,
                                             pT[:, u, j // JH, (j % JH) * WH:(j % JH + 1) * WH], start=j == 0, stop=j == T - 1)
                m.then_inc(summed.sem, 1)

            def turn(w, u, i):
                before = (w - 1, (u - 1) % U, i if u else i - 1)
                turn_features(w, u, i)
                turn_weights(*before)
                scores(w, u, i)
                sums(*before)

            with pe.If(pe.value_load(k.fits[0:1, 0:1], min_val=0, max_val=1) == 1):
                for s in (turned, scored, weights_turned, summed):
                    s.prime(pe)
                turn_features(0, 0, 0)
                scores(0, 0, 0)
                with pe.Fori(0, NW // U - 1) as i:
                    turn(U * i + 1, 1, i)
                    turn(U * i + 2, 2, i)
                    turn(U * i + 3, 0, i + 1)
                turn(NW - 2, 1, NW // U - 1)
                turn(NW - 1, 2, NW // U - 1)
                turn_weights(NW - 1, 2, NW // U - 1)
                sums(NW - 1, 2, NW // U - 1)

        @block.scalar
        def _(act):
            def copy_features(w, u, i):
                for n in range(3):
                    act.wait_ge(turned.sem, turned.of(w, f"T{n}"))
                    act.sem_inc(hop["act"], 1)
                    act.wait_ge(scored.sem, scored.of(w - U, "S"))
                    nc.scalar.activation(yT[:, u, :, :].rearrange("p t s -> p (t s)")[:, n * 512:(n + 1) * 512], k.ps[:, n, :],
                                         ACT.Copy).then_inc(yT_ok.sem, 1)

            def exponentials(w, u, i):
                act.wait_ge(soft.sem, soft.of(w, "NEG"))
                act.sem_inc(hop["act"], 1)
                act.wait_ge(weights_turned.sem, weights_turned.of(w - U, "PT"))
                nc.scalar.activation(p[:, u, :, :], k.ps[0:WH, 3:5, 0:HS], ACT.Exp, bias=neg[:, u:u + 1], scale=SCALE,
                                     accum_out=den[:, u:u + 1]).then_inc(exped.sem, 1)

            def copy_weights(w, u, i):
                act.wait_ge(weights_turned.sem, weights_turned.of(w, "PT"))
                act.sem_inc(hop["act"], 1)
                act.wait_ge(summed.sem, summed.of(w - U, "AG"))
                for half in range(2):
                    nc.scalar.activation(pT[:, u, half, :], k.ps[:, 5 + half, 0:JH * WH], ACT.Copy).then_inc(pT_ok.sem, 1)

            def copy_sums(w, u, i):
                act.wait_ge(summed.sem, summed.of(w, "AG"))
                act.sem_inc(hop["act"], 1)
                act.wait_ge(out[u], (i + 1) * 32)
                nc.scalar.activation(ag[:, u, :], k.ps[:, 7, 0:2 * WH], ACT.Copy).then_inc(ag_ok.sem, 1)
                nc.scalar.activation(agg[:, u, :], k.ps[0:GK, 7, 2 * WH:3 * WH], ACT.Copy).then_inc(ag_ok.sem, 1)
                act.wait_ge(ag_ok.sem, ag_ok.of(w, "G"))
                act.sem_inc(hop["act"], 1)
                act.dma_start(d["agx"][bass.ds(w, 1), :, :].rearrange("w k n -> (w k) n"), ag[:, u, :]).then_inc(out[u], 16)
                act.dma_start(d["agg"][bass.ds(w, 1), :, :].rearrange("w k n -> (w k) n"), agg[:, u, :]).then_inc(out[u], 16)

            def turn(w, u, i):
                before = (w - 1, (u - 1) % U, i if u else i - 1)
                copy_features(w, u, i)
                copy_weights(*before)
                exponentials(w, u, i)
                copy_sums(*before)

            with act.If(act.value_load(k.fits[0:1, 0:1], min_val=0, max_val=1) == 1):
                for s in (yT_ok, pT_ok, exped, ag_ok):
                    s.prime(act)
                for u in range(U):
                    act.sem_inc(out[u], 32)
                copy_features(0, 0, 0)
                exponentials(0, 0, 0)
                with act.Fori(0, NW // U - 1) as i:
                    turn(U * i + 1, 1, i)
                    turn(U * i + 2, 2, i)
                    turn(U * i + 3, 0, i + 1)
                turn(NW - 2, 1, NW // U - 1)
                turn(NW - 1, 2, NW // U - 1)
                copy_weights(NW - 1, 2, NW // U - 1)
                copy_sums(NW - 1, 2, NW // U - 1)
                for u in range(U):
                    act.wait_ge(out[u], 32 * (NW // U + 1))

        @block.vector
        def _(dve):
            def inputs(w, u, i):
                dve.wait_ge(rows_in[u], (i + 1) * 16 * T + rows_base[u])
                dve.wait_ge(in_[u], (i + 1) * 64)
                dve.wait_ge(summed.sem, summed.of(w - U, "AG"))
                s = ready.sem
                nc.vector.tensor_tensor(dx[:, u, :, :], g[:, u, :, x0:x0 + D], bc(geo[:, u, :, 0:1], [128, T, D]),
                                        ALU.mult).then_inc(s, 1)
                dve.wait_ge(s, ready.of(w - 1, "BASE"))
                nc.vector.tensor_scalar(dl[:, u, :], sd[:, u, :].rearrange("p (j s) -> p s j", s=2)[:, 1, :], base[:, 0:1], None,
                                        ALU.subtract).then_inc(s, 1)
                dve.wait_ge(s, ready.of(w, "DL"))
                nc.vector.tensor_tensor(sel[:, u, :, :], bc(k.iota_wn[:, :].unsqueeze(1), [128, T, WN]),
                                        bc(dl[:, u, :].unsqueeze(2), [128, T, WN]), ALU.is_equal).then_inc(s, 1)
                dve.wait_ge(s, ready.of(w, "SEL"))
                nc.vector.tensor_scalar(off[:, u, :, :, :], bc(sel[:, u, :, :].unsqueeze(2), [128, T, H, WN]), -1.0, None, ALU.add).then_inc(s, 1)
                nc.vector.tensor_scalar(base[:, :], base[:, :], float(WN), None, ALU.add).then_inc(s, 1)

            def maximum(w, u, i):
                s = soft.sem
                dve.wait_ge(scored.sem, scored.of(w, "S"))
                nc.vector.tensor_reduce(mx[:, u:u + 1], k.ps[0:WH, 3:5, 0:HS], AX.XY, ALU.max).then_inc(s, 1)
                dve.wait_ge(s, soft.of(w, "MAX"))
                nc.vector.tensor_scalar(neg[:, u:u + 1], mx[:, u:u + 1], FLOOR, -SCALE, ALU.max, ALU.mult).then_inc(s, 1)

            def normalise(w, u, i):
                s = soft.sem
                dve.wait_ge(exped.sem, exped.of(w, "E"))
                nc.vector.tensor_scalar(den3[:, u:u + 1], den[:, u:u + 1], 1e-16, float(H), ALU.add, ALU.mult).then_inc(s, 1)
                dve.wait_ge(s, soft.of(w, "DEN"))
                nc.vector.reciprocal(inv[:, u:u + 1], den3[:, u:u + 1]).then_inc(s, 1)
                dve.wait_ge(s, soft.of(w, "INV"))
                nc.vector.tensor_scalar(p[:, u, :, :], p[:, u, :, :], inv[:, u:u + 1], None, ALU.mult).then_inc(s, 1)

            def turn(w, u, i, more=True):
                maximum(w, u, i)
                if more:
                    inputs(w + 1, (u + 1) % U, i if u < U - 1 else i + 1)
                normalise(w, u, i)

            with dve.If(dve.value_load(k.fits[0:1, 0:1], min_val=0, max_val=1) == 1):
                ready.prime(dve)
                soft.prime(dve)
                dve.wait_ge(base_ok, 1)
                inputs(0, 0, 0)
                with dve.Fori(0, NW // U - 1) as i:
                    for u in range(U):
                        turn(U * i + u, u, i)
                for u in range(U):
                    turn(NW - U + u, u, NW // U - 1, more=u < U - 1)
        for u in range(U):
            k.rows_base[u] += NW // U * 16 * T


def attention_outputs(k, l, h0, x, outT):
    nc, d = k.nc, k.dram
    U = 3
    with k.phase(f"ao{l}") as (sb, sem, block, hop):
        wv = sb("wv", [D, H * D])
        we = sb("we", [D, H * D])
        w_eeT = sb("w_eeT", [D, 2 * D + GK])
        ws = sb("ws", [D, D])
        wr = sb("wr", [D, D])
        hb = sb("hb", [D, 4, H])
        bs = sb("bs", [D, 4])
        veb = sb("veb", [D, H])
        bias = sb("bias", [D, 1])
        eh, ex = sb("eh", [D, H * D]), sb("ex", [D, H * D])
        eg = sb("eg", [GK, H * D])
        last = sb("last", [GK, D])
        ax = sb("ax", [D, U, WC, 2, H, WN])
        ag = sb("ag", [GK, U, WC, H, WN])
        z = sb("z", [D, U, H, CW])
        z01, z2, y, y2 = (sb(n, [D, U, CW]) for n in ("z01", "z2", "y", "y2"))
        kcs = sb("kcs", [D, U, H, CW])
        w_in, made, mixed, mixed_c = sem("w_in"), sem("made"), sem("mixed"), sem("mixed_c")
        in_ = [sem(f"in{u}") for u in range(U)]
        pe_ = Steps(sem("pe"), ["OUT", "KC", "SW"], U)
        act_ = Steps(sem("act"), [f"KC{h}" for h in range(H)], U)
        dve_ = Steps(sem("dve"), [f"Z{h}" for h in range(H)] + ["Z01", "ZZ", "Y", "OUT"] + (["RELU"] if l else []), U)
        loads = [(wv[:, :], d["Wv"][l]), (we[:, :], d["We"][l]), (w_eeT[:, :], d["W_eeT"]), (ws[:, :], d["Ws"][l]),
                 (wr[:, :], d["W_res"]), (hb[:, :, :], d["hb"][l]), (bs[:, :], d["bs"])]

        @block.sync
        def _(sp):
            k.clear_old(sp)
            for to, src in loads:
                sp.dma_start(to, src).then_inc(w_in, 16)
            with sp.Fori(0, NWC // U) as i:
                for u in range(U):
                    c = U * i + u
                    sp.wait_ge(pe_.sem, pe_.of(c - U, "SW"))
                    sp.dma_start(ax[:, u, :, :, :, :].rearrange("k w t h n -> k w (t h n)"),
                                 d["agx"][bass.ds(c * WC, WC), :, :].rearrange("w k n -> k w n")).then_inc(in_[u], 16)
                    sp.dma_start(ag[:, u, :, :, :].rearrange("k w h n -> k w (h n)"),
                                 d["agg"][bass.ds(c * WC, WC), :, :].rearrange("w k n -> k w n")).then_inc(in_[u], 16)

        @block.gpsimd
        def _(pool):
            pool.memset(last[:, :], 1.0).then_inc(made, 1)
            pool.wait_ge(made, 1)
            pool.affine_select(out=last[:, :], in_=last[:, :], compare_op=ALU.is_ge, fill=0.0, base=-(GK - 1),
                               pattern=[[0, D]], channel_multiplier=1).then_inc(made, 1)

        @block.tensor
        def _(pe):
            pe.wait_ge(w_in, 16 * len(loads))
            pe.wait_ge(made, 2)
            nc.tensor.matmul(k.ps[:, 0, 0:H * D], w_eeT[:, 0:D], we[:, :], start=True, stop=True)
            nc.tensor.matmul(k.ps[:, 1, 0:H * D], w_eeT[:, D:2 * D], we[:, :], start=True, stop=True)
            nc.tensor.matmul(k.ps[0:GK, 2, 0:H * D], w_eeT[:, 2 * D:2 * D + GK], we[:, :], start=True, stop=True).then_inc(mixed, 1)
            pe.wait_ge(mixed_c, 5)
            pe_.prime(pe)
            with pe.Fori(0, NWC // U) as i:
                for u in range(U):
                    c = U * i + u
                    cols = bass.ds(c * CW, CW)
                    b = u % 2
                    pe.wait_ge(in_[u], (i + 1) * 32)
                    pe.wait_ge(dve_.sem, dve_.of(c - (1 if u == 0 else 2), "Y"))
                    to = k.ps[:, b, 0:CW]
                    nc.tensor.matmul(to, ws[:, :], x[:, cols], start=True, stop=False)
                    if l == 0:
                        nc.tensor.matmul(to, wr[:, :], x[:, cols], start=False, stop=False)
                    for h in range(H):
                        hs = slice(h * D, (h + 1) * D)
                        nc.tensor.matmul(to, wv[:, hs], ax[:, u, :, 0, h, :], start=False, stop=False)
                        nc.tensor.matmul(to, ex[:, hs], ax[:, u, :, 1, h, :], start=False, stop=False)
                        m = nc.tensor.matmul(to, eg[:, hs], ag[:, u, :, h, :], start=False, stop=h == H - 1)
                    m.then_inc(pe_.sem, 1)
                    pe.wait_ge(act_.sem, act_.of(c - 1, f"KC{H - 1}"))
                    for h in range(H):
                        m = nc.tensor.matmul(k.ps[:, 2 + h // 2, (h % 2) * CW:(h % 2 + 1) * CW], eh[:, h * D:(h + 1) * D],
                                             h0[:, cols], start=True, stop=True)
                    m.then_inc(pe_.sem, 1)
                    pe.wait_ge(dve_.sem, dve_.of(c - 1, f"Z{H - 1}"))
                    for h in range(H):
                        m = nc.tensor.matmul(k.ps[:, 4 + h // 2, (h % 2) * CW:(h % 2 + 1) * CW], last[:, :],
                                             ag[:, u, :, h, :], start=True, stop=True)
                    m.then_inc(pe_.sem, 1)

        @block.scalar
        def _(act):
            act_.prime(act)
            act.wait_ge(mixed_c, 5)
            with act.Fori(0, NWC // U) as i:
                for u in range(U):
                    c = U * i + u
                    act.wait_ge(pe_.sem, pe_.of(c, "KC"))
                    act.sem_inc(hop["act"], 1)
                    act.wait_ge(dve_.sem, dve_.of(c - U, f"Z{H - 1}"))
                    act.sem_inc(hop["act"], 1)
                    for h in range(H):
                        nc.scalar.activation(kcs[:, u, h, :], k.ps[:, 2 + h // 2, (h % 2) * CW:(h % 2 + 1) * CW], ACT.Identity,
                                             bias=veb[:, h:h + 1]).then_inc(act_.sem, 1)

        @block.vector
        def _(dve):
            s = dve_.sem
            dve.wait_ge(w_in, 16 * len(loads))
            dve.wait_ge(mixed, 1)
            nc.vector.tensor_copy(eh[:, :], k.ps[:, 0, 0:H * D]).then_inc(mixed_c, 1)
            nc.vector.tensor_copy(ex[:, :], k.ps[:, 1, 0:H * D]).then_inc(mixed_c, 1)
            nc.vector.tensor_copy(eg[:, :], k.ps[0:GK, 2, 0:H * D]).then_inc(mixed_c, 1)
            nc.vector.tensor_tensor(veb[:, :], hb[:, 2, :], hb[:, 3, :], ALU.add).then_inc(mixed_c, 1)
            if l == 0:
                nc.vector.tensor_tensor(bias[:, :], bs[:, 0:1], bs[:, 3:4], ALU.add).then_inc(mixed_c, 1)
            else:
                nc.vector.tensor_copy(bias[:, :], bs[:, l:l + 1]).then_inc(mixed_c, 1)
            dve.wait_ge(mixed_c, 5)
            dve_.prime(dve)
            with dve.Fori(0, NWC // U) as i:
                for u in range(U):
                    c = U * i + u
                    cols = bass.ds(c * CW, CW)
                    dve.wait_ge(pe_.sem, pe_.of(c, "SW"))
                    for h in range(H):
                        dve.wait_ge(act_.sem, act_.of(c, f"KC{h}"))
                        nc.vector.tensor_tensor(z[:, u, h, :], kcs[:, u, h, :], k.ps[:, 4 + h // 2, (h % 2) * CW:(h % 2 + 1) * CW],
                                                ALU.mult).then_inc(s, 1)
                    dve.wait_ge(s, dve_.of(c, "Z2"))
                    nc.vector.tensor_tensor(z01[:, u, :], z[:, u, 0, :], z[:, u, 1, :], ALU.add).then_inc(s, 1)
                    dve.wait_ge(s, dve_.of(c, "Z01"))
                    nc.vector.tensor_tensor(z2[:, u, :], z01[:, u, :], z[:, u, 2, :], ALU.add).then_inc(s, 1)
                    dve.wait_ge(s, dve_.of(c, "ZZ"))
                    nc.vector.scalar_tensor_tensor(y[:, u, :], k.ps[:, u % 2, 0:CW], bias[:, 0:1], z2[:, u, :], ALU.add,
                                                   ALU.add).then_inc(s, 1)
                    dve.wait_ge(s, dve_.of(c, "Y"))
                    if l == 0:
                        nc.vector.tensor_scalar(outT[:, cols], y[:, u, :], 0.0, None, ALU.max).then_inc(s, 1)
                    else:
                        nc.vector.tensor_tensor(y2[:, u, :], y[:, u, :], x[:, cols], ALU.add).then_inc(s, 1)
                        dve.wait_ge(s, dve_.of(c, "OUT"))
                        nc.vector.tensor_scalar(outT[:, cols], y2[:, u, :], 0.0, None, ALU.max).then_inc(s, 1)
            dve.wait_ge(s, dve_.of(NWC - 1, "RELU" if l else "OUT"))


def attention_layers(k):
    nc, d = k.nc, k.dram
    with ExitStack() as l1:
        h0 = l1.enter_context(nc.sbuf_tensor("l1_h0", [128, 1, NP], F32))
        x = l1.enter_context(nc.sbuf_tensor("l1_x", [128, 1, NP], F32))
        layer_norm(k, "ln1", k.xT[:, :].unsqueeze(1), h0, relu=True)
        node_rows(k, "lr0", h0[:, 0, :], None, D, [(d["lrows0"], 0, D), (d["lrows1"][:, D:2 * D], 0, D), (d["lrows2"][:, D:2 * D], 0, D)])
        now = h0
        for l in range(3):
            attention_queries(k, l, h0[:, 0, :], now[:, 0, :])
            attention_windows(k, l)
            attention_outputs(k, l, h0[:, 0, :], now[:, 0, :], x[:, 0, :])
            now = x
            if l < 2:
                node_rows(k, f"lr{l + 1}", x[:, 0, :], None, D, [(d[f"lrows{l + 1}"][:, 0:D], 0, D)])
        dense(k, "ctr", k.xT[:, :].unsqueeze(1), [[(d["W_ctr"][0:D, :], h0[:, 0, :]), (d["W_ctr"][D:2 * D, :], x[:, 0, :])]],
              bias=d["b_ctr"], add=k.xT[:, :])


def degree_scales(k, inv_deg, dinv):
    nc, d = k.nc, k.dram
    with k.phase("deg") as (sb, sem, block, hop):
        deg, root = sb("deg", [128, NP]), sb("root", [128, NP])
        deg_in, most_ok, root_ok, done = (sem(n) for n in ("deg_in", "most_ok", "root_ok", "done"))

        @block.sync
        def _(sp):
            k.clear_old(sp)
            sp.dma_start(deg[:, :], d["deg"].partition_broadcast(128)).then_inc(deg_in, 16)

        @block.scalar
        def _(act):
            act.wait_ge(deg_in, 16)
            nc.scalar.activation(root[:, :], deg[:, :], ACT.Sqrt, bias=k.ones[:, 0:1]).then_inc(root_ok, 1)

        @block.vector
        def _(dve):
            dve.wait_ge(deg_in, 16)
            nc.vector.tensor_scalar(inv_deg[:, :], deg[:, :], 1.0, None, ALU.max).then_inc(most_ok, 1)
            dve.wait_ge(most_ok, 1)
            nc.vector.reciprocal(inv_deg[:, :], inv_deg[:, :]).then_inc(done, 1)
            dve.wait_ge(root_ok, 1)
            nc.vector.reciprocal(dinv[:, :], root[:, :]).then_inc(done, 1)
            dve.wait_ge(done, 2)


def aggregate(k, name, h, out, scale, parts=1, loops=False, bias=None):
    nc, d = k.nc, k.dram
    GB = 4
    groups = [(g, p) for g in range(-(-NB // GB)) for p in range(parts)]
    chunks = [(c, p) for c in range(-(-NW // AW)) for p in range(parts)]
    with k.phase(name) as (sb, sem, block, hop):
        table = sb("table", [BM, parts, 3, NB, D], BF16)
        rest = sb("rest", [BM, 2, GB, D])
        adj = sb("adj", [BM, 2, AW, NB * WN], BF16)
        tmp = sb("tmp", [128, 2, AW * WN])
        scaled, turned, hi_ok, rest_ok, mid_ok, lo_ok, summed, added, times_ok, stored = (
            sem(n) for n in ("scaled", "turned", "hi_ok", "rest_ok", "mid_ok", "lo_ok", "summed", "added", "times_ok", "stored"))
        adj_in = [sem(f"adj_in{u}") for u in range(2)]
        bias_in = sem("bias_in")
        bt = None
        if bias is not None:
            bt = sb("bt", [128, 1])

        def blocks(g):
            return range(g * GB, min((g + 1) * GB, NB))

        def windows(c):
            return min(AW, NW - c * AW)

        @block.sync
        def _(sp):
            k.clear_old(sp)
            if bt is not None:
                sp.dma_start(bt[:, :], bias).then_inc(bias_in, 16)
            for c in range(len(chunks) // parts):
                if c >= 2:
                    sp.wait_ge(summed, parts * (c - 1))
                n = windows(c)
                sp.dma_start(adj[:, c % 2, 0:n, :], d["adj"][c * AW:c * AW + n, :, :].rearrange("w m q -> m w q")).then_inc(adj_in[c % 2], 16)

        @block.tensor
        def _(pe):
            for n, (g, p) in enumerate(groups):
                if loops:
                    pe.wait_ge(scaled, n + 1)
                if n >= 2:
                    pe.wait_ge(rest_ok, n - 1)
                for q, b in enumerate(blocks(g)):
                    m = nc.tensor.transpose(k.ps[0:BM, n % 2, q * D:(q + 1) * D], h[:, p, b * BM:(b + 1) * BM], k.ident[:, :])
                m.then_inc(turned, 1)
            pe.wait_ge(lo_ok, len(groups))
            for n, (c, p) in enumerate(chunks):
                pe.wait_ge(adj_in[c % 2], 16 * (c // 2 + 1))
                if n >= 4:
                    pe.wait_ge(stored if not loops else added, n - 3)
                cols = windows(c)
                for b in range(NB):
                    for t in range(3):
                        m = nc.tensor.matmul(k.ps[:, 2 + n % 4, 0:cols * WN], table[:, p, t, b, :],
                                             adj[:, c % 2, 0:cols, b * WN:(b + 1) * WN],
                                             start=b == 0 and t == 0, stop=b == NB - 1 and t == 2)
                m.then_inc(summed, 1)

        @block.scalar
        def _(act):
            def middle(n):
                g, p = groups[n]
                b = blocks(g)
                act.wait_ge(rest_ok, n + 1)
                nc.scalar.activation(table[:, p, 1, b.start:b.stop, :], rest[:, n % 2, 0:len(b), :], ACT.Copy).then_inc(mid_ok, 1)

            for n, (g, p) in enumerate(groups):
                b = blocks(g)
                act.wait_ge(turned, n + 1)
                nc.scalar.activation(table[:, p, 0, b.start:b.stop, :],
                                     k.ps[0:BM, n % 2, 0:len(b) * D].rearrange("m (b f) -> m b f", f=D), ACT.Copy).then_inc(hi_ok, 1)
                if n:
                    middle(n - 1)
            middle(len(groups) - 1)

        @block.vector
        def _(dve):
            if loops:
                for g, p in groups:
                    b = blocks(g)
                    cols = slice(b.start * BM, b.stop * BM)
                    nc.vector.tensor_tensor(h[:, p, cols], h[:, p, cols], scale[:, cols], ALU.mult).then_inc(scaled, 1)

            def lowest(n):
                g, p = groups[n]
                b = blocks(g)
                dve.wait_ge(mid_ok, n + 1)
                nc.vector.tensor_tensor(table[:, p, 2, b.start:b.stop, :], rest[:, n % 2, 0:len(b), :],
                                        table[:, p, 1, b.start:b.stop, :], ALU.subtract).then_inc(lo_ok, 1)

            for n, (g, p) in enumerate(groups):
                b = blocks(g)
                dve.wait_ge(hi_ok, n + 1)
                if n >= 2:
                    dve.wait_ge(lo_ok, n - 1)
                nc.vector.tensor_tensor(rest[:, n % 2, 0:len(b), :],
                                        k.ps[0:BM, n % 2, 0:len(b) * D].rearrange("m (b f) -> m b f", f=D),
                                        table[:, p, 0, b.start:b.stop, :], ALU.subtract).then_inc(rest_ok, 1)
                if n:
                    lowest(n - 1)
            lowest(len(groups) - 1)
            if bt is not None:
                dve.wait_ge(bias_in, 16)
            if loops:
                dve.wait_ge(scaled, len(groups))
            for n, (c, p) in enumerate(chunks):
                size = windows(c) * WN
                cols = slice(c * AW * WN, c * AW * WN + size)
                dve.wait_ge(summed, n + 1)
                sums = k.ps[:, 2 + n % 4, 0:size]
                if not loops:
                    nc.vector.tensor_tensor(out[:, p, cols], sums, scale[:, cols], ALU.mult).then_inc(stored, 1)
                    continue
                if n >= 2:
                    dve.wait_ge(times_ok, n - 1)
                nc.vector.tensor_tensor(tmp[:, n % 2, 0:size], sums, h[:, p, cols], ALU.add).then_inc(added, 1)
                dve.wait_ge(added, n + 1)
                nc.vector.tensor_tensor(out[:, p, cols], tmp[:, n % 2, 0:size], scale[:, cols], ALU.mult).then_inc(times_ok, 1)
                if bt is not None:
                    dve.wait_ge(times_ok, n + 1)
                    nc.vector.tensor_scalar(out[:, p, cols], out[:, p, cols], bt[:, 0:1], 0.0, ALU.add, ALU.max).then_inc(stored, 1)
            if loops:
                dve.wait_ge(times_ok, len(chunks))
            if bt is not None or not loops:
                dve.wait_ge(stored, len(chunks))


def adjacency_layers(k):
    nc, d = k.nc, k.dram
    x3 = k.xT[:, :].unsqueeze(1)
    with ExitStack() as both:
        inv_deg = both.enter_context(nc.sbuf_tensor("inv_deg", [128, NP], F32))
        dinv = both.enter_context(nc.sbuf_tensor("dinv", [128, NP], F32))
        degree_scales(k, inv_deg, dinv)
        with ExitStack() as l2:
            h, sums, h1 = (l2.enter_context(nc.sbuf_tensor(f"l2_{n}", [128, 1, NP], F32)) for n in ("h", "sums", "h1"))
            layer_norm(k, "ln2", x3, h, relu=True)
            aggregate(k, "n0", h, sums, inv_deg)
            dense(k, "sage0", h1, [[(d["W_self0T"], h[:, 0, :]), (d["W_neigh0T"], sums[:, 0, :])]], bias=d["b20"], relu=True)
            aggregate(k, "n1", h1, sums, inv_deg)
            dense(k, "sage1", x3, [[(d["W_self1T"], h1[:, 0, :]), (d["W_neigh1T"], sums[:, 0, :])]], bias=d["b21"], add=k.xT[:, :])
        with ExitStack() as l3:
            a, b = (l3.enter_context(nc.sbuf_tensor(f"l3_{n}", [128, 2, NP], F32)) for n in ("a", "b"))
            col = l3.enter_context(nc.sbuf_tensor("l3_col", [128, 10], F32))
            with k.phase("l3w") as (sb, sem, block, hop):
                w_in = sem("w_in")
                at = 0
                cols = {}
                for n, size in (("g1", 2), ("be1", 2), ("g2", 2), ("be2", 2), ("g3", 1), ("be3", 1)):
                    cols[n] = col[:, at:at + size]
                    at += size

                @block.sync
                def _(sp):
                    k.clear_old(sp)
                    for n, to in cols.items():
                        sp.dma_start(to, d["c" + n]).then_inc(w_in, 16)
                    sp.wait_ge(w_in, 16 * len(cols))

            def blocks(name, p, q):
                return d["g" + name][p * D:(p + 1) * D, q * D:(q + 1) * D]

            layer_norm(k, "ln3", x3, a[:, 0:1, :], relu=True)
            aggregate(k, "c1", a, a, dinv, loops=True)
            dense(k, "gcn1", b, [[(blocks("W1", 0, q), a[:, 0, :])] for q in range(2)], bias=d["cb1"], relu=True, parts=2)
            layer_norm(k, "lnc1", b, a, parts=2, gain=cols["g1"], shift=cols["be1"])
            aggregate(k, "c2", a, a, dinv, parts=2, loops=True)
            dense(k, "gcn2", b, [[(blocks("W2", p, q), a[:, p, :]) for p in range(2)] for q in range(2)], bias=d["cb2"], relu=True, parts=2)
            layer_norm(k, "lnc2", b, a, parts=2, gain=cols["g2"], shift=cols["be2"])
            dense(k, "gcn3", b, [[(blocks("W3", p, 0), a[:, p, :]) for p in range(2)]])
            aggregate(k, "c3", b, b, dinv, loops=True, bias=d["cb3"])
            layer_norm(k, "lnc3", b[:, 0:1, :], x3, gain=cols["g3"], shift=cols["be3"], add=True)


def gnn_kernel(nc, dram, out):
    with ExitStack() as ctx:
        k = Kit(nc, dram, ctx)
        prepare(k)
        with ExitStack() as l0:
            hT = l0.enter_context(nc.sbuf_tensor("l0_hT", [128, 1, NP], F32))
            x3 = k.xT[:, :].unsqueeze(1)
            layer_norm(k, "ln0", x3, hT, relu=True)
            d = dram
            node_rows(k, "rows0", hT[:, 0, :], [(0, D, d["W_node"]), (D, D // 2, d["aW1"][0:D // 2, :]),
                                                (2 * D, D // 2, d["aW1"][D // 2:D, :])], 3 * D,
                      [(d["rows0"], 0, 2 * D), (d["rows0d"], 2 * D, D)])
            with ExitStack() as l0a:
                a_all = l0a.enter_context(nc.sbuf_tensor("a_all", [128, NC, 4, AH], F32))
                edge_messages(k, a_all)
                edge_softmax(k, a_all)
            aggT = l0.enter_context(nc.sbuf_tensor("l0_aggT", [128, NP], F32))
            window_sums(k, aggT)
            dense(k, "out0", hT, [[(d["W_out"], aggT)]], add=hT[:, 0, :])
            layer_norm(k, "ln0b", hT, x3, add=True)
        if STOP > 1:
            attention_layers(k)
        if STOP > 2:
            adjacency_layers(k)
        with k.phase("end") as (sb, sem, block, hop):
            done = sem("done")

            @block.sync
            def _(sp):
                k.clear_old(sp)
                sp.dma_start(out, k.xT[:, :]).then_inc(done, 16)
                sp.wait_ge(done, 16)


STOP = 9


def kernel(**inputs):
    import numpy as np
    import concourse.bacc as bacc
    from concourse.bass_utils import run_bass_kernel_spmd as run

    a = {n: np.ascontiguousarray(v) for n, v in inputs.items()}
    f32 = np.float32
    src = np.zeros(EW, np.int32)
    dst = np.full(EW, NP - 1, np.int32)
    src[:E], dst[:E] = a["src"], a["dst"]

    def chunked(v):
        full = np.zeros((EP, v.shape[1]), f32)
        full[:E] = v
        return np.ascontiguousarray(full.reshape(NC, 128, 4, -1).transpose(0, 3, 2, 1)).reshape(NC, v.shape[1], CE)

    geo = np.zeros((EW, GK), f32)
    geo[:E, 0:1], geo[:E, 1:1 + GEO] = a["edge_weight1"], a["edge_attr_20"]
    geo[:, GK - 1] = 1.0
    xT = np.zeros((D, NP), f32)
    xT[:, :N] = a["x"].T
    p0, p1, p2, p3 = "L0_gnn_", "L1_gnn_", "L2_gnn_", "L3_gnn_"
    col = lambda v: np.ascontiguousarray(v.reshape(-1, D).T)
    host = {
        "xT": xT, "sd": np.stack([src, dst], 1), "dst": dst, "geo": geo, "geoT": np.ascontiguousarray(geo.T),
        "ea32": chunked(a["edge_attr_32"]), "sh16": chunked(a["edge_attr_16"]),
        "em_bias": np.stack([a[p0 + n] for n in ("b1", "b2", "ab1", "ab2")], 1),
        "b3": a[p0 + "b3"], "ab3": a[p0 + "ab3"],
        "W_eeT": np.ascontiguousarray(np.concatenate([a[p1 + "W_ee"], a[p1 + "b_ee"][None]], 0).T),
        "WkT": np.ascontiguousarray(a[p1 + "Wk"].transpose(0, 2, 1)),
        "hb": np.ascontiguousarray(np.stack([a[p1 + n].reshape(3, H, D) for n in ("bq", "bk", "bv", "be")], 1).transpose(0, 3, 1, 2)),
        "bs": np.stack([a[p1 + "bs"][0], a[p1 + "bs"][1], a[p1 + "bs"][2], a[p1 + "b_res"]], 1), "b_ctr": col(a[p1 + "b_ctr"]),
        "b20": col(a[p2 + "b0"]), "b21": col(a[p2 + "b1"]),
    }
    for n in ("W_node", "fc1", "fc2", "fc3", "W_sh", "aW1", "aW2", "aW3", "W_out"):
        host[n] = a[p0 + n]
    for n in ("W_res", "Wq", "Wv", "We", "Ws", "W_ctr"):
        host[n] = a[p1 + n]
    for n in ("W_self0", "W_neigh0", "W_self1", "W_neigh1"):
        host[n + "T"] = np.ascontiguousarray(a[p2 + n].T)
    for n in ("W1", "W2", "W3"):
        host["g" + n] = a[p3 + n]
    for n in ("b1", "g1", "be1", "b2", "g2", "be2", "b3", "g3", "be3"):
        host["c" + n] = col(a[p3 + n])

    nc = bacc.Bacc("TRN2", target_bir_lowering=False, num_devices=1)
    arrays, dram = {}, {}
    for n, v in host.items():
        arrays["in_" + n] = np.ascontiguousarray(v)
        dram[n] = nc.dram_tensor("in_" + n, v.shape, mybir.dt.from_np(v.dtype), kind="ExternalInput").ap()
    for n, shape, dt in (("rows0", (NP, 2 * D), F32), ("rows0d", (NP, D), F32), ("msg", (EW, D), F32), ("am", (EW,), F32),
                         ("adj", (NW, BM, NB * WN), BF16), ("deg", (NP,), F32),
                         ("lrows0", (NP, D), F32), ("lrows1", (NP, 2 * D), F32), ("lrows2", (NP, 2 * D), F32),
                         ("qt", (NW, D, 2, WH), F32), ("qg", (NW, GK, WH), F32), ("agx", (NW, D, 2 * WH), F32), ("agg", (NW, GK, WH), F32)):
        dram[n] = nc.dram_tensor("s_" + n, shape, dt).ap()
    out = nc.dram_tensor("out_T", (D, NP), F32, kind="ExternalOutput").ap()
    gnn_kernel(nc, dram, out)
    got = run(nc, [arrays], core_ids=[0]).results[0]["out_T"]
    return np.ascontiguousarray(got[:, :N].T)
```

```python
from contextlib import ExitStack, contextmanager

import concourse.bass as bass
from concourse import mybir

F32 = mybir.dt.float32
BF16 = mybir.dt.bfloat16
I32 = mybir.dt.int32
I16 = mybir.dt.int16
ALU = mybir.AluOpType
ACT = mybir.ActivationFunctionType
AX = mybir.AxisListType
RMAX = bass.bass_isa.ReduceOp.max
RADD = bass.bass_isa.ReduceOp.add

N, E, D, H = 3125, 50000, 128, 3
EA, SH, GEO, AH = 32, 16, 20, 8
WN = 42
NW = -(-N // WN)
NP = NW * WN
WH = WN * H
T = 6
S = 128 * T
BM, NB = 3 * WN, NW // 3
CE = 512
NC = 3 * -(-E // (3 * CE))
EP = NC * CE
EW = E + S + 256
NG = -(-E // S)
PAD = EW - EP
PADP = max(q for q in range(1, 129) if PAD % q == 0)
GQ = max(q for q in range(1, 7) if EW % q == 0)
NCOL, NCH = 450, 7
WC, NWC = 5, 15
CW = WC * WN
GK = GEO + 1
QUERY_PARTS = (0, 0, 1, 0, 2, 1)
GEO_PARTS = (0, 1, 0, 2, 0, 1)
PAIRS = len(GEO_PARTS)
KS = PAIRS * GK
AW = 12
MOST = 256
KEY0 = 8192
EPS = 1e-5
FAR = float(2.0 ** 100)
FLOOR = -float(2.0 ** 90)


class Steps:

    def __init__(self, sem, names, ahead=0):
        self.sem, self.per, self.ahead = sem, len(names), ahead
        self.at = {n: k + 1 for k, n in enumerate(names)}

    def of(self, turn, name):
        return (turn + self.ahead) * self.per + self.at[name]

    def prime(self, eng):
        eng.sem_inc(self.sem, self.ahead * self.per)


class Kit:

    def __init__(self, nc, dram, ctx):
        self.nc, self.dram, self.ctx = nc, dram, ctx
        self.old = []
        self.rows_in = [ctx.enter_context(nc.semaphore(f"rows_in{u}")) for u in range(5)]
        self.general_rows = [ctx.enter_context(nc.semaphore(f"general_rows{u}")) for u in range(8)]
        self.rows_base = [0] * 5
        self.ps = ctx.enter_context(nc.psum_tensor("ps", [128, 8, 512], F32))

    def keep(self, name, shape, dt=F32):
        return self.ctx.enter_context(self.nc.sbuf_tensor(name, shape, dt))

    @contextmanager
    def phase(self, name):
        nc = self.nc
        sems = ExitStack()
        used = []

        def sem(what):
            used.append(sems.enter_context(nc.semaphore(f"{name}_{what}")))
            return used[-1]

        with ExitStack() as bufs:
            def sb(what, shape, dt=F32):
                return bufs.enter_context(nc.sbuf_tensor(f"{name}_{what}", shape, dt))

            hop = {e: sem(f"hop_{e}") for e in ("pool", "act", "pe", "dve")}
            with nc.Block() as block:
                yield sb, sem, block, hop
        if self.old:
            self.old[-1].close()
        self.old = [used, sems]

    def clear_old(self, sp):
        for s in (self.old[0] if self.old else []):
            sp.sem_clear(s)


def bc(ap, shape):
    return ap.to_broadcast(shape)


def prepare(k):
    nc, d = k.nc, k.dram
    k.ident = k.keep("ident", [128, 128])
    k.far = k.keep("far", [128, 128], BF16)
    k.mean = k.keep("mean", [128, 128])
    k.ones = k.keep("ones", [128, 128])
    k.iota_wn = k.keep("iota_wn", [128, WN])
    k.eps = k.keep("eps", [128, 1])
    k.xT = k.keep("xT", [128, NP])
    k.starts = k.keep("starts", [1, NW], I32)
    k.fits = k.keep("fits", [1, 1], I32)
    PC = EP // 128
    with k.phase("prep") as (sb, sem, block, hop):
        dsts = sb("dsts", [128, PC], I32)
        nexts = sb("nexts", [128, PC], I32)
        dstf = sb("dstf", [128, PC])
        nextf = sb("nextf", [128, PC])
        fars = sb("fars", [128, PC], I32)
        farf = sb("farf", [128, PC])
        junk = sb("junk", [128, PC], BF16)
        cnt = sb("cnt", [128, NW + 3])
        row = sb("row", [1, NW + 3])
        gap = sb("gap", [1, NW])
        most = sb("most", [1, 1])
        is_sorted = sb("is_sorted", [1, 1])
        is_few = sb("is_few", [1, 1])
        zero = sb("zero", [128, PAD // PADP * D])
        pads_out = sem("pads_out")
        x_in, dst_in, made, pe_sums, dve = (sem(n) for n in ("x_in", "dst_in", "made", "pe_sums", "dve"))

        @block.sync
        def _(sp):
            sp.dma_start(dsts[:, :], d["dst"][0:EP].rearrange("(p c) -> p c", c=PC)).then_inc(dst_in, 16)
            sp.dma_start(nexts[:, :], d["dst"][1:EP + 1].rearrange("(p c) -> p c", c=PC)).then_inc(dst_in, 16)
            sp.dma_start(fars[:, :], d["dst"][MOST:EP + MOST].rearrange("(p c) -> p c", c=PC)).then_inc(dst_in, 16)
            sp.dma_start(k.xT[:, :], d["xT"]).then_inc(x_in, 16)
            sp.wait_ge(made, 1)
            sp.dma_start(d["am"][EP:EW].rearrange("(p j) -> p j", p=PADP), zero[0:PADP, 0:PAD // PADP]).then_inc(pads_out, 16)
            sp.dma_start(d["msg"][EP:EW, :].rearrange("(p j) f -> p (j f)", p=PADP), zero[0:PADP, :]).then_inc(pads_out, 16)
            sp.wait_ge(x_in, 16)
            sp.wait_ge(pads_out, 32)

        @block.gpsimd
        def _(pool):
            pool.memset(zero[:, :], 0.0).then_inc(made, 1)
            pool.memset(k.mean[:, :], 1.0 / D).then_inc(made, 1)
            pool.memset(k.ones[:, :], 1.0).then_inc(made, 1)
            pool.memset(k.eps[:, :], EPS).then_inc(made, 1)
            pool.iota(k.iota_wn[:, :], pattern=[[1, WN]], base=0, channel_multiplier=0,
                      allow_small_or_imprecise_dtypes=True).then_inc(made, 1)
            pool.wait_ge(made, 1)
            for m, fill in ((k.ident, 1.0), (k.far, FAR)):
                pool.affine_select(out=m[:, :], in_=zero[:, 0:128], compare_op=ALU.not_equal, fill=fill,
                                   base=0, pattern=[[-1, 128]], channel_multiplier=1).then_inc(made, 1)
            pool.wait_ge(made, 7)

        @block.vector
        def _(dve_):
            dve_.wait_ge(dst_in, 48)
            nc.vector.tensor_copy(dstf[:, :], dsts[:, :]).then_inc(dve, 1)
            nc.vector.tensor_copy(nextf[:, :], nexts[:, :]).then_inc(dve, 1)
            dve_.wait_ge(dve, 2)
            for w in range(NW + 1):
                if w:
                    dve_.wait_ge(dve, 2 + w)
                nc.vector.tensor_scalar(junk[:, :], dstf[:, :], float(min(w * WN, N)), 0.0, ALU.is_lt, ALU.add,
                                        accum_out=cnt[:, w:w + 1]).then_inc(dve, 1)
            dve_.wait_ge(dve, NW + 3)
            nc.vector.tensor_copy(farf[:, :], fars[:, :]).then_inc(dve, 1)
            dve_.wait_ge(dve, NW + 4)
            nc.vector.tensor_tensor(farf[:, :], farf[:, :], dstf[:, :], ALU.is_equal).then_inc(dve, 1)
            dve_.wait_ge(dve, NW + 5)
            nc.vector.scalar_tensor_tensor(farf[:, :], dstf[:, :], float(N), farf[:, :], ALU.is_lt, ALU.mult).then_inc(dve, 1)
            dve_.wait_ge(dve, NW + 6)
            nc.vector.reduce_sum(cnt[:, NW + 2:NW + 3], farf[:, :], AX.X).then_inc(dve, 1)
            nc.vector.tensor_tensor(dstf[:, :], dstf[:, :], nextf[:, :], ALU.is_gt).then_inc(dve, 1)
            dve_.wait_ge(dve, NW + 8)
            nc.vector.reduce_sum(cnt[:, NW + 1:NW + 2], dstf[:, :], AX.X).then_inc(dve, 1)
            dve_.wait_ge(pe_sums, 1)
            nc.vector.tensor_copy(row[:, :], k.ps[0:1, 0, 0:NW + 3]).then_inc(dve, 1)
            dve_.wait_ge(dve, NW + 10)
            nc.vector.tensor_copy(k.starts[:, :], row[:, 0:NW]).then_inc(dve, 1)
            nc.vector.tensor_sub(gap[:, :], row[:, 1:NW + 1], row[:, 0:NW]).then_inc(dve, 1)
            nc.vector.tensor_scalar(is_sorted[:, :], row[:, NW + 1:NW + 2], 0.0, None, ALU.is_le).then_inc(dve, 1)
            dve_.wait_ge(dve, NW + 13)
            nc.vector.reduce_max(most[:, :], gap[:, :], AX.X).then_inc(dve, 1)
            nc.vector.scalar_tensor_tensor(is_few[:, :], row[:, NW + 2:NW + 3], 0.0, is_sorted[:, :],
                                           ALU.is_le, ALU.mult).then_inc(dve, 1)
            dve_.wait_ge(dve, NW + 15)
            nc.vector.scalar_tensor_tensor(k.fits[:, :], most[:, :], float(S), is_few[:, :],
                                           ALU.is_le, ALU.mult).then_inc(dve, 1)
            dve_.wait_ge(dve, NW + 16)

        @block.tensor
        def _(pe):
            pe.wait_ge(made, 7)
            pe.wait_ge(dve, NW + 9)
            nc.tensor.matmul(k.ps[0:1, 0, 0:NW + 3], k.ones[:, 0:1], cnt[:, :], start=True, stop=True).then_inc(pe_sums, 1)


def layer_norm(k, name, src, out, parts=1, relu=False, gain=None, shift=None, add=False, inner_relu=False):
    nc = k.nc
    with k.phase(name) as (sb, sem, block, hop):
        xc = sb("xc", [128, 2, parts, NCOL])
        sq = sb("sq", [128, 2, parts, NCOL])
        std = sb("std", [128, 2, NCOL])
        rec = sb("rec", [128, 2, NCOL])
        y = sb("y", [128, 2, parts, NCOL])
        centred, squared, mean_ok, var_ok, std_ok, rec_ok, scaled, moved, stored = (
            sem(n) for n in ("centred", "squared", "mean_ok", "var_ok", "std_ok", "rec_ok", "scaled", "moved", "stored"))
        half = k.mean if parts == 1 else sb("half", [128, 128])
        half_ok = sem("half_ok")

        def cols(c):
            return slice(c * NCOL, (c + 1) * NCOL)

        @block.sync
        def _(sp):
            k.clear_old(sp)

        @block.gpsimd
        def _(pool):
            if parts > 1:
                pool.memset(half[:, :], 1.0 / (D * parts)).then_inc(half_ok, 1)

        @block.tensor
        def _(pe):
            def mean(c):
                if c >= 2:
                    pe.wait_ge(centred, c - 1)
                for p in range(parts):
                    m = nc.tensor.matmul(k.ps[:, c % 2, 0:NCOL], half[:, :], src[:, p, cols(c)],
                                         start=p == 0, stop=p == parts - 1)
                m.then_inc(mean_ok, 1)

            if parts > 1:
                pe.wait_ge(half_ok, 1)
            mean(0)
            for c in range(NCH):
                if c + 1 < NCH:
                    mean(c + 1)
                pe.wait_ge(squared, c + 1)
                if c >= 2:
                    pe.wait_ge(std_ok, c - 1)
                for p in range(parts):
                    m = nc.tensor.matmul(k.ps[:, 2 + c % 2, 0:NCOL], half[:, :], sq[:, c % 2, p, :],
                                         start=p == 0, stop=p == parts - 1)
                m.then_inc(var_ok, 1)

        @block.scalar
        def _(act):
            for c in range(NCH):
                act.wait_ge(var_ok, c + 1)
                if c >= 2:
                    act.wait_ge(rec_ok, c - 1)
                nc.scalar.activation(std[:, c % 2, :], k.ps[:, 2 + c % 2, 0:NCOL], ACT.Sqrt,
                                     bias=k.eps[:, 0:1]).then_inc(std_ok, 1)

        @block.vector
        def _(dve):
            def centre(c):
                dve.wait_ge(mean_ok, c + 1)
                if c >= 2:
                    dve.wait_ge(stored, c - 1)
                    dve.wait_ge(var_ok, c - 1)
                nc.vector.tensor_tensor(xc[:, c % 2, :, :], src[:, :, cols(c)],
                                        bc(k.ps[:, c % 2, 0:NCOL].unsqueeze(1), [128, parts, NCOL]),
                                        ALU.subtract).then_inc(centred, 1)
                dve.wait_ge(centred, c + 1)
                nc.vector.tensor_tensor(sq[:, c % 2, :, :], xc[:, c % 2, :, :], xc[:, c % 2, :, :],
                                        ALU.mult).then_inc(squared, 1)

            def finish(c):
                b = c % 2
                dve.wait_ge(std_ok, c + 1)
                nc.vector.reciprocal(rec[:, b, :], std[:, b, :]).then_inc(rec_ok, 1)
                dve.wait_ge(rec_ok, c + 1)
                recs = bc(rec[:, b, :].unsqueeze(1), [128, parts, NCOL])
                last = not (gain is not None or add)
                to = out[:, :, cols(c)] if last else y[:, b, :, :]
                if relu:
                    nc.vector.scalar_tensor_tensor(to, xc[:, b, :, :], 0.0, recs, ALU.max,
                                                   ALU.mult).then_inc(stored if last else scaled, 1)
                else:
                    nc.vector.tensor_tensor(to, xc[:, b, :, :], recs, ALU.mult).then_inc(stored if last else scaled, 1)
                if last:
                    return
                dve.wait_ge(scaled, c + 1)
                if gain is not None:
                    for p in range(parts):
                        to = y[:, b, p, :] if add else out[:, p, cols(c)]
                        nc.vector.tensor_scalar(to, y[:, b, p, :], gain[:, p:p + 1], shift[:, p:p + 1], ALU.mult,
                                                ALU.add).then_inc(moved if add or p < parts - 1 else stored, 1)
                    if not add:
                        return
                    dve.wait_ge(moved, parts * (c + 1))
                nc.vector.tensor_tensor(out[:, :, cols(c)], out[:, :, cols(c)], y[:, b, :, :],
                                        ALU.add).then_inc(stored, 1)

            for c in range(NCH + 1):
                if c < NCH:
                    centre(c)
                if c:
                    finish(c - 1)
            dve.wait_ge(stored, NCH)


def node_rows(k, name, srcT, weights, width, stores):
    nc = k.nc
    with k.phase(name) as (sb, sem, block, hop):
        rows = sb("rows", [BM, 4, width])
        w = None
        if weights is not None:
            w, w_in, w_zero = sb("w", [128, width]), sem("w_in"), sem("w_zero")
        made, copied = sem("made"), sem("copied")
        out = [sem(f"out{n}") for n in range(4)]
        ns = len(stores)

        @block.sync
        def _(sp):
            k.clear_old(sp)
            if w is not None:
                sp.wait_ge(w_zero, 1)
                for at, rows_, src in weights:
                    sp.dma_start(w[0:rows_, at:at + src.shape[1]], src).then_inc(w_in, 16)
            for b in range(NB):
                sp.wait_ge(copied, b + 1)
                for dst, at, n in stores:
                    sp.dma_start(dst[b * BM:(b + 1) * BM, :], rows[:, b % 4, at:at + n]).then_inc(out[b % 4], 16)
            for q in range(4):
                sp.wait_ge(out[q], 16 * ns * len(range(q, NB, 4)))

        @block.gpsimd
        def _(pool):
            if w is not None:
                pool.memset(w[:, :], 0.0).then_inc(w_zero, 1)

        @block.tensor
        def _(pe):
            if w is not None:
                pe.wait_ge(w_in, 16 * len(weights))
            for b in range(NB):
                if b >= 4:
                    pe.wait_ge(copied, b - 3)
                block_ = srcT[:, b * BM:(b + 1) * BM]
                if w is None:
                    m = nc.tensor.transpose(k.ps[0:BM, b % 4, 0:width], block_, k.ident[:, :])
                else:
                    m = nc.tensor.matmul(k.ps[0:BM, b % 4, 0:width], block_, w[:, :], start=True, stop=True)
                m.then_inc(made, 1)

        @block.scalar
        def _(act):
            for b in range(NB):
                act.wait_ge(made, b + 1)
                if b >= 4:
                    act.wait_ge(out[b % 4], 16 * ns * (b // 4))
                nc.scalar.activation(rows[:, b % 4, :], k.ps[0:BM, b % 4, 0:width], ACT.Copy).then_inc(copied, 1)


def edge_messages(k, a_all):
    nc, d = k.nc, k.dram
    U = 3
    with k.phase("em") as (sb, sem, block, hop):
        feat = sb("feat", [128, U, CE])
        fc1, aw1e, wsh = (sb(n, [128, D]) for n in ("fc1", "aw1e", "wsh"))
        fc2, fc3, aw2 = sb("fc2", [D, D]), sb("fc3", [D, D]), sb("aw2", [D, D])
        aw3 = sb("aw3", [D, AH])
        bias = sb("bias", [128, 4])
        b3 = sb("b3", [128, D])
        ab3 = sb("ab3", [128, AH])
        idx = sb("idx", [128, U, 8], I32)
        gs = sb("gs", [128, U, 4, 2 * D])
        gd = sb("gd", [128, U, 4, D])
        ga = sb("ga", [128, U, 4, D])
        h1, h2, a1, a2 = (sb(n, [128, U, CE]) for n in ("h1", "h2", "a1", "a2"))
        t1, t2, t3, msg = (sb(n, [128, U, 4, D]) for n in ("t1", "t2", "t3", "msg"))
        w_in, zeroed = sem("w_in"), sem("zeroed")
        idx_in, feat_in, msg_out = ([sem(f"{n}{u}") for u in range(U)] for n in ("idx_in", "feat_in", "msg_out"))
        rows_in, rows_base = k.rows_in, list(k.rows_base)
        early = Steps(sem("early"), ["FC1", "A1", "FC2", "A2"], U)
        late = Steps(sem("late"), ["SCALE", "SH", "A3"], U)
        act_ = Steps(sem("act"), ["H1", "A1", "H2", "A2"], U)
        act_msg = Steps(sem("act_msg"), ["MSG"], U)
        gathered = Steps(sem("gathered"), ["GA"], U)
        dve_ = Steps(sem("dve"), ["A3", "TB", "TG", "TS"], U)
        FC1, A1, FC2, A2, SCALE, SHB, A3 = range(7)
        loads = [(fc1[0:EA, :], d["fc1"]), (aw1e[0:EA, :], d["aW1"][D:D + EA, :]), (fc2[:, :], d["fc2"]), (fc3[:, :], d["fc3"]),
                 (aw2[:, :], d["aW2"]), (wsh[EA:EA + SH, :], d["W_sh"]), (aw3[:, :], d["aW3"]), (bias[:, :], d["em_bias"]),
                 (b3[:, :], d["b3"].partition_broadcast(128)), (ab3[:, :], d["ab3"].partition_broadcast(128))]
        edges = d["sd"][0:EP, :].rearrange("(c p j) s -> c p (j s)", p=128, j=4)
        msgs = d["msg"][0:EP, :].rearrange("(c p j) f -> c p (j f)", p=128, j=4)

        @block.sync
        def _(sp):
            def load(c, u):
                sp.dma_start(idx[:, u, :], edges[bass.ds(c, 1), :, :].rearrange("c p q -> (c p) q")).then_inc(idx_in[u], 16)
                sp.wait_ge(late.sem, late.of(c - U, "SH"))
                sp.dma_start(feat[0:EA, u, :], d["ea32"][bass.ds(c, 1), :, :].rearrange("c p q -> (c p) q")).then_inc(feat_in[u], 16)
                sp.dma_start(feat[EA:EA + SH, u, :], d["sh16"][bass.ds(c, 1), :, :].rearrange("c p q -> (c p) q")).then_inc(feat_in[u], 16)

            def store(c, u):
                sp.wait_ge(act_msg.sem, act_msg.of(c, "MSG"))
                sp.dma_start(msgs[bass.ds(c, 1), :, :].rearrange("c p q -> (c p) q"),
                             msg[:, u, :, :].rearrange("p j f -> p (j f)")).then_inc(msg_out[u], 16)

            k.clear_old(sp)
            sp.wait_ge(zeroed, 4)
            for to, src in loads:
                sp.dma_start(to, src).then_inc(w_in, 16)
            for u in range(U):
                load(u, u)
                sp.sem_inc(msg_out[u], 16)
            with sp.Fori(0, NC // U - 1) as i:
                for u in range(U):
                    c = U * i + u
                    sp.wait_ge(gathered.sem, gathered.of(c, "GA"))
                    load(c + U, u)
                    store(c, u)
            for u in range(U):
                store(NC - U + u, u)
            for u in range(U):
                sp.wait_ge(msg_out[u], 16 * (NC // U + 1))

        @block.gpsimd
        def _(pool):
            for m in (fc1[:, :], aw1e[:, :], wsh[:, :], feat[:, :, :]):
                pool.memset(m, 0.0).then_inc(zeroed, 1)
            with pool.Fori(0, NC // U) as i:
                for u in range(U):
                    c = U * i + u
                    pool.wait_ge(dve_.sem, dve_.of(c - U, "TG"))
                    pool.sem_inc(hop["pool"], 1)
                    pool.wait_ge(idx_in[u], (i + 1) * 16)
                    pool.sem_inc(hop["pool"], 1)
                    for j in range(4):
                        pool.indirect_dma_start(out=gs[:, u, j, :], out_offset=None, in_=d["rows0"],
                                                in_offset=bass.IndirectOffsetOnAxis(ap=idx[:, u, 2 * j:2 * j + 1], axis=0)
                                                ).then_inc(rows_in[u], 16)
                        pool.indirect_dma_start(out=gd[:, u, j, :], out_offset=None, in_=d["rows0d"],
                                                in_offset=bass.IndirectOffsetOnAxis(ap=idx[:, u, 2 * j + 1:2 * j + 2], axis=0)
                                                ).then_inc(rows_in[u], 16)

        @block.tensor
        def _(pe):
            def begin(c, u, i):
                pe.wait_ge(feat_in[u], (i + 1) * 32)
                pe.wait_ge(act_.sem, act_.of(c - 1, "H1"))
                nc.tensor.matmul(k.ps[:, FC1, :], fc1[:, :], feat[:, u, :], start=True, stop=True).then_inc(early.sem, 1)
                pe.wait_ge(act_.sem, act_.of(c - 1, "A1"))
                nc.tensor.matmul(k.ps[:, A1, :], aw1e[:, :], feat[:, u, :], start=True, stop=False)
                pe.wait_ge(gathered.sem, gathered.of(c, "GA"))
                for j in range(4):
                    m = nc.tensor.matmul(k.ps[:, A1, j * 128:(j + 1) * 128], ga[:, u, j, :], k.ident[:, :],
                                         start=False, stop=j == 3)
                m.then_inc(early.sem, 1)

            def finish(c, u):
                pe.wait_ge(act_.sem, act_.of(c, "H2"))
                pe.wait_ge(dve_.sem, dve_.of(c - 1, "TB"))
                for j in range(4):
                    m = nc.tensor.matmul(k.ps[:, SCALE, j * 128:(j + 1) * 128], h2[:, u, j * 128:(j + 1) * 128], fc3[:, :],
                                         start=True, stop=True)
                m.then_inc(late.sem, 1)
                pe.wait_ge(dve_.sem, dve_.of(c - 1, "TS"))
                for j in range(4):
                    m = nc.tensor.matmul(k.ps[:, SHB, j * 128:(j + 1) * 128], feat[:, u, j * 128:(j + 1) * 128], wsh[:, :],
                                         start=True, stop=True)
                m.then_inc(late.sem, 1)
                pe.wait_ge(act_.sem, act_.of(c, "A2"))
                for j in range(4):
                    m = nc.tensor.matmul(k.ps[:, A3, j * AH:(j + 1) * AH], a2[:, u, j * 128:(j + 1) * 128], aw3[:, :],
                                         start=True, stop=True)
                m.then_inc(late.sem, 1)

            def middle(c, u):
                pe.wait_ge(act_.sem, act_.of(c, "H1"))
                nc.tensor.matmul(k.ps[:, FC2, :], fc2[:, :], h1[:, u, :], start=True, stop=True).then_inc(early.sem, 1)
                pe.wait_ge(act_.sem, act_.of(c, "A1"))
                nc.tensor.matmul(k.ps[:, A2, :], aw2[:, :], a1[:, u, :], start=True, stop=True).then_inc(early.sem, 1)

            def turn(c, u, i):
                begin(c, u, i)
                finish(c - 1, (u - 1) % U)
                middle(c, u)

            early.prime(pe)
            late.prime(pe)
            pe.wait_ge(w_in, 16 * len(loads))
            begin(0, 0, 0)
            middle(0, 0)
            with pe.Fori(0, NC // U - 1) as i:
                for u in range(1, U):
                    turn(U * i + u, u, i)
                turn(U * i + U, 0, i + 1)
            for u in range(1, U):
                turn(NC - U + u, u, NC // U - 1)
            finish(NC - 1, U - 1)

        @block.scalar
        def _(act):
            def layers(c, u):
                for what, bank, to, col in (("FC1", FC1, h1, 0), ("A1", A1, a1, 2), ("FC2", FC2, h2, 1), ("A2", A2, a2, 3)):
                    act.wait_ge(early.sem, early.of(c, what))
                    nc.scalar.activation(to[:, u, :], k.ps[:, bank, :], ACT.Silu, bias=bias[:, col:col + 1]).then_inc(act_.sem, 1)

            def message(c, u, i):
                act.wait_ge(dve_.sem, dve_.of(c, "TS"))
                act.sem_inc(hop["act"], 1)
                act.wait_ge(msg_out[u], (i + 1) * 16)
                nc.scalar.activation(msg[:, u, :, :], t3[:, u, :, :], ACT.Silu).then_inc(act_msg.sem, 1)

            def turn(c, u, i):
                layers(c, u)
                message(c - 1, (u - 1) % U, i if u else i - 1)

            act_.prime(act)
            act_msg.prime(act)
            act.wait_ge(w_in, 16 * len(loads))
            layers(0, 0)
            with act.Fori(0, NC // U - 1) as i:
                for u in range(1, U):
                    turn(U * i + u, u, i)
                turn(U * i + U, 0, i + 1)
            for u in range(1, U):
                turn(NC - U + u, u, NC // U - 1)
            message(NC - 1, U - 1, NC // U - 1)

        @block.vector
        def _(dve):
            def ends(c, u, i):
                dve.wait_ge(rows_in[u], (i + 1) * 128 + rows_base[u])
                dve.wait_ge(early.sem, early.of(c - U, "A1"))
                nc.vector.tensor_tensor(ga[:, u, :, :], gs[:, u, :, D:2 * D], gd[:, u, :, :], ALU.add).then_inc(gathered.sem, 1)

            def finish(c, u):
                s = dve_.sem
                dve.wait_ge(late.sem, late.of(c, "A3"))
                nc.vector.tensor_tensor(a_all[:, bass.ds(c, 1), :, :].rearrange("p c j h -> p (c j) h"),
                                        k.ps[:, A3, 0:4 * AH].rearrange("p (j h) -> p j h", h=AH),
                                        bc(ab3[:, :].unsqueeze(1), [128, 4, AH]), ALU.add).then_inc(s, 1)
                nc.vector.tensor_tensor(t1[:, u, :, :], k.ps[:, SCALE, :].rearrange("p (j f) -> p j f", f=D),
                                        bc(b3[:, :].unsqueeze(1), [128, 4, D]), ALU.add).then_inc(s, 1)
                dve.wait_ge(s, dve_.of(c, "TB"))
                nc.vector.tensor_tensor(t2[:, u, :, :], t1[:, u, :, :], gs[:, u, :, 0:D], ALU.mult).then_inc(s, 1)
                dve.wait_ge(s, dve_.of(c, "TG"))
                dve.wait_ge(act_msg.sem, act_msg.of(c - U, "MSG"))
                nc.vector.tensor_tensor(t3[:, u, :, :], t2[:, u, :, :], k.ps[:, SHB, :].rearrange("p (j f) -> p j f", f=D),
                                        ALU.add).then_inc(s, 1)

            def turn(c, u, i):
                ends(c, u, i)
                finish(c - 1, (u - 1) % U)

            gathered.prime(dve)
            dve_.prime(dve)
            dve.wait_ge(w_in, 16 * len(loads))
            ends(0, 0, 0)
            with dve.Fori(0, NC // U - 1) as i:
                for u in range(1, U):
                    turn(U * i + u, u, i)
                turn(U * i + U, 0, i + 1)
            for u in range(1, U):
                turn(NC - U + u, u, NC // U - 1)
            finish(NC - 1, U - 1)
        for u in range(U):
            k.rows_base[u] += NC // U * 128


def edge_softmax(k, a_all):
    nc, d = k.nc, k.dram
    ns = NC * 4
    with k.phase("es") as (sb, sem, block, hop):
        part, most, total, inv = (sb(n, [128, AH]) for n in ("part", "most", "total", "inv"))
        part2 = sb("part2", [128, AH])
        am = sb("am", [128, ns])
        masked, dve, pooled, exped, out = (sem(n) for n in ("masked", "dve", "pooled", "exped", "out"))
        flat = a_all[:, :, :, :].rearrange("p c j h -> p (c j) h")
        by_head = a_all[:, :, :, :].rearrange("p c j h -> p h (c j)")
        last = a_all[:, NC - 3:NC, :, :].rearrange("p c j h -> p c (j h)")
        whole = bc

        @block.sync
        def _(sp):
            k.clear_old(sp)
            sp.wait_ge(dve, 7)
            sp.dma_start(d["am"][0:EP].rearrange("(c p j) -> p c j", p=128, j=4),
                         am[:, :].rearrange("p (c j) -> p c j", j=4)).then_inc(out, 16)
            sp.wait_ge(out, 16)

        @block.gpsimd
        def _(pool):
            pool.affine_select(out=last, in_=last, compare_op=ALU.is_ge, fill=-1e30,
                               base=(E - (NC - 3) * CE) // 4 - 1, pattern=[[-CE // 4, 3], [0, 4 * AH]], channel_multiplier=-1).then_inc(masked, 1)
            pool.wait_ge(dve, 1)
            pool.partition_all_reduce(most[:, :], part[:, :], 128, RMAX).then_inc(pooled, 1)
            pool.wait_ge(dve, 3)
            pool.partition_all_reduce(total[:, :], part2[:, :], 128, RADD).then_inc(pooled, 1)

        @block.scalar
        def _(act):
            act.wait_ge(dve, 2)
            nc.scalar.activation(flat, flat, ACT.Exp).then_inc(exped, 1)

        @block.vector
        def _(v):
            v.wait_ge(masked, 1)
            nc.vector.tensor_reduce(part[:, :], by_head, AX.X, ALU.max).then_inc(dve, 1)
            v.wait_ge(pooled, 1)
            nc.vector.tensor_tensor(flat, flat, whole(most[:, :].unsqueeze(1), [128, ns, AH]), ALU.subtract).then_inc(dve, 1)
            v.wait_ge(exped, 1)
            nc.vector.tensor_reduce(part2[:, :], by_head, AX.X, ALU.add).then_inc(dve, 1)
            v.wait_ge(pooled, 2)
            nc.vector.reciprocal(inv[:, :], total[:, :]).then_inc(dve, 1)
            v.wait_ge(dve, 4)
            nc.vector.tensor_scalar(part[:, :], inv[:, :], 1.0 / AH, None, ALU.mult).then_inc(dve, 1)
            v.wait_ge(dve, 5)
            nc.vector.tensor_tensor(flat, flat, whole(part[:, :].unsqueeze(1), [128, ns, AH]), ALU.mult).then_inc(dve, 1)
            v.wait_ge(dve, 6)
            nc.vector.tensor_reduce(am[:, :], flat, AX.X, ALU.add).then_inc(dve, 1)


def window_sums(k, aggT):
    nc, d = k.nc, k.dram
    U = 3
    with k.phase("ws") as (sb, sem, block, hop):
        sd = sb("sd", [128, U, 2 * T], I32)
        am = sb("am", [128, U, T])
        msg = sb("msg", [128, U, T * D])
        base = sb("base", [128, 1])
        srcf, dl, blk, res, ok1, ok, key0, key = (sb(n, [128, U, T]) for n in
                                                  ("srcf", "dl", "blk", "res", "ok1", "ok", "key0", "key"))
        sel = sb("sel", [128, U, T, WN])
        wsel = sb("wsel", [128, U, T, WN])
        ge = sb("ge", [128, U, T, NB - 1])
        oh_res = sb("oh_res", [128, U, T, BM], BF16)
        oh_key = sb("oh_key", [128, U, T, NB * WN], BF16)
        bounds = sb("bounds", [128, NB - 1])
        iota_bm = sb("iota_bm", [128, BM])
        iota_key = sb("iota_key", [128, NB * WN], I16)
        adj = sb("adj", [BM, U, NB * WN], BF16)
        deg = sb("deg", [1, NP])
        made = sem("made")
        in_ = [sem(f"in{u}") for u in range(U)]
        adj_out = [sem(f"adj_out{u}") for u in range(U)]
        deg_out = sem("deg_out")
        dve_ = Steps(sem("dve"), ["SRC", "DL", "GE", "SEL", "OK1", "BLK", "WSEL", "OK", "RES", "KEY0", "KEY", "OH_RES"]
                     + [f"OH_KEY{j}" for j in range(T)] + ["BASE"], U)
        pe_ = Steps(sem("pe"), ["AGG", "DEG", "ADJ"], U)
        act_ = Steps(sem("act"), ["AGG", "DEG", "ADJ"], U)

        @block.sync
        def _(sp):
            k.clear_old(sp)
            with sp.If(sp.value_load(k.fits[0:1, 0:1], min_val=0, max_val=1) == 1):
                with sp.Fori(0, NW // U) as i:
                    for u in range(U):
                        w = U * i + u
                        at = sp.value_load(k.starts[0:1, bass.ds(w, 1)], min_val=0, max_val=E)
                        sp.wait_ge(pe_.sem, pe_.of(w - U, "ADJ"))
                        sp.dma_start(sd[:, u, :], d["sd"][bass.ds(at, S), :].rearrange("(p j) s -> p (j s)", j=T)).then_inc(in_[u], 16)
                        sp.dma_start(am[:, u, :], d["am"][bass.ds(at, S)].rearrange("(p j) -> p j", j=T)).then_inc(in_[u], 16)
                        sp.dma_start(msg[:, u, :], d["msg"][bass.ds(at, S), :].rearrange("(p j) f -> p (j f)", j=T)).then_inc(in_[u], 16)

        @block.gpsimd
        def _(pool):
            pool.iota(bounds[:, :], pattern=[[BM, NB - 1]], base=BM, channel_multiplier=0,
                      allow_small_or_imprecise_dtypes=True).then_inc(made, 1)
            pool.iota(iota_bm[:, :], pattern=[[1, BM]], base=0, channel_multiplier=0,
                      allow_small_or_imprecise_dtypes=True).then_inc(made, 1)
            pool.iota(iota_key[:, :], pattern=[[1, NB * WN]], base=-KEY0, channel_multiplier=0,
                      allow_small_or_imprecise_dtypes=True).then_inc(made, 1)
            pool.memset(base[:, :], 0.0).then_inc(made, 1)

        @block.vector
        def _(dve):
            with dve.If(dve.value_load(k.fits[0:1, 0:1], min_val=0, max_val=1) == 1):
                dve_.prime(dve)
                dve.wait_ge(made, 4)
                s = dve_.sem
                with dve.Fori(0, NW // U) as i:
                    for u in range(U):
                        w = U * i + u
                        sdv = sd[:, u, :].rearrange("p (j s) -> p s j", s=2)
                        dve.wait_ge(in_[u], (i + 1) * 48)
                        nc.vector.tensor_copy(srcf[:, u, :], sdv[:, 0, :]).then_inc(s, 1)
                        dve.wait_ge(s, dve_.of(w - 1, "BASE"))
                        nc.vector.tensor_scalar(dl[:, u, :], sdv[:, 1, :], base[:, 0:1], None, ALU.subtract).then_inc(s, 1)
                        dve.wait_ge(s, dve_.of(w, "SRC"))
                        nc.vector.tensor_tensor(ge[:, u, :, :], bc(srcf[:, u, :].unsqueeze(2), [128, T, NB - 1]),
                                                bc(bounds[:, :].unsqueeze(1), [128, T, NB - 1]), ALU.is_ge).then_inc(s, 1)
                        dve.wait_ge(s, dve_.of(w, "DL"))
                        dve.wait_ge(pe_.sem, pe_.of(w - U, "ADJ"))
                        nc.vector.tensor_tensor(sel[:, u, :, :], bc(k.iota_wn[:, :].unsqueeze(1), [128, T, WN]),
                                                bc(dl[:, u, :].unsqueeze(2), [128, T, WN]), ALU.is_equal).then_inc(s, 1)
                        nc.vector.tensor_scalar(ok1[:, u, :], dl[:, u, :], 0.0, None, ALU.is_ge).then_inc(s, 1)
                        dve.wait_ge(s, dve_.of(w, "GE"))
                        nc.vector.tensor_reduce(blk[:, u, :], ge[:, u, :, :], AX.X, ALU.add).then_inc(s, 1)
                        dve.wait_ge(s, dve_.of(w, "SEL"))
                        nc.vector.tensor_tensor(wsel[:, u, :, :], sel[:, u, :, :], bc(am[:, u, :].unsqueeze(2), [128, T, WN]),
                                                ALU.mult).then_inc(s, 1)
                        dve.wait_ge(s, dve_.of(w, "OK1"))
                        nc.vector.scalar_tensor_tensor(ok[:, u, :], dl[:, u, :], float(WN - 1), ok1[:, u, :], ALU.is_le,
                                                       ALU.mult).then_inc(s, 1)
                        dve.wait_ge(s, dve_.of(w, "BLK"))
                        nc.vector.scalar_tensor_tensor(res[:, u, :], blk[:, u, :], -float(BM), srcf[:, u, :], ALU.mult,
                                                       ALU.add).then_inc(s, 1)
                        nc.vector.scalar_tensor_tensor(key0[:, u, :], blk[:, u, :], float(WN), dl[:, u, :], ALU.mult,
                                                       ALU.add).then_inc(s, 1)
                        dve.wait_ge(s, dve_.of(w, "KEY0"))
                        nc.vector.scalar_tensor_tensor(key[:, u, :], ok[:, u, :], -float(KEY0), key0[:, u, :], ALU.mult,
                                                       ALU.add).then_inc(s, 1)
                        nc.vector.tensor_tensor(oh_res[:, u, :, :], bc(iota_bm[:, :].unsqueeze(1), [128, T, BM]),
                                                bc(res[:, u, :].unsqueeze(2), [128, T, BM]), ALU.is_equal).then_inc(s, 1)
                        dve.wait_ge(s, dve_.of(w, "KEY"))
                        for j in range(T):
                            nc.vector.tensor_scalar(oh_key[:, u, j, :], iota_key[:, :], key[:, u, j:j + 1], None,
                                                    ALU.is_equal).then_inc(s, 1)
                        nc.vector.tensor_scalar(base[:, :], base[:, :], float(WN), None, ALU.add).then_inc(s, 1)

        @block.tensor
        def _(pe):
            with pe.If(pe.value_load(k.fits[0:1, 0:1], min_val=0, max_val=1) == 1):
                pe_.prime(pe)
                with pe.Fori(0, NW // U) as i:
                    for u in range(U):
                        w = U * i + u
                        pe.wait_ge(in_[u], (i + 1) * 48)
                        pe.wait_ge(dve_.sem, dve_.of(w, "WSEL"))
                        pe.wait_ge(act_.sem, act_.of(w - 1, "DEG"))
                        for j in range(T):
                            m = nc.tensor.matmul(k.ps[:, 0, 0:WN], msg[:, u, j * D:(j + 1) * D], wsel[:, u, j, :],
                                                 start=j == 0, stop=j == T - 1)
                        m.then_inc(pe_.sem, 1)
                        for j in range(T):
                            m = nc.tensor.matmul(k.ps[0:1, 1, 0:WN], k.ones[:, 0:1], sel[:, u, j, :],
                                                 start=j == 0, stop=j == T - 1)
                        m.then_inc(pe_.sem, 1)
                        b = 2 + 3 * (u % 2)
                        pe.wait_ge(act_.sem, act_.of(w - (1 if u == 0 else 2), "ADJ"))
                        for j in range(T):
                            pe.wait_ge(dve_.sem, dve_.of(w, f"OH_KEY{j}"))
                            for q in range(3):
                                m = nc.tensor.matmul(k.ps[0:BM, b + q, 0:NB * WN // 3], oh_res[:, u, j, :],
                                                     oh_key[:, u, j, q * (NB * WN // 3):(q + 1) * (NB * WN // 3)],
                                                     start=j == 0, stop=j == T - 1)
                        m.then_inc(pe_.sem, 1)

        @block.scalar
        def _(act):
            with act.If(act.value_load(k.fits[0:1, 0:1], min_val=0, max_val=1) == 1):
                act_.prime(act)
                for u in range(U):
                    act.sem_inc(adj_out[u], 16)
                with act.Fori(0, NW // U) as i:
                    for u in range(U):
                        w = U * i + u
                        b = 2 + 3 * (u % 2)
                        act.wait_ge(pe_.sem, pe_.of(w, "AGG"))
                        act.sem_inc(hop["act"], 1)
                        nc.scalar.activation(aggT[:, bass.ds(w * WN, WN)], k.ps[:, 0, 0:WN], ACT.Copy).then_inc(act_.sem, 1)
                        act.wait_ge(pe_.sem, pe_.of(w, "DEG"))
                        act.sem_inc(hop["act"], 1)
                        nc.scalar.activation(deg[:, bass.ds(w * WN, WN)], k.ps[0:1, 1, 0:WN], ACT.Copy).then_inc(act_.sem, 1)
                        act.wait_ge(pe_.sem, pe_.of(w, "ADJ"))
                        act.sem_inc(hop["act"], 1)
                        act.wait_ge(adj_out[u], (i + 1) * 16)
                        nc.scalar.activation(adj[:, u, :].rearrange("p (q c) -> p q c", q=3), k.ps[0:BM, b:b + 3, 0:NB * WN // 3],
                                             ACT.Copy).then_inc(act_.sem, 1)
                        act.wait_ge(act_.sem, act_.of(w, "ADJ"))
                        act.sem_inc(hop["act"], 1)
                        act.dma_start(d["adj"][bass.ds(w, 1), :, :].rearrange("w p c -> (w p) c"), adj[:, u, :]).then_inc(adj_out[u], 16)
                act.dma_start(d["deg"].unsqueeze(0), deg[:, :]).then_inc(deg_out, 16)
                act.wait_ge(deg_out, 16)
                for u in range(U):
                    act.wait_ge(adj_out[u], 16 * (NW // U + 1))


def dense(k, name, outT, terms, bias=None, relu=False, add=None, parts=1):
    nc = k.nc
    with k.phase(name) as (sb, sem, block, hop):
        loads = []
        prog = []
        for p, ts in enumerate(terms):
            row = []
            for n, (src, feat) in enumerate(ts):
                w = sb(f"w{p}_{n}", [128, D])
                loads.append((w[:, :], src))
                row.append((w, feat))
            prog.append(row)
        bt = None
        if bias is not None:
            bt = sb("bt", [128, parts])
            loads.append((bt[:, :], bias))
        w_in, summed, moved, stored = (sem(n) for n in ("w_in", "summed", "moved", "stored"))
        tmp = sb("tmp", [128, 2, NCOL])

        @block.sync
        def _(sp):
            k.clear_old(sp)
            for to, src in loads:
                sp.dma_start(to, src).then_inc(w_in, 16)

        @block.tensor
        def _(pe):
            pe.wait_ge(w_in, 16 * len(loads))
            for n in range(NCH * parts):
                c, p = divmod(n, parts)
                if n >= 4:
                    pe.wait_ge(stored, n - 3)
                for q, (w, feat) in enumerate(prog[p]):
                    m = nc.tensor.matmul(k.ps[:, n % 4, 0:NCOL], w[:, :], feat[:, c * NCOL:(c + 1) * NCOL],
                                         start=q == 0, stop=q == len(prog[p]) - 1)
                m.then_inc(summed, 1)

        @block.vector
        def _(dve):
            dve.wait_ge(w_in, 16 * len(loads))
            for n in range(NCH * parts):
                c, p = divmod(n, parts)
                cols = slice(c * NCOL, (c + 1) * NCOL)
                dve.wait_ge(summed, n + 1)
                src = k.ps[:, n % 4, 0:NCOL]
                if bt is None:
                    if add is None:
                        nc.vector.tensor_copy(outT[:, p, cols], src).then_inc(stored, 1)
                    else:
                        nc.vector.tensor_tensor(outT[:, p, cols], add[:, cols], src, ALU.add).then_inc(stored, 1)
                elif add is not None:
                    nc.vector.scalar_tensor_tensor(outT[:, p, cols], src, bt[:, p:p + 1], add[:, cols], ALU.add,
                                                   ALU.add).then_inc(stored, 1)
                elif relu:
                    nc.vector.tensor_scalar(outT[:, p, cols], src, bt[:, p:p + 1], 0.0, ALU.add, ALU.max).then_inc(stored, 1)
                else:
                    nc.vector.tensor_scalar(outT[:, p, cols], src, bt[:, p:p + 1], None, ALU.add).then_inc(stored, 1)
            dve.wait_ge(stored, NCH * parts)


def geometry_parts(k):
    nc, d = k.nc, k.dram
    rows, size, pieces = GK * GQ, EW // GQ, 4
    step = size // pieces
    with k.phase("gp") as (sb, sem, block, hop):
        geo = sb("geo", [rows, size])
        rest = sb("rest", [rows, size])
        part = [sb(f"part{t}", [rows, size], BF16) for t in range(3)]
        geo_in, hi_ok, rest_ok, mid_ok, lo_ok, out = (sem(n) for n in ("geo_in", "hi_ok", "rest_ok", "mid_ok", "lo_ok", "out"))
        done = (hi_ok, mid_ok, lo_ok)

        def view(ap):
            return ap.rearrange("f (q c) -> (f q) c", q=GQ)

        def piece(n):
            return slice(n * step, (n + 1) * step)

        @block.sync
        def _(sp):
            k.clear_old(sp)
            for n in range(pieces):
                sp.dma_start(geo[:, piece(n)], view(d["geoT"])[:, piece(n)]).then_inc(geo_in, 16)
            for n in range(pieces):
                for i, t in enumerate(GEO_PARTS):
                    sp.wait_ge(done[t], n + 1)
                    sp.dma_start(view(d["geoS"][i * GK:(i + 1) * GK, :])[:, piece(n)], part[t][:, piece(n)]).then_inc(out, 16)
            sp.wait_ge(out, 16 * pieces * PAIRS)

        @block.scalar
        def _(act):
            for n in range(pieces):
                act.wait_ge(geo_in, 16 * pieces)
                nc.scalar.activation(part[0][:, piece(n)], geo[:, piece(n)], ACT.Copy).then_inc(hi_ok, 1)
                act.wait_ge(rest_ok, n + 1)
                nc.scalar.activation(part[1][:, piece(n)], rest[:, piece(n)], ACT.Copy).then_inc(mid_ok, 1)

        @block.vector
        def _(dve):
            for n in range(pieces):
                dve.wait_ge(hi_ok, n + 1)
                nc.vector.tensor_tensor(rest[:, piece(n)], geo[:, piece(n)], part[0][:, piece(n)], ALU.subtract).then_inc(rest_ok, 1)
                dve.wait_ge(mid_ok, n + 1)
                nc.vector.tensor_tensor(part[2][:, piece(n)], rest[:, piece(n)], part[1][:, piece(n)], ALU.subtract).then_inc(lo_ok, 1)


def attention_queries(k, l, x):
    nc, d = k.nc, k.dram
    U = 3
    with k.phase(f"aq{l}") as (sb, sem, block, hop):
        wq = sb("wq", [D, H * D])
        wkT = sb("wkT", [D, H, D])
        we = sb("we", [D, H * D])
        w_eeT = sb("w_eeT", [D, 2 * D + GK + 1])
        hb = sb("hb", [D, 4, H])
        eg = sb("eg", [D, H, D + GK])
        q = sb("q", [D, U, H, CW])
        qt = sb("qt", [D, U, WC, 2, H, WN])
        rest = sb("rest", [GK, U, WC, H, WN])
        part = sb("part", [GK, U, 3, WC, H, WN], BF16)
        w_in, mixed, mixed_c = sem("w_in"), sem("mixed"), sem("mixed_c")
        out = [sem(f"out{u}") for u in range(U)]
        pe_q, pe_both, pe_geo = sem("pe_q"), sem("pe_both"), sem("pe_geo")
        act_ = Steps(sem("act"), [f"Q{h}" for h in range(H)] + [f"QK{h}" for h in range(H)] + ["HI0", "HI1"], U)
        dve_ = Steps(sem("dve"), ["REST0", "REST1", "MID", "LO"], U)
        heads = (slice(0, 2), slice(2, 3))
        loads = [(wq[:, :], d["Wq"][l]), (wkT[:, :, :], d["WkT"][l].rearrange("(h c) i -> c h i", c=D)), (we[:, :], d["We"][l]),
                 (w_eeT[:, :], d["W_eeT"]), (hb[:, :, :], d["hb"][l])]
        outs = 16 * (1 + PAIRS)

        def geo_bank(n):
            hs = heads[n]
            return k.ps[0:GK, 2 + n, 0:(hs.stop - hs.start) * CW].rearrange("p (h w n) -> p h w n", w=WC, n=WN)

        @block.sync
        def _(sp):
            k.clear_old(sp)
            for to, src in loads:
                sp.dma_start(to, src).then_inc(w_in, 16)
            for u in range(U):
                sp.sem_inc(out[u], outs)
            with sp.Fori(0, NWC // U) as i:
                for u in range(U):
                    c = U * i + u
                    sp.wait_ge(act_.sem, act_.of(c, f"QK{H - 1}"))
                    sp.dma_start(d["qt"][bass.ds(c * WC, WC), :, :, :].rearrange("w k t n -> k w (t n)"),
                                 qt[:, u, :, :, :, :].rearrange("k w t h n -> k w (t h n)")).then_inc(out[u], 16)
                    sp.wait_ge(dve_.sem, dve_.of(c, "LO"))
                    for n, t in enumerate(QUERY_PARTS):
                        sp.dma_start(d["qs"][bass.ds(c * WC, WC), n * GK:(n + 1) * GK, :].rearrange("w k n -> k w n"),
                                     part[:, u, t, :, :, :].rearrange("k w h n -> k w (h n)")).then_inc(out[u], 16)
            for u in range(U):
                sp.wait_ge(out[u], outs * (NWC // U + 1))

        @block.tensor
        def _(pe):
            pe.wait_ge(w_in, 16 * len(loads))
            for h in range(H):
                nc.tensor.matmul(k.ps[:, h, 0:D + GK], we[:, h * D:(h + 1) * D], w_eeT[:, D:2 * D + GK],
                                 start=True, stop=True).then_inc(mixed, 1)
            pe.wait_ge(mixed_c, H)
            with pe.Fori(0, NWC // U) as i:
                def first(u):
                    c = U * i + u
                    cols = bass.ds(c * CW, CW)
                    pe.wait_ge(act_.sem, act_.of(c - 1, f"Q{H - 1}"))
                    for h in range(H):
                        m = nc.tensor.matmul(k.ps[:, h // 2, (h % 2) * CW:(h % 2 + 1) * CW], wq[:, h * D:(h + 1) * D],
                                             x[:, cols], start=True, stop=True)
                    m.then_inc(pe_q, 1)

                def second(u):
                    c = U * i + u
                    for h in range(H):
                        pe.wait_ge(act_.sem, act_.of(c, f"Q{h}"))
                        pe.wait_ge(act_.sem, act_.of(c - 1, f"QK{h}"))
                        nc.tensor.matmul(k.ps[:, 4 + h, 0:CW], wkT[:, h, :], q[:, u, h, :], start=True, stop=True)
                        nc.tensor.matmul(k.ps[:, 4 + h, CW:2 * CW], eg[:, h, 0:D], q[:, u, h, :], start=True, stop=True
                                         ).then_inc(pe_both, 1)
                    pe.wait_ge(dve_.sem, dve_.of(c - 1, "REST1"))
                    for h in range(H):
                        m = nc.tensor.matmul(k.ps[0:GK, 2 + h // 2, (h % 2) * CW:(h % 2 + 1) * CW], eg[:, h, D:D + GK],
                                             q[:, u, h, :], start=True, stop=True)
                    m.then_inc(pe_geo, 1)

                first(0)
                first(1)
                second(0)
                first(2)
                second(1)
                second(2)

        @block.scalar
        def _(act):
            act.wait_ge(w_in, 16 * len(loads))
            act_.prime(act)
            with act.Fori(0, NWC // U) as i:
                for u in range(U):
                    c = U * i + u
                    act.wait_ge(pe_q, c + 1)
                    for h in range(H):
                        nc.scalar.activation(q[:, u, h, :], k.ps[:, h // 2, (h % 2) * CW:(h % 2 + 1) * CW], ACT.Identity,
                                             bias=hb[:, 0, h:h + 1]).then_inc(act_.sem, 1)
                    act.wait_ge(out[u], i * outs + outs)
                    for h in range(H):
                        act.wait_ge(pe_both, c * H + h + 1)
                        nc.scalar.activation(qt[:, u, :, :, h, :].rearrange("p w t n -> p t w n"),
                                             k.ps[:, 4 + h, 0:2 * CW].rearrange("p (t w n) -> p t w n", t=2, n=WN),
                                             ACT.Copy).then_inc(act_.sem, 1)
                    act.wait_ge(pe_geo, c + 1)
                    for n in range(2):
                        nc.scalar.activation(part[:, u, 0, :, heads[n], :].rearrange("p w h n -> p h w n"), geo_bank(n),
                                             ACT.Copy).then_inc(act_.sem, 1)

        @block.vector
        def _(dve):
            for h in range(H):
                dve.wait_ge(mixed, h + 1)
                nc.vector.tensor_copy(eg[:, h, :], k.ps[:, h, 0:D + GK]).then_inc(mixed_c, 1)
            dve_.prime(dve)
            s = dve_.sem
            with dve.Fori(0, NWC // U) as i:
                for u in range(U):
                    c = U * i + u
                    for n in range(2):
                        dve.wait_ge(act_.sem, act_.of(c, f"HI{n}"))
                        nc.vector.tensor_tensor(rest[:, u, :, heads[n], :].rearrange("p w h n -> p h w n"), geo_bank(n),
                                                part[:, u, 0, :, heads[n], :].rearrange("p w h n -> p h w n"), ALU.subtract
                                                ).then_inc(s, 1)
                    dve.wait_ge(s, dve_.of(c, "REST1"))
                    nc.vector.tensor_copy(part[:, u, 1, :, :, :], rest[:, u, :, :, :]).then_inc(s, 1)
                    dve.wait_ge(s, dve_.of(c, "MID"))
                    nc.vector.tensor_tensor(part[:, u, 2, :, :, :], rest[:, u, :, :, :], part[:, u, 1, :, :, :],
                                            ALU.subtract).then_inc(s, 1)


def attention_windows(k, l):
    nc, d = k.nc, k.dram
    U = 5
    W = D if l == 0 else 2 * D
    HS = S // 2
    JH = T // 2
    SCALE = float(D) ** -0.5
    table = d[f"lrows{l}"]
    with k.phase(f"aw{l}") as (sb, sem, block, hop):
        sd = sb("sd", [128, U, 2 * T], I32)
        geoS = sb("geoS", [KS, U, S], BF16)
        qt = sb("qt", [D, U, 2, WH])
        qs = sb("qs", [KS, U, WH], BF16)
        g = sb("g", [128, U, T, W])
        dxg = sb("dxg", [128, U, T, D + GK])
        base = sb("base", [128, 1])
        dl = sb("dl", [128, U, T])
        sel = sb("sel", [128, U, T, WN], BF16)
        off = sb("off", [128, U, T, H, WN], BF16)
        yT = sb("yT", [D, U, 2, S])
        p = sb("p", [WH, U, 2, HS])
        pT = sb("pT", [128, U, 2, JH * WH])
        mx, neg, den, den3, inv = (sb(n, [WH, U]) for n in ("mx", "neg", "den", "den3", "inv"))
        ag = sb("ag", [D, U, WH])
        agr = sb("agr", [WH, U, D + GK])
        base_ok = sem("base_ok")
        idx_in, in_, out = ([sem(f"{n}{u}") for u in range(U)] for n in ("idx_in", "in", "out"))
        rows_in, rows_base = k.rows_in, list(k.rows_base)
        turned = Steps(sem("turned"), ["T0", "T1", "T2"], U)
        scored = Steps(sem("scored"), ["S"], U)
        weights_turned = Steps(sem("weights_turned"), ["PT"], U)
        summed = Steps(sem("summed"), ["AG"], U)
        yT_ok = Steps(sem("yT_ok"), ["T0", "T1", "T2"], U)
        pT_ok = Steps(sem("pT_ok"), ["P0", "P1"], U)
        exped = Steps(sem("exped"), ["E"], U)
        ag_ok = Steps(sem("ag_ok"), ["X", "G"], U)
        ready = Steps(sem("ready"), ["DX", "DL", "SEL", "OFF", "BASE"], U)
        soft = Steps(sem("soft"), ["MAX", "NEG", "DEN", "INV", "P"], U)
        x0 = W - D

        @block.sync
        def _(sp):
            def load(w, u):
                at = sp.value_load(k.starts[0:1, bass.ds(w, 1)], min_val=0, max_val=E)
                sp.wait_ge(ready.sem, ready.of(w - U, "OFF"))
                sp.dma_start(sd[:, u, :], d["sd"][bass.ds(at, S), :].rearrange("(p j) s -> p (j s)", j=T)).then_inc(idx_in[u], 16)
                sp.wait_ge(summed.sem, summed.of(w - U, "AG"))
                sp.dma_start(dxg[:, u, :, D:D + GK], d["geo"][bass.ds(at, S), :].rearrange("(p j) f -> p j f", j=T)).then_inc(in_[u], 16)
                sp.dma_start(geoS[:, u, :], d["geoS"][:, bass.ds(at, S)]).then_inc(in_[u], 16)
                sp.dma_start(qt[:, u, :, :], d["qt"][bass.ds(w, 1), :, :, :].rearrange("w k t n -> (w k) t n")).then_inc(in_[u], 16)
                sp.dma_start(qs[:, u, :], d["qs"][bass.ds(w, 1), :, :].rearrange("w k n -> (w k) n")).then_inc(in_[u], 16)

            def store(w, u):
                sp.wait_ge(ag_ok.sem, ag_ok.of(w, "G"))
                sp.dma_start(d["agx"][bass.ds(w, 1), :, :].rearrange("w k n -> (w k) n"), ag[:, u, :]).then_inc(out[u], 16)
                sp.dma_start(d["agr"][bass.ds(w, 1), :, :].rearrange("w k n -> (w k) n"), agr[:, u, :]).then_inc(out[u], 16)

            k.clear_old(sp)
            with sp.If(sp.value_load(k.fits[0:1, 0:1], min_val=0, max_val=1) == 1):
                for u in range(U):
                    load(u, u)
                with sp.Fori(0, NW // U - 1) as i:
                    for u in range(U):
                        w = U * i + u
                        load(w + U, u)
                        store(w, u)
                for u in range(U):
                    store(NW - U + u, u)
                for u in range(U):
                    sp.wait_ge(out[u], 32 * (NW // U + 1))

        @block.gpsimd
        def _(pool):
            pool.memset(base[:, :], 0.0).then_inc(base_ok, 1)
            with pool.If(pool.value_load(k.fits[0:1, 0:1], min_val=0, max_val=1) == 1):
                with pool.Fori(0, NW // U) as i:
                    for u in range(U):
                        w = U * i + u
                        pool.wait_ge(summed.sem, summed.of(w - U, "AG"))
                        pool.sem_inc(hop["pool"], 1)
                        pool.wait_ge(idx_in[u], (i + 1) * 16)
                        pool.sem_inc(hop["pool"], 1)
                        for j in range(T):
                            pool.indirect_dma_start(out=g[:, u, j, :], out_offset=None, in_=table,
                                                    in_offset=bass.IndirectOffsetOnAxis(ap=sd[:, u, 2 * j:2 * j + 1], axis=0)
                                                    ).then_inc(rows_in[u], 16)

        @block.tensor
        def _(pe):
            def turn_features(w, u, i):
                pe.wait_ge(rows_in[u], (i + 1) * 16 * T + rows_base[u])
                pe.wait_ge(ready.sem, ready.of(w, "DX"))
                for n in range(3):
                    pe.wait_ge(yT_ok.sem, yT_ok.of(w - 1, f"T{n}"))
                    for q in range(4):
                        what, j = divmod(4 * n + q, T)
                        m = nc.tensor.transpose(k.ps[:, n, q * 128:(q + 1) * 128],
                                                dxg[:, u, j, 0:D] if what else g[:, u, j, 0:D], k.ident[:, :])
                    m.then_inc(turned.sem, 1)

            def scores(w, u, i):
                pe.wait_ge(in_[u], (i + 1) * 64)
                pe.wait_ge(ready.sem, ready.of(w, "OFF"))
                pe.wait_ge(exped.sem, exped.of(w - 1, "E"))
                for half in range(2):
                    to = k.ps[0:WH, 3 + half, 0:HS]
                    for j in range(JH):
                        nc.tensor.matmul(k.ps[0:WH, 3 + half, j * 128:(j + 1) * 128],
                                         off[:, u, half * JH + j, :, :].rearrange("p h n -> p (h n)"), k.far[:, :],
                                         start=j == 0, stop=False)
                    nc.tensor.matmul(to, qs[:, u, :], geoS[:, u, :].rearrange("f (p j) -> f j p", j=T)[:, half * JH:(half + 1) * JH, :],
                                     start=False, stop=False)
                    pe.wait_ge(yT_ok.sem, yT_ok.of(w, "T2"))
                    for t in range(2):
                        m = nc.tensor.matmul(to, qt[:, u, t, :], yT[:, u, t, half * HS:(half + 1) * HS], start=False, stop=t == 1)
                m.then_inc(scored.sem, 1)

            def turn_weights(w, u, i):
                pe.wait_ge(soft.sem, soft.of(w, "P"))
                pe.wait_ge(pT_ok.sem, pT_ok.of(w - 1, "P1"))
                for j in range(T):
                    m = nc.tensor.transpose(k.ps[:, 5 + j // JH, (j % JH) * WH:(j % JH + 1) * WH],
                                            p[:, u, j // JH, (j % JH) * 128:(j % JH + 1) * 128], k.ident[0:WH, 0:WH])
                m.then_inc(weights_turned.sem, 1)

            def sums(w, u, i):
                pe.wait_ge(pT_ok.sem, pT_ok.of(w, "P1"))
                pe.wait_ge(ag_ok.sem, ag_ok.of(w - 1, "G"))
                for j in range(T):
                    w_ = pT[:, u, j // JH, (j % JH) * WH:(j % JH + 1) * WH]
                    nc.tensor.matmul(k.ps[:, 7, 0:WH], g[:, u, j, 0:D], w_, start=j == 0, stop=j == T - 1)
                for j in range(T):
                    w_ = pT[:, u, j // JH, (j % JH) * WH:(j % JH + 1) * WH]
                    m = nc.tensor.matmul(k.ps[0:WH, 7, WH:WH + D + GK], w_, dxg[:, u, j, :], start=j == 0, stop=j == T - 1)
                m.then_inc(summed.sem, 1)

            def turn(w, u, i):
                before = (w - 1, (u - 1) % U, i if u else i - 1)
                turn_features(w, u, i)
                turn_weights(*before)
                scores(w, u, i)
                sums(*before)

            with pe.If(pe.value_load(k.fits[0:1, 0:1], min_val=0, max_val=1) == 1):
                for s in (turned, scored, weights_turned, summed):
                    s.prime(pe)
                turn_features(0, 0, 0)
                scores(0, 0, 0)
                with pe.Fori(0, NW // U - 1) as i:
                    for u in range(1, U):
                        turn(U * i + u, u, i)
                    turn(U * i + U, 0, i + 1)
                for u in range(1, U):
                    turn(NW - U + u, u, NW // U - 1)
                turn_weights(NW - 1, U - 1, NW // U - 1)
                sums(NW - 1, U - 1, NW // U - 1)

        @block.scalar
        def _(act):
            def copy_features(w, u, i):
                for n in range(3):
                    act.wait_ge(turned.sem, turned.of(w, f"T{n}"))
                    act.sem_inc(hop["act"], 1)
                    act.wait_ge(scored.sem, scored.of(w - U, "S"))
                    nc.scalar.activation(yT[:, u, :, :].rearrange("p t s -> p (t s)")[:, n * 512:(n + 1) * 512], k.ps[:, n, :],
                                         ACT.Copy).then_inc(yT_ok.sem, 1)

            def exponentials(w, u, i):
                act.wait_ge(soft.sem, soft.of(w, "NEG"))
                act.sem_inc(hop["act"], 1)
                act.wait_ge(weights_turned.sem, weights_turned.of(w - U, "PT"))
                nc.scalar.activation(p[:, u, :, :], k.ps[0:WH, 3:5, 0:HS], ACT.Exp, bias=neg[:, u:u + 1], scale=SCALE,
                                     accum_out=den[:, u:u + 1]).then_inc(exped.sem, 1)

            def copy_weights(w, u, i):
                act.wait_ge(weights_turned.sem, weights_turned.of(w, "PT"))
                act.sem_inc(hop["act"], 1)
                act.wait_ge(summed.sem, summed.of(w - U, "AG"))
                for half in range(2):
                    nc.scalar.activation(pT[:, u, half, :], k.ps[:, 5 + half, 0:JH * WH], ACT.Copy).then_inc(pT_ok.sem, 1)

            def copy_sums(w, u, i):
                act.wait_ge(summed.sem, summed.of(w, "AG"))
                act.sem_inc(hop["act"], 1)
                act.wait_ge(out[u], (i + 1) * 32)
                nc.scalar.activation(ag[:, u, :], k.ps[:, 7, 0:WH], ACT.Copy).then_inc(ag_ok.sem, 1)
                nc.scalar.activation(agr[:, u, :], k.ps[0:WH, 7, WH:WH + D + GK], ACT.Copy).then_inc(ag_ok.sem, 1)

            def turn(w, u, i):
                before = (w - 1, (u - 1) % U, i if u else i - 1)
                copy_features(w, u, i)
                copy_weights(*before)
                exponentials(w, u, i)
                copy_sums(*before)

            with act.If(act.value_load(k.fits[0:1, 0:1], min_val=0, max_val=1) == 1):
                for s in (yT_ok, pT_ok, exped, ag_ok):
                    s.prime(act)
                for u in range(U):
                    act.sem_inc(out[u], 32)
                copy_features(0, 0, 0)
                exponentials(0, 0, 0)
                with act.Fori(0, NW // U - 1) as i:
                    for u in range(1, U):
                        turn(U * i + u, u, i)
                    turn(U * i + U, 0, i + 1)
                for u in range(1, U):
                    turn(NW - U + u, u, NW // U - 1)
                copy_weights(NW - 1, U - 1, NW // U - 1)
                copy_sums(NW - 1, U - 1, NW // U - 1)

        @block.vector
        def _(dve):
            def inputs(w, u, i):
                dve.wait_ge(rows_in[u], (i + 1) * 16 * T + rows_base[u])
                dve.wait_ge(in_[u], (i + 1) * 64)
                dve.wait_ge(summed.sem, summed.of(w - U, "AG"))
                s = ready.sem
                nc.vector.tensor_tensor(dxg[:, u, :, 0:D], g[:, u, :, x0:x0 + D], bc(dxg[:, u, :, D:D + 1], [128, T, D]),
                                        ALU.mult).then_inc(s, 1)
                dve.wait_ge(s, ready.of(w - 1, "BASE"))
                nc.vector.tensor_scalar(dl[:, u, :], sd[:, u, :].rearrange("p (j s) -> p s j", s=2)[:, 1, :], base[:, 0:1], None,
                                        ALU.subtract).then_inc(s, 1)
                dve.wait_ge(s, ready.of(w, "DL"))
                nc.vector.tensor_tensor(sel[:, u, :, :], bc(k.iota_wn[:, :].unsqueeze(1), [128, T, WN]),
                                        bc(dl[:, u, :].unsqueeze(2), [128, T, WN]), ALU.is_equal).then_inc(s, 1)
                dve.wait_ge(s, ready.of(w, "SEL"))
                nc.vector.tensor_scalar(off[:, u, :, :, :], bc(sel[:, u, :, :].unsqueeze(2), [128, T, H, WN]), -1.0, None, ALU.add).then_inc(s, 1)
                nc.vector.tensor_scalar(base[:, :], base[:, :], float(WN), None, ALU.add).then_inc(s, 1)

            def maximum(w, u, i):
                s = soft.sem
                dve.wait_ge(scored.sem, scored.of(w, "S"))
                nc.vector.tensor_reduce(mx[:, u:u + 1], k.ps[0:WH, 3:5, 0:HS], AX.XY, ALU.max).then_inc(s, 1)
                dve.wait_ge(s, soft.of(w, "MAX"))
                nc.vector.tensor_scalar(neg[:, u:u + 1], mx[:, u:u + 1], FLOOR, -SCALE, ALU.max, ALU.mult).then_inc(s, 1)

            def normalise(w, u, i):
                s = soft.sem
                dve.wait_ge(exped.sem, exped.of(w, "E"))
                nc.vector.tensor_scalar(den3[:, u:u + 1], den[:, u:u + 1], 1e-16, float(H), ALU.add, ALU.mult).then_inc(s, 1)
                dve.wait_ge(s, soft.of(w, "DEN"))
                nc.vector.reciprocal(inv[:, u:u + 1], den3[:, u:u + 1]).then_inc(s, 1)
                dve.wait_ge(s, soft.of(w, "INV"))
                nc.vector.tensor_scalar(p[:, u, :, :], p[:, u, :, :], inv[:, u:u + 1], None, ALU.mult).then_inc(s, 1)

            def turn(w, u, i, more=True):
                maximum(w, u, i)
                if more:
                    inputs(w + 1, (u + 1) % U, i if u < U - 1 else i + 1)
                normalise(w, u, i)

            with dve.If(dve.value_load(k.fits[0:1, 0:1], min_val=0, max_val=1) == 1):
                ready.prime(dve)
                soft.prime(dve)
                dve.wait_ge(base_ok, 1)
                inputs(0, 0, 0)
                with dve.Fori(0, NW // U - 1) as i:
                    for u in range(U):
                        turn(U * i + u, u, i)
                for u in range(U):
                    turn(NW - U + u, u, NW // U - 1, more=u < U - 1)
        for u in range(U):
            k.rows_base[u] += NW // U * 16 * T


def attention_outputs(k, l, h0, x, outT):
    nc, d = k.nc, k.dram
    U = 3
    with k.phase(f"ao{l}") as (sb, sem, block, hop):
        wv = sb("wv", [D, H * D])
        we = sb("we", [D, H * D])
        w_eeT = sb("w_eeT", [D, 2 * D + GK + 1])
        ws = sb("ws", [D, D])
        wr = sb("wr", [D, D])
        hb = sb("hb", [D, 4, H])
        bs = sb("bs", [D, 4])
        bias = sb("bias", [D, 1])
        ex = sb("ex", [D, H * D])
        eg = sb("eg", [GK, H * D])
        eh = sb("eh", [D, D])
        vb, vsum, vall = sb("vb", [D, 1]), sb("vsum", [D, H]), sb("vall", [D, 1])
        has = sb("has", [128, NP])
        ax = sb("ax", [D, U, WC, H, WN])
        ar = sb("ar", [WH, U, WC, D + GK])
        ad = sb("ad", [D, U, WC, H, WN])
        ag = sb("ag", [GK, U, WC, H, WN])
        own, y, y2 = (sb(n, [D, U, CW]) for n in ("own", "y", "y2"))
        w_in, mixed, mixed_c, deg_in = sem("w_in"), sem("mixed"), sem("mixed_c"), sem("deg_in")
        in_ = [sem(f"in{u}") for u in range(U)]
        pe_ = Steps(sem("pe"), ["TG", "OUT"], U)
        act_ = Steps(sem("act"), ["AD0", "AG0", "AD1", "AG1"], U)
        dve_ = Steps(sem("dve"), ["OWN", "Y", "OUT"] + (["RELU"] if l else []), U)
        loads = [(wv[:, :], d["Wv"][l]), (we[:, :], d["We"][l]), (w_eeT[:, :], d["W_eeT"]), (ws[:, :], d["Ws"][l]),
                 (wr[:, :], d["W_res"]), (hb[:, :, :], d["hb"][l]), (bs[:, :], d["bs"])]
        steps = 9
        turn_banks = (range(0, WC // 2 + 1), range(WC // 2 + 1, WC))

        @block.sync
        def _(sp):
            k.clear_old(sp)
            for to, src in loads:
                sp.dma_start(to, src).then_inc(w_in, 16)
            sp.dma_start(has[:, :], d["deg"].partition_broadcast(128)).then_inc(deg_in, 16)
            with sp.Fori(0, NWC // U) as i:
                for u in range(U):
                    c = U * i + u
                    sp.wait_ge(pe_.sem, pe_.of(c - U, "OUT"))
                    sp.dma_start(ax[:, u, :, :, :].rearrange("k w h n -> k w (h n)"),
                                 d["agx"][bass.ds(c * WC, WC), :, :].rearrange("w k n -> k w n")).then_inc(in_[u], 16)
                    sp.dma_start(ar[:, u, :, :], d["agr"][bass.ds(c * WC, WC), :, :].rearrange("w m g -> m w g")).then_inc(in_[u], 16)

        @block.tensor
        def _(pe):
            pe.wait_ge(w_in, 16 * len(loads))
            nc.tensor.matmul(k.ps[:, 1, 0:H * D], w_eeT[:, D:2 * D], we[:, :], start=True, stop=True)
            nc.tensor.matmul(k.ps[0:GK, 2, 0:H * D], w_eeT[:, 2 * D:2 * D + GK], we[:, :], start=True, stop=True)
            for h in range(H):
                nc.tensor.matmul(k.ps[:, 0, 0:D], w_eeT[:, 0:D], we[:, h * D:(h + 1) * D], start=h == 0, stop=h == H - 1)
            for h in range(H):
                m = nc.tensor.matmul(k.ps[:, 3, 0:1], we[:, h * D:(h + 1) * D], w_eeT[:, 2 * D + GK:2 * D + GK + 1],
                                     start=h == 0, stop=h == H - 1)
            m.then_inc(mixed, 1)
            pe.wait_ge(mixed_c, steps)
            pe_.prime(pe)
            with pe.Fori(0, NWC // U) as i:
                for u in range(U):
                    c = U * i + u
                    cols = bass.ds(c * CW, CW)
                    b = u % 2
                    pe.wait_ge(in_[u], (i + 1) * 32)
                    pe.wait_ge(act_.sem, act_.of(c - 1, "AG1"))
                    for n in range(2):
                        for q, w in enumerate(turn_banks[n]):
                            nc.tensor.transpose(k.ps[:, 6 + n, q * WH:(q + 1) * WH], ar[:, u, w, 0:D], k.ident[0:WH, 0:WH])
                            m = nc.tensor.transpose(k.ps[0:GK, 4 + n, q * WH:(q + 1) * WH], ar[:, u, w, D:D + GK], k.ident[0:WH, 0:WH])
                    m.then_inc(pe_.sem, 1)
                    pe.wait_ge(dve_.sem, dve_.of(c - (1 if u == 0 else 2), "Y"))
                    nc.tensor.matmul(k.ps[:, 2 + b, 0:CW], eh[:, :], h0[:, cols], start=True, stop=True)
                    to = k.ps[:, b, 0:CW]
                    nc.tensor.matmul(to, ws[:, :], x[:, cols], start=True, stop=False)
                    if l == 0:
                        nc.tensor.matmul(to, wr[:, :], x[:, cols], start=False, stop=False)
                    for h in range(H):
                        hs = slice(h * D, (h + 1) * D)
                        nc.tensor.matmul(to, wv[:, hs], ax[:, u, :, h, :], start=False, stop=False)
                    pe.wait_ge(act_.sem, act_.of(c, "AG1"))
                    for h in range(H):
                        nc.tensor.matmul(to, ex[:, h * D:(h + 1) * D], ad[:, u, :, h, :], start=False, stop=False)
                        m = nc.tensor.matmul(to, eg[:, h * D:(h + 1) * D], ag[:, u, :, h, :], start=False, stop=h == H - 1)
                    m.then_inc(pe_.sem, 1)

        @block.scalar
        def _(act):
            act_.prime(act)
            with act.Fori(0, NWC // U) as i:
                for u in range(U):
                    c = U * i + u
                    act.wait_ge(pe_.sem, pe_.of(c, "TG"))
                    for n in range(2):
                        ws_ = turn_banks[n]
                        nc.scalar.activation(ad[:, u, ws_.start:ws_.stop, :, :].rearrange("p w h n -> p (w h n)"),
                                             k.ps[:, 6 + n, 0:len(ws_) * WH], ACT.Copy).then_inc(act_.sem, 1)
                        nc.scalar.activation(ag[:, u, ws_.start:ws_.stop, :, :].rearrange("p w h n -> p (w h n)"),
                                             k.ps[0:GK, 4 + n, 0:len(ws_) * WH], ACT.Copy).then_inc(act_.sem, 1)

        @block.vector
        def _(dve):
            s = dve_.sem
            dve.wait_ge(w_in, 16 * len(loads))
            dve.wait_ge(mixed, 1)
            nc.vector.tensor_copy(ex[:, :], k.ps[:, 1, 0:H * D]).then_inc(mixed_c, 1)
            nc.vector.tensor_copy(eg[:, :], k.ps[0:GK, 2, 0:H * D]).then_inc(mixed_c, 1)
            nc.vector.tensor_scalar(eh[:, :], k.ps[:, 0, 0:D], 1.0 / H, None, ALU.mult).then_inc(mixed_c, 1)
            nc.vector.tensor_tensor(vsum[:, :], hb[:, 2, :], hb[:, 3, :], ALU.add).then_inc(mixed_c, 1)
            if l == 0:
                nc.vector.tensor_tensor(bias[:, :], bs[:, 0:1], bs[:, 3:4], ALU.add).then_inc(mixed_c, 1)
            else:
                nc.vector.tensor_copy(bias[:, :], bs[:, l:l + 1]).then_inc(mixed_c, 1)
            dve.wait_ge(deg_in, 16)
            nc.vector.tensor_scalar(has[:, :], has[:, :], 1.0, None, ALU.min).then_inc(mixed_c, 1)
            dve.wait_ge(mixed_c, 6)
            nc.vector.reduce_sum(vall[:, :], vsum[:, :], AX.X).then_inc(mixed_c, 1)
            dve.wait_ge(mixed_c, 7)
            nc.vector.tensor_tensor(vall[:, :], vall[:, :], k.ps[:, 3, 0:1], ALU.add).then_inc(mixed_c, 1)
            dve.wait_ge(mixed_c, 8)
            nc.vector.tensor_scalar(vb[:, :], vall[:, :], 1.0 / H, None, ALU.mult).then_inc(mixed_c, 1)
            dve.wait_ge(mixed_c, steps)
            dve_.prime(dve)
            with dve.Fori(0, NWC // U) as i:
                for u in range(U):
                    c = U * i + u
                    cols = bass.ds(c * CW, CW)
                    b = u % 2
                    dve.wait_ge(pe_.sem, pe_.of(c, "OUT"))
                    nc.vector.scalar_tensor_tensor(own[:, u, :], k.ps[:, 2 + b, 0:CW], vb[:, 0:1], has[:, cols], ALU.add,
                                                   ALU.mult).then_inc(s, 1)
                    dve.wait_ge(s, dve_.of(c, "OWN"))
                    nc.vector.scalar_tensor_tensor(y[:, u, :], k.ps[:, b, 0:CW], bias[:, 0:1], own[:, u, :], ALU.add,
                                                   ALU.add).then_inc(s, 1)
                    dve.wait_ge(s, dve_.of(c, "Y"))
                    if l == 0:
                        nc.vector.tensor_scalar(outT[:, cols], y[:, u, :], 0.0, None, ALU.max).then_inc(s, 1)
                    else:
                        nc.vector.tensor_tensor(y2[:, u, :], y[:, u, :], x[:, cols], ALU.add).then_inc(s, 1)
                        dve.wait_ge(s, dve_.of(c, "OUT"))
                        nc.vector.tensor_scalar(outT[:, cols], y2[:, u, :], 0.0, None, ALU.max).then_inc(s, 1)
            dve.wait_ge(s, dve_.of(NWC - 1, "RELU" if l else "OUT"))


def attention_layers(k):
    nc, d = k.nc, k.dram
    geometry_parts(k)
    with ExitStack() as l1:
        h0 = l1.enter_context(nc.sbuf_tensor("l1_h0", [128, 1, NP], F32))
        x = l1.enter_context(nc.sbuf_tensor("l1_x", [128, 1, NP], F32))
        layer_norm(k, "ln1", k.xT[:, :].unsqueeze(1), h0, relu=True)
        node_rows(k, "lr0", h0[:, 0, :], None, D, [(d["lrows0"], 0, D), (d["lrows1"][:, D:2 * D], 0, D), (d["lrows2"][:, D:2 * D], 0, D)])
        now = h0
        for l in range(3):
            attention_queries(k, l, now[:, 0, :])
            attention_windows(k, l)
            general_attention(k, l)
            attention_outputs(k, l, h0[:, 0, :], now[:, 0, :], x[:, 0, :])
            now = x
            if l < 2:
                node_rows(k, f"lr{l + 1}", x[:, 0, :], None, D, [(d[f"lrows{l + 1}"][:, 0:D], 0, D)])
        dense(k, "ctr", k.xT[:, :].unsqueeze(1), [[(d["W_ctr"][0:D, :], h0[:, 0, :]), (d["W_ctr"][D:2 * D, :], x[:, 0, :])]],
              bias=d["b_ctr"], add=k.xT[:, :])


def degree_scales(k, inv_deg, dinv):
    nc, d = k.nc, k.dram
    with k.phase("deg") as (sb, sem, block, hop):
        deg, root = sb("deg", [128, NP]), sb("root", [128, NP])
        deg_in, most_ok, root_ok, done = (sem(n) for n in ("deg_in", "most_ok", "root_ok", "done"))

        @block.sync
        def _(sp):
            k.clear_old(sp)
            sp.dma_start(deg[:, :], d["deg"].partition_broadcast(128)).then_inc(deg_in, 16)

        @block.scalar
        def _(act):
            act.wait_ge(deg_in, 16)
            nc.scalar.activation(root[:, :], deg[:, :], ACT.Sqrt, bias=k.ones[:, 0:1]).then_inc(root_ok, 1)

        @block.vector
        def _(dve):
            dve.wait_ge(deg_in, 16)
            nc.vector.tensor_scalar(inv_deg[:, :], deg[:, :], 1.0, None, ALU.max).then_inc(most_ok, 1)
            dve.wait_ge(most_ok, 1)
            nc.vector.reciprocal(inv_deg[:, :], inv_deg[:, :]).then_inc(done, 1)
            dve.wait_ge(root_ok, 1)
            nc.vector.reciprocal(dinv[:, :], root[:, :]).then_inc(done, 1)
            dve.wait_ge(done, 2)


def aggregate(k, name, h, out, scale, parts=1, loops=False, bias=None):
    nc, d = k.nc, k.dram
    GB = 4
    groups = [(g, p) for g in range(-(-NB // GB)) for p in range(parts)]
    chunks = [(c, p) for c in range(-(-NW // AW)) for p in range(parts)]
    with k.phase(name) as (sb, sem, block, hop):
        table = sb("table", [BM, parts, 3, NB, D], BF16)
        rest = sb("rest", [BM, 2, GB, D])
        adj = sb("adj", [BM, 2, AW, NB * WN], BF16)
        tmp = sb("tmp", [128, 2, AW * WN])
        scaled, turned, hi_ok, rest_ok, mid_ok, lo_ok, summed, added, times_ok, stored = (
            sem(n) for n in ("scaled", "turned", "hi_ok", "rest_ok", "mid_ok", "lo_ok", "summed", "added", "times_ok", "stored"))
        adj_in = [sem(f"adj_in{u}") for u in range(2)]
        bias_in = sem("bias_in")
        bt = None
        if bias is not None:
            bt = sb("bt", [128, 1])

        def blocks(g):
            return range(g * GB, min((g + 1) * GB, NB))

        def windows(c):
            return min(AW, NW - c * AW)

        @block.sync
        def _(sp):
            k.clear_old(sp)
            with sp.If(sp.value_load(k.fits[0:1, 0:1], min_val=0, max_val=1) == 1):
                if bt is not None:
                    sp.dma_start(bt[:, :], bias).then_inc(bias_in, 16)
                for c in range(len(chunks) // parts):
                    if c >= 2:
                        sp.wait_ge(summed, parts * (c - 1))
                    n = windows(c)
                    sp.dma_start(adj[:, c % 2, 0:n, :], d["adj"][c * AW:c * AW + n, :, :].rearrange("w m q -> m w q")).then_inc(adj_in[c % 2], 16)

        @block.tensor
        def _(pe):
            with pe.If(pe.value_load(k.fits[0:1, 0:1], min_val=0, max_val=1) == 1):
                for n, (g, p) in enumerate(groups):
                    if loops:
                        pe.wait_ge(scaled, n + 1)
                    if n >= 2:
                        pe.wait_ge(rest_ok, n - 1)
                    for q, b in enumerate(blocks(g)):
                        m = nc.tensor.transpose(k.ps[0:BM, n % 2, q * D:(q + 1) * D], h[:, p, b * BM:(b + 1) * BM], k.ident[:, :])
                    m.then_inc(turned, 1)
                pe.wait_ge(lo_ok, len(groups))
                for n, (c, p) in enumerate(chunks):
                    pe.wait_ge(adj_in[c % 2], 16 * (c // 2 + 1))
                    if n >= 4:
                        pe.wait_ge(stored if not loops else added, n - 3)
                    cols = windows(c)
                    for b in range(NB):
                        for t in range(3):
                            m = nc.tensor.matmul(k.ps[:, 2 + n % 4, 0:cols * WN], table[:, p, t, b, :],
                                                 adj[:, c % 2, 0:cols, b * WN:(b + 1) * WN],
                                                 start=b == 0 and t == 0, stop=b == NB - 1 and t == 2)
                    m.then_inc(summed, 1)

        @block.scalar
        def _(act):
            with act.If(act.value_load(k.fits[0:1, 0:1], min_val=0, max_val=1) == 1):
                def middle(n):
                    g, p = groups[n]
                    b = blocks(g)
                    act.wait_ge(rest_ok, n + 1)
                    nc.scalar.activation(table[:, p, 1, b.start:b.stop, :], rest[:, n % 2, 0:len(b), :], ACT.Copy).then_inc(mid_ok, 1)

                for n, (g, p) in enumerate(groups):
                    b = blocks(g)
                    act.wait_ge(turned, n + 1)
                    nc.scalar.activation(table[:, p, 0, b.start:b.stop, :],
                                         k.ps[0:BM, n % 2, 0:len(b) * D].rearrange("m (b f) -> m b f", f=D), ACT.Copy).then_inc(hi_ok, 1)
                    if n:
                        middle(n - 1)
                middle(len(groups) - 1)

        @block.vector
        def _(dve):
            with dve.If(dve.value_load(k.fits[0:1, 0:1], min_val=0, max_val=1) == 1):
                if loops:
                    for g, p in groups:
                        b = blocks(g)
                        cols = slice(b.start * BM, b.stop * BM)
                        nc.vector.tensor_tensor(h[:, p, cols], h[:, p, cols], scale[:, cols], ALU.mult).then_inc(scaled, 1)

                def lowest(n):
                    g, p = groups[n]
                    b = blocks(g)
                    dve.wait_ge(mid_ok, n + 1)
                    nc.vector.tensor_tensor(table[:, p, 2, b.start:b.stop, :], rest[:, n % 2, 0:len(b), :],
                                            table[:, p, 1, b.start:b.stop, :], ALU.subtract).then_inc(lo_ok, 1)

                for n, (g, p) in enumerate(groups):
                    b = blocks(g)
                    dve.wait_ge(hi_ok, n + 1)
                    if n >= 2:
                        dve.wait_ge(lo_ok, n - 1)
                    nc.vector.tensor_tensor(rest[:, n % 2, 0:len(b), :],
                                            k.ps[0:BM, n % 2, 0:len(b) * D].rearrange("m (b f) -> m b f", f=D),
                                            table[:, p, 0, b.start:b.stop, :], ALU.subtract).then_inc(rest_ok, 1)
                    if n:
                        lowest(n - 1)
                lowest(len(groups) - 1)
                if bt is not None:
                    dve.wait_ge(bias_in, 16)
                if loops:
                    dve.wait_ge(scaled, len(groups))
                for n, (c, p) in enumerate(chunks):
                    size = windows(c) * WN
                    cols = slice(c * AW * WN, c * AW * WN + size)
                    dve.wait_ge(summed, n + 1)
                    sums = k.ps[:, 2 + n % 4, 0:size]
                    if not loops:
                        nc.vector.tensor_tensor(out[:, p, cols], sums, scale[:, cols], ALU.mult).then_inc(stored, 1)
                        continue
                    if n >= 2:
                        dve.wait_ge(times_ok, n - 1)
                    nc.vector.tensor_tensor(tmp[:, n % 2, 0:size], sums, h[:, p, cols], ALU.add).then_inc(added, 1)
                    dve.wait_ge(added, n + 1)
                    nc.vector.tensor_tensor(out[:, p, cols], tmp[:, n % 2, 0:size], scale[:, cols], ALU.mult).then_inc(times_ok, 1)
                    if bt is not None:
                        dve.wait_ge(times_ok, n + 1)
                        nc.vector.tensor_scalar(out[:, p, cols], out[:, p, cols], bt[:, 0:1], 0.0, ALU.add, ALU.max).then_inc(stored, 1)
                if loops:
                    dve.wait_ge(times_ok, len(chunks))
                if bt is not None or not loops:
                    dve.wait_ge(stored, len(chunks))
    general_sums(k, "g" + name, out, h=h, scale=scale, parts=parts, loops=loops, bias=bias)


def adjacency_layers(k):
    nc, d = k.nc, k.dram
    x3 = k.xT[:, :].unsqueeze(1)
    with ExitStack() as both:
        inv_deg = both.enter_context(nc.sbuf_tensor("inv_deg", [128, NP], F32))
        dinv = both.enter_context(nc.sbuf_tensor("dinv", [128, NP], F32))
        degree_scales(k, inv_deg, dinv)
        with ExitStack() as l2:
            h, sums, h1 = (l2.enter_context(nc.sbuf_tensor(f"l2_{n}", [128, 1, NP], F32)) for n in ("h", "sums", "h1"))
            layer_norm(k, "ln2", x3, h, relu=True)
            aggregate(k, "n0", h, sums, inv_deg)
            dense(k, "sage0", h1, [[(d["W_self0T"], h[:, 0, :]), (d["W_neigh0T"], sums[:, 0, :])]], bias=d["b20"], relu=True)
            aggregate(k, "n1", h1, sums, inv_deg)
            dense(k, "sage1", x3, [[(d["W_self1T"], h1[:, 0, :]), (d["W_neigh1T"], sums[:, 0, :])]], bias=d["b21"], add=k.xT[:, :])
        with ExitStack() as l3:
            a, b = (l3.enter_context(nc.sbuf_tensor(f"l3_{n}", [128, 2, NP], F32)) for n in ("a", "b"))
            col = l3.enter_context(nc.sbuf_tensor("l3_col", [128, 10], F32))
            with k.phase("l3w") as (sb, sem, block, hop):
                w_in = sem("w_in")
                at = 0
                cols = {}
                for n, size in (("g1", 2), ("be1", 2), ("g2", 2), ("be2", 2), ("g3", 1), ("be3", 1)):
                    cols[n] = col[:, at:at + size]
                    at += size

                @block.sync
                def _(sp):
                    k.clear_old(sp)
                    for n, to in cols.items():
                        sp.dma_start(to, d["c" + n]).then_inc(w_in, 16)
                    sp.wait_ge(w_in, 16 * len(cols))

            def blocks(name, p, q):
                return d["g" + name][p * D:(p + 1) * D, q * D:(q + 1) * D]

            layer_norm(k, "ln3", x3, a[:, 0:1, :], relu=True)
            aggregate(k, "c1", a, a, dinv, loops=True)
            dense(k, "gcn1", b, [[(blocks("W1", 0, q), a[:, 0, :])] for q in range(2)], bias=d["cb1"], relu=True, parts=2)
            layer_norm(k, "lnc1", b, a, parts=2, gain=cols["g1"], shift=cols["be1"])
            aggregate(k, "c2", a, a, dinv, parts=2, loops=True)
            dense(k, "gcn2", b, [[(blocks("W2", p, q), a[:, p, :]) for p in range(2)] for q in range(2)], bias=d["cb2"], relu=True, parts=2)
            layer_norm(k, "lnc2", b, a, parts=2, gain=cols["g2"], shift=cols["be2"])
            dense(k, "gcn3", b, [[(blocks("W3", p, 0), a[:, p, :]) for p in range(2)]])
            aggregate(k, "c3", b, b, dinv, loops=True, bias=d["cb3"])
            layer_norm(k, "lnc3", b[:, 0:1, :], x3, gain=cols["g3"], shift=cols["be3"], add=True)


def general_sums(k, name, out, rows=None, weights=None, deg=None, h=None, scale=None, parts=1, loops=False, bias=None):
    nc, d = k.nc, k.dram
    with k.phase(name) as (sb, sem, block, hop):
        sd = sb("sd", [128, 2 * T], I32)
        am = sb("am", [128, T])
        row = sb("row", [128, T, parts * D])
        bases = sb("bases", [128, NW])
        dl = sb("dl", [128, T])
        sel = sb("sel", [128, T, WN])
        wsel = sb("wsel", [128, T, WN])
        acc = sb("acc", [128, parts, NP])
        node = sb("node", [BM, parts * D])
        degs = sb("degs", [1, NP])
        bt = sb("bt", [128, 1])
        bias_in, idx_in, made, table_ok, scaled, turned, copied, node_out, deg_in, ended = (sem(n) for n in (
            "bias_in", "idx_in", "made", "table_ok", "scaled", "turned", "copied", "node_out", "deg_in", "ended"))
        rows_in = k.general_rows.pop() if rows is None else None
        pe_ = Steps(sem("pe"), ["SUM"], 1)
        dve_ = Steps(sem("dve"), ["DL", "SEL", "WSEL", "ADD"] + (["DEG"] if deg is not None else []), 1)
        loaded = 16 * (1 + (weights is not None) + (rows is not None))
        last = dve_.per - 1

        @block.sync
        def _(sp):
            k.clear_old(sp)
            with sp.If(sp.value_load(k.fits[0:1, 0:1], min_val=0, max_val=1) == 0):
                if bias is not None:
                    sp.dma_start(bt[:, :], bias).then_inc(bias_in, 16)
                if rows is None:
                    for b in range(NB):
                        sp.wait_ge(copied, b + 1)
                        sp.dma_start(d[f"grows{parts}"][b * BM:(b + 1) * BM, :], node[:, :]).then_inc(node_out, 16)
                    sp.wait_ge(node_out, 16 * NB)
                    sp.sem_inc(table_ok, 1)
                with sp.Fori(0, NG) as c:
                    sp.wait_ge(dve_.sem, dve_.of(c * NW - 1, "ADD" if deg is None else "DEG"))
                    sp.dma_start(sd[:, :], d["sd"][bass.ds(c * S, S), :].rearrange("(p j) s -> p (j s)", j=T)).then_inc(idx_in, 16)
                    if weights is not None:
                        sp.dma_start(am[:, :], weights[bass.ds(c * S, S)].rearrange("(p j) -> p j", j=T)).then_inc(idx_in, 16)
                    if rows is not None:
                        sp.dma_start(row[:, :, :].rearrange("p j f -> p (j f)"),
                                     rows[bass.ds(c * S, S), :].rearrange("(p j) f -> p (j f)", j=T)).then_inc(idx_in, 16)
                if deg is not None:
                    sp.wait_ge(dve_.sem, dve_.of(NG * NW - 1, "DEG"))
                    sp.dma_start(deg.unsqueeze(0), degs[:, :]).then_inc(deg_in, 16)
                    sp.wait_ge(deg_in, 16)

        @block.gpsimd
        def _(pool):
            with pool.If(pool.value_load(k.fits[0:1, 0:1], min_val=0, max_val=1) == 0):
                pool.iota(bases[:, :], pattern=[[WN, NW]], base=0, channel_multiplier=0,
                          allow_small_or_imprecise_dtypes=True).then_inc(made, 1)
                pool.memset(acc[:, :, :], 0.0).then_inc(made, 1)
                pool.memset(degs[:, :], 0.0).then_inc(made, 1)
                if rows is None:
                    pool.wait_ge(table_ok, 1)
                    with pool.Fori(0, NG) as c:
                        pool.wait_ge(idx_in, c * loaded + loaded)
                        pool.sem_inc(hop["pool"], 1)
                        for j in range(T):
                            pool.indirect_dma_start(out=row[:, j, :], out_offset=None, in_=d[f"grows{parts}"],
                                                    in_offset=bass.IndirectOffsetOnAxis(ap=sd[:, 2 * j:2 * j + 1], axis=0)
                                                    ).then_inc(rows_in, 16)

        @block.tensor
        def _(pe):
            with pe.If(pe.value_load(k.fits[0:1, 0:1], min_val=0, max_val=1) == 0):
                if rows is None:
                    for b in range(NB):
                        if loops:
                            pe.wait_ge(scaled, parts)
                        if b:
                            pe.wait_ge(copied, b)
                        for p in range(parts):
                            m = nc.tensor.transpose(k.ps[0:BM, 3, p * D:(p + 1) * D], h[:, p, b * BM:(b + 1) * BM], k.ident[:, :])
                        m.then_inc(turned, 1)
                pe_.prime(pe)
                with pe.Fori(0, NG) as c:
                    if rows is None:
                        pe.wait_ge(rows_in, c * (16 * T) + 16 * T)
                    pe.sem_inc(hop["pe"], 1)
                    with pe.Fori(0, NW) as w:
                        t = c * NW + w
                        pe.wait_ge(dve_.sem, dve_.of(t, "WSEL"))
                        for p in range(parts):
                            for j in range(T):
                                m = nc.tensor.matmul(k.ps[:, p, 0:WN], row[:, j, p * D:(p + 1) * D], wsel[:, j, :],
                                                     start=j == 0, stop=j == T - 1)
                        if deg is not None:
                            for j in range(T):
                                m = nc.tensor.matmul(k.ps[0:1, 2, 0:WN], k.ones[:, 0:1], sel[:, j, :], start=j == 0, stop=j == T - 1)
                        m.then_inc(pe_.sem, 1)

        @block.scalar
        def _(act):
            if rows is None:
                with act.If(act.value_load(k.fits[0:1, 0:1], min_val=0, max_val=1) == 0):
                    for b in range(NB):
                        act.wait_ge(turned, b + 1)
                        if b:
                            act.wait_ge(node_out, 16 * b)
                        nc.scalar.activation(node[:, :], k.ps[0:BM, 3, 0:parts * D], ACT.Copy).then_inc(copied, 1)

        @block.vector
        def _(dve):
            with dve.If(dve.value_load(k.fits[0:1, 0:1], min_val=0, max_val=1) == 0):
                s = dve_.sem
                if loops:
                    for p in range(parts):
                        nc.vector.tensor_tensor(h[:, p, :], h[:, p, :], scale[:, :], ALU.mult).then_inc(scaled, 1)
                dve.wait_ge(made, 3)
                dve_.prime(dve)
                with dve.Fori(0, NG) as c:
                    dve.wait_ge(idx_in, c * loaded + loaded)
                    dve.sem_inc(hop["dve"], 1)
                    with dve.Fori(0, NW) as w:
                        t = c * NW + w
                        cols = bass.ds(w * WN, WN)
                        nc.vector.tensor_tensor(dl[:, :], sd[:, :].rearrange("p (j s) -> p s j", s=2)[:, 1, :],
                                                bc(bases[:, bass.ds(w, 1)], [128, T]), ALU.subtract).then_inc(s, 1)
                        dve.wait_ge(s, dve_.of(t, "DL"))
                        nc.vector.tensor_tensor(sel[:, :, :], bc(k.iota_wn[:, :].unsqueeze(1), [128, T, WN]),
                                                bc(dl[:, :].unsqueeze(2), [128, T, WN]), ALU.is_equal).then_inc(s, 1)
                        dve.wait_ge(s, dve_.of(t, "SEL"))
                        if weights is not None:
                            nc.vector.tensor_tensor(wsel[:, :, :], sel[:, :, :], bc(am[:, :].unsqueeze(2), [128, T, WN]),
                                                    ALU.mult).then_inc(s, 1)
                        else:
                            nc.vector.tensor_copy(wsel[:, :, :], sel[:, :, :]).then_inc(s, 1)
                        dve.wait_ge(pe_.sem, pe_.of(t, "SUM"))
                        nc.vector.tensor_tensor(acc[:, :, cols], acc[:, :, cols], k.ps[:, 0:parts, 0:WN], ALU.add).then_inc(s, 1)
                        if deg is not None:
                            nc.vector.tensor_tensor(degs[:, cols], degs[:, cols], k.ps[0:1, 2, 0:WN], ALU.add).then_inc(s, 1)
                        dve.wait_ge(s, dve_.of(t, "ADD" if deg is None else "DEG"))
                if bias is not None:
                    dve.wait_ge(bias_in, 16)
                if loops:
                    dve.wait_ge(turned, NB)
                n = 0
                for p in range(parts):
                    if rows is not None:
                        nc.vector.tensor_copy(out[:, :], acc[:, 0, :]).then_inc(ended, 1)
                        n += 1
                        continue
                    if loops:
                        nc.vector.tensor_tensor(acc[:, p, :], acc[:, p, :], h[:, p, :], ALU.add).then_inc(ended, 1)
                        n += 1
                        dve.wait_ge(ended, n)
                    nc.vector.tensor_tensor(out[:, p, :], acc[:, p, :], scale[:, :], ALU.mult).then_inc(ended, 1)
                    n += 1
                    if bias is not None:
                        dve.wait_ge(ended, n)
                        nc.vector.tensor_scalar(out[:, p, :], out[:, p, :], bt[:, 0:1], 0.0, ALU.add, ALU.max).then_inc(ended, 1)
                        n += 1
                dve.wait_ge(ended, n)


def general_attention(k, l):
    nc, d = k.nc, k.dram
    W = D if l == 0 else 2 * D
    HS = S // 2
    JH = T // 2
    SCALE = float(D) ** -0.5
    x0 = W - D
    table = d[f"lrows{l}"]
    with k.phase(f"ga{l}") as (sb, sem, block, hop):
        sd = sb("sd", [128, 2 * T], I32)
        geoS = sb("geoS", [KS, S], BF16)
        qt = sb("qt", [D, 2, WH])
        qs = sb("qs", [KS, WH], BF16)
        g = sb("g", [128, T, W])
        dxg = sb("dxg", [128, T, D + GK])
        bases = sb("bases", [128, NW])
        dl = sb("dl", [128, T])
        sel = sb("sel", [128, T, WN], BF16)
        off = sb("off", [128, T, H, WN], BF16)
        yT = sb("yT", [D, 2, S])
        p = sb("p", [WH, 2, HS])
        pT = sb("pT", [128, 2, JH * WH])
        most, total = sb("most", [WH, NW]), sb("total", [WH, NW])
        one, now = sb("one", [WH, 1]), sb("now", [WH, 1])
        agx = sb("agx", [D, NW, WH])
        agr = sb("agr", [WH, NW, D + GK])
        rows_in = k.general_rows.pop()
        made, out = sem("made"), sem("out")
        names = (["DL", "SEL", "OFF", "A", "B"], ["DL", "SEL", "OFF", "A", "B"], ["DL", "SEL", "OFF", "A", "B", "C", "D"])
        ps_ = range(3)
        idx_in = [sem(f"idx_in{n}") for n in ps_]
        q_in = [sem(f"q_in{n}") for n in ps_]
        dx_ok = [Steps(sem(f"dx_ok{n}"), ["DX"], 1) for n in ps_]
        turned = [Steps(sem(f"turned{n}"), ["T0", "T1", "T2"], 1) for n in ps_]
        yT_ok = [Steps(sem(f"yT_ok{n}"), ["T0", "T1", "T2"], 1) for n in ps_]
        scored = [Steps(sem(f"scored{n}"), ["S"] + (["PT", "SUM"] if n == 2 else []), 1) for n in ps_]
        exped = [Steps(sem(f"exped{n}"), ["E"] + (["P0", "P1"] if n == 2 else []), 1) for n in ps_]
        dve_ = [Steps(sem(f"dve{n}"), names[n], 1) for n in ps_]
        end = [v[-1] for v in names]
        between = sem("between")

        @block.sync
        def _(sp):
            k.clear_old(sp)
            with sp.If(sp.value_load(k.fits[0:1, 0:1], min_val=0, max_val=1) == 0):
                for n in ps_:
                    with sp.Fori(0, NG) as c:
                        sp.wait_ge(dve_[n].sem, dve_[n].of(c * NW - 1, end[n]))
                        if n:
                            sp.wait_ge(dve_[n - 1].sem, dve_[n - 1].of(NG * NW - 1, end[n - 1]))
                        sp.dma_start(sd[:, :], d["sd"][bass.ds(c * S, S), :].rearrange("(p j) s -> p (j s)", j=T)).then_inc(idx_in[n], 16)
                        sp.dma_start(dxg[:, :, D:D + GK], d["geo"][bass.ds(c * S, S), :].rearrange("(p j) f -> p j f", j=T)).then_inc(idx_in[n], 16)
                        sp.dma_start(geoS[:, :], d["geoS"][:, bass.ds(c * S, S)]).then_inc(idx_in[n], 16)
                        with sp.Fori(0, NW) as w:
                            t = c * NW + w
                            sp.wait_ge(dve_[n].sem, dve_[n].of(t - 1, end[n]))
                            sp.dma_start(qt[:, :, :], d["qt"][bass.ds(w, 1), :, :, :].rearrange("w k t n -> (w k) t n")).then_inc(q_in[n], 16)
                            sp.dma_start(qs[:, :], d["qs"][bass.ds(w, 1), :, :].rearrange("w k n -> (w k) n")).then_inc(q_in[n], 16)
                sp.wait_ge(dve_[2].sem, dve_[2].of(NG * NW - 1, end[2]))
                sp.dma_start(d["agx"].rearrange("w k n -> k w n"), agx[:, :, :]).then_inc(out, 16)
                sp.dma_start(d["agr"].rearrange("w m g -> m w g"), agr[:, :, :]).then_inc(out, 16)
                sp.wait_ge(out, 32)

        @block.gpsimd
        def _(pool):
            with pool.If(pool.value_load(k.fits[0:1, 0:1], min_val=0, max_val=1) == 0):
                pool.iota(bases[:, :], pattern=[[WN, NW]], base=0, channel_multiplier=0,
                          allow_small_or_imprecise_dtypes=True).then_inc(made, 1)
                pool.memset(most[:, :], FLOOR).then_inc(made, 1)
                pool.memset(total[:, :], 0.0).then_inc(made, 1)
                pool.memset(agx[:, :, :], 0.0).then_inc(made, 1)
                pool.memset(agr[:, :, :], 0.0).then_inc(made, 1)
                for n in ps_:
                    with pool.Fori(0, NG) as c:
                        pool.wait_ge(idx_in[n], c * 48 + 48)
                        pool.sem_inc(hop["pool"], 1)
                        for j in range(T):
                            pool.indirect_dma_start(out=g[:, j, :], out_offset=None, in_=table,
                                                    in_offset=bass.IndirectOffsetOnAxis(ap=sd[:, 2 * j:2 * j + 1], axis=0)
                                                    ).then_inc(rows_in, 16)

        @block.tensor
        def _(pe):
            with pe.If(pe.value_load(k.fits[0:1, 0:1], min_val=0, max_val=1) == 0):
                for n in ps_:
                    turned[n].prime(pe)
                    scored[n].prime(pe)
                for n in ps_:
                    with pe.Fori(0, NG) as c:
                        pe.wait_ge(dx_ok[n].sem, dx_ok[n].of(c, "DX"))
                        for q in range(3):
                            for i in range(4):
                                what, j = divmod(4 * q + i, T)
                                m = nc.tensor.transpose(k.ps[:, q, i * 128:(i + 1) * 128],
                                                        dxg[:, j, 0:D] if what else g[:, j, 0:D], k.ident[:, :])
                            m.then_inc(turned[n].sem, 1)
                        pe.wait_ge(yT_ok[n].sem, yT_ok[n].of(c, "T2"))
                        pe.sem_inc(hop["pe"], 1)
                        with pe.Fori(0, NW) as w:
                            t = c * NW + w
                            pe.wait_ge(q_in[n], t * 32 + 32)
                            pe.wait_ge(dve_[n].sem, dve_[n].of(t, "OFF"))
                            for half in range(2):
                                to = k.ps[0:WH, 3 + half, 0:HS]
                                for j in range(JH):
                                    nc.tensor.matmul(k.ps[0:WH, 3 + half, j * 128:(j + 1) * 128],
                                                     off[:, half * JH + j, :, :].rearrange("p h n -> p (h n)"), k.far[:, :],
                                                     start=j == 0, stop=False)
                                nc.tensor.matmul(to, qs[:, :], geoS[:, :].rearrange("f (p j) -> f j p", j=T)[:, half * JH:(half + 1) * JH, :],
                                                 start=False, stop=False)
                                for v in range(2):
                                    m = nc.tensor.matmul(to, qt[:, v, :], yT[:, v, half * HS:(half + 1) * HS], start=False, stop=v == 1)
                            m.then_inc(scored[n].sem, 1)
                            if n == 2:
                                pe.wait_ge(dve_[n].sem, dve_[n].of(t, "B"))
                                for j in range(T):
                                    m = nc.tensor.transpose(k.ps[:, 5 + j // JH, (j % JH) * WH:(j % JH + 1) * WH],
                                                            p[:, j // JH, (j % JH) * 128:(j % JH + 1) * 128], k.ident[0:WH, 0:WH])
                                m.then_inc(scored[n].sem, 1)
                                pe.wait_ge(exped[n].sem, exped[n].of(t, "P1"))
                                for j in range(T):
                                    nc.tensor.matmul(k.ps[:, 7, 0:WH], g[:, j, 0:D], pT[:, j // JH, (j % JH) * WH:(j % JH + 1) * WH],
                                                     start=j == 0, stop=j == T - 1)
                                for j in range(T):
                                    m = nc.tensor.matmul(k.ps[0:WH, 7, WH:WH + D + GK],
                                                         pT[:, j // JH, (j % JH) * WH:(j % JH + 1) * WH], dxg[:, j, :],
                                                         start=j == 0, stop=j == T - 1)
                                m.then_inc(scored[n].sem, 1)

        @block.scalar
        def _(act):
            with act.If(act.value_load(k.fits[0:1, 0:1], min_val=0, max_val=1) == 0):
                for n in ps_:
                    yT_ok[n].prime(act)
                    exped[n].prime(act)
                for n in ps_:
                    with act.Fori(0, NG) as c:
                        for q in range(3):
                            act.wait_ge(turned[n].sem, turned[n].of(c, f"T{q}"))
                            act.sem_inc(hop["act"], 1)
                            nc.scalar.activation(yT[:, :, :].rearrange("p v s -> p (v s)")[:, q * 512:(q + 1) * 512], k.ps[:, q, :],
                                                 ACT.Copy).then_inc(yT_ok[n].sem, 1)
                        if n:
                            with act.Fori(0, NW) as w:
                                t = c * NW + w
                                act.wait_ge(scored[n].sem, scored[n].of(t, "S"))
                                act.sem_inc(hop["act"], 1)
                                act.wait_ge(dve_[n].sem, dve_[n].of(t, "A"))
                                nc.scalar.activation(p[:, :, :], k.ps[0:WH, 3:5, 0:HS], ACT.Exp, bias=now[:, 0:1], scale=SCALE,
                                                     accum_out=one[:, 0:1]).then_inc(exped[n].sem, 1)
                                if n == 2:
                                    act.wait_ge(scored[n].sem, scored[n].of(t, "PT"))
                                    for half in range(2):
                                        nc.scalar.activation(pT[:, half, :], k.ps[:, 5 + half, 0:JH * WH], ACT.Copy).then_inc(exped[n].sem, 1)

        @block.vector
        def _(dve):
            with dve.If(dve.value_load(k.fits[0:1, 0:1], min_val=0, max_val=1) == 0):
                dve.wait_ge(made, 5)
                for n in ps_:
                    dx_ok[n].prime(dve)
                    dve_[n].prime(dve)
                for n in ps_:
                    s = dve_[n].sem
                    of = dve_[n].of
                    with dve.Fori(0, NG) as c:
                        dve.wait_ge(rows_in, c * (16 * T) + 16 * T * (n * NG + 1))
                        dve.wait_ge(idx_in[n], c * 48 + 48)
                        nc.vector.tensor_tensor(dxg[:, :, 0:D], g[:, :, x0:x0 + D], bc(dxg[:, :, D:D + 1], [128, T, D]),
                                                ALU.mult).then_inc(dx_ok[n].sem, 1)
                        with dve.Fori(0, NW) as w:
                            t = c * NW + w
                            col = bass.ds(w, 1)
                            nc.vector.tensor_tensor(dl[:, :], sd[:, :].rearrange("p (j s) -> p s j", s=2)[:, 1, :],
                                                    bc(bases[:, col], [128, T]), ALU.subtract).then_inc(s, 1)
                            dve.wait_ge(s, of(t, "DL"))
                            nc.vector.tensor_tensor(sel[:, :, :], bc(k.iota_wn[:, :].unsqueeze(1), [128, T, WN]),
                                                    bc(dl[:, :].unsqueeze(2), [128, T, WN]), ALU.is_equal).then_inc(s, 1)
                            dve.wait_ge(s, of(t, "SEL"))
                            nc.vector.tensor_scalar(off[:, :, :, :], bc(sel[:, :, :].unsqueeze(2), [128, T, H, WN]), -1.0, None,
                                                    ALU.add).then_inc(s, 1)
                            if n == 0:
                                dve.wait_ge(scored[n].sem, scored[n].of(t, "S"))
                                nc.vector.tensor_reduce(one[:, 0:1], k.ps[0:WH, 3:5, 0:HS], AX.XY, ALU.max).then_inc(s, 1)
                                dve.wait_ge(s, of(t, "A"))
                                nc.vector.tensor_tensor(most[:, col], most[:, col], one[:, 0:1], ALU.max).then_inc(s, 1)
                            else:
                                nc.vector.tensor_copy(now[:, 0:1], most[:, col]).then_inc(s, 1)
                                dve.wait_ge(exped[n].sem, exped[n].of(t, "E"))
                            if n == 1:
                                nc.vector.tensor_tensor(total[:, col], total[:, col], one[:, 0:1], ALU.add).then_inc(s, 1)
                            elif n == 2:
                                nc.vector.tensor_tensor(p[:, :, :].rearrange("m v s -> m (v s)"), p[:, :, :].rearrange("m v s -> m (v s)"),
                                                        bc(total[:, col], [WH, S]), ALU.mult).then_inc(s, 1)
                                dve.wait_ge(scored[n].sem, scored[n].of(t, "SUM"))
                                nc.vector.tensor_tensor(agx[:, col, :].rearrange("k w n -> k (w n)"),
                                                        agx[:, col, :].rearrange("k w n -> k (w n)"),
                                                        k.ps[:, 7, 0:WH], ALU.add).then_inc(s, 1)
                                nc.vector.tensor_tensor(agr[:, col, :].rearrange("k w n -> k (w n)"),
                                                        agr[:, col, :].rearrange("k w n -> k (w n)"),
                                                        k.ps[0:WH, 7, WH:WH + D + GK], ALU.add).then_inc(s, 1)
                            dve.wait_ge(s, of(t, end[n]))
                            dve.sem_inc(hop["dve"], 1)
                    if n == 0:
                        nc.vector.tensor_scalar(most[:, :], most[:, :], -SCALE, None, ALU.mult).then_inc(between, 1)
                        dve.wait_ge(between, 1)
                    elif n == 1:
                        nc.vector.tensor_scalar(total[:, :], total[:, :], 1e-16, float(H), ALU.add, ALU.mult).then_inc(between, 1)
                        dve.wait_ge(between, 2)
                        nc.vector.reciprocal(total[:, :], total[:, :]).then_inc(between, 1)
                        dve.wait_ge(between, 3)


def gnn_kernel(nc, dram, out):
    with ExitStack() as ctx:
        k = Kit(nc, dram, ctx)
        prepare(k)
        with ExitStack() as l0:
            hT = l0.enter_context(nc.sbuf_tensor("l0_hT", [128, 1, NP], F32))
            x3 = k.xT[:, :].unsqueeze(1)
            layer_norm(k, "ln0", x3, hT, relu=True)
            d = dram
            node_rows(k, "rows0", hT[:, 0, :], [(0, D, d["W_node"]), (D, D // 2, d["aW1"][0:D // 2, :]),
                                                (2 * D, D // 2, d["aW1"][D // 2:D, :])], 3 * D,
                      [(d["rows0"], 0, 2 * D), (d["rows0d"], 2 * D, D)])
            with ExitStack() as l0a:
                a_all = l0a.enter_context(nc.sbuf_tensor("a_all", [128, NC, 4, AH], F32))
                edge_messages(k, a_all)
                edge_softmax(k, a_all)
            aggT = l0.enter_context(nc.sbuf_tensor("l0_aggT", [128, NP], F32))
            window_sums(k, aggT)
            general_sums(k, "gs", aggT, rows=d["msg"], weights=d["am"], deg=d["deg"])
            dense(k, "out0", hT, [[(d["W_out"], aggT)]], add=hT[:, 0, :])
            layer_norm(k, "ln0b", hT, x3, add=True)
        if STOP > 1:
            attention_layers(k)
        if STOP > 2:
            adjacency_layers(k)
        with k.phase("end") as (sb, sem, block, hop):
            done = sem("done")

            @block.sync
            def _(sp):
                k.clear_old(sp)
                sp.dma_start(out, k.xT[:, :]).then_inc(done, 16)
                sp.wait_ge(done, 16)


STOP = 9


def kernel(**inputs):
    import numpy as np
    import concourse.bacc as bacc
    from concourse.bass_utils import run_bass_kernel_spmd as run

    a = {n: np.ascontiguousarray(v) for n, v in inputs.items()}
    f32 = np.float32
    src = np.zeros(EW, np.int32)
    dst = np.full(EW, NP - 1, np.int32)
    src[:E], dst[:E] = a["src"], a["dst"]

    def chunked(v):
        full = np.zeros((EP, v.shape[1]), f32)
        full[:E] = v
        return np.ascontiguousarray(full.reshape(NC, 128, 4, -1).transpose(0, 3, 2, 1)).reshape(NC, v.shape[1], CE)

    geo = np.zeros((EW, GK), f32)
    geo[:E, 0:1], geo[:E, 1:1 + GEO] = a["edge_weight1"], a["edge_attr_20"]
    xT = np.zeros((D, NP), f32)
    xT[:, :N] = a["x"].T
    p0, p1, p2, p3 = "L0_gnn_", "L1_gnn_", "L2_gnn_", "L3_gnn_"
    col = lambda v: np.ascontiguousarray(v.reshape(-1, D).T)
    host = {
        "xT": xT, "sd": np.stack([src, dst], 1), "dst": dst, "geo": geo, "geoT": np.ascontiguousarray(geo.T),
        "ea32": chunked(a["edge_attr_32"]), "sh16": chunked(a["edge_attr_16"]),
        "em_bias": np.stack([a[p0 + n] for n in ("b1", "b2", "ab1", "ab2")], 1),
        "b3": a[p0 + "b3"], "ab3": a[p0 + "ab3"],
        "W_eeT": np.ascontiguousarray(np.concatenate([a[p1 + "W_ee"], a[p1 + "b_ee"][None]], 0).T),
        "WkT": np.ascontiguousarray(a[p1 + "Wk"].transpose(0, 2, 1)),
        "hb": np.ascontiguousarray(np.stack([a[p1 + n].reshape(3, H, D) for n in ("bq", "bk", "bv", "be")], 1).transpose(0, 3, 1, 2)),
        "bs": np.stack([a[p1 + "bs"][0], a[p1 + "bs"][1], a[p1 + "bs"][2], a[p1 + "b_res"]], 1), "b_ctr": col(a[p1 + "b_ctr"]),
        "b20": col(a[p2 + "b0"]), "b21": col(a[p2 + "b1"]),
    }
    for n in ("W_node", "fc1", "fc2", "fc3", "W_sh", "aW1", "aW2", "aW3", "W_out"):
        host[n] = a[p0 + n]
    for n in ("W_res", "Wq", "Wv", "We", "Ws", "W_ctr"):
        host[n] = a[p1 + n]
    for n in ("W_self0", "W_neigh0", "W_self1", "W_neigh1"):
        host[n + "T"] = np.ascontiguousarray(a[p2 + n].T)
    for n in ("W1", "W2", "W3"):
        host["g" + n] = a[p3 + n]
    for n in ("b1", "g1", "be1", "b2", "g2", "be2", "b3", "g3", "be3"):
        host["c" + n] = col(a[p3 + n])

    nc = bacc.Bacc("TRN2", target_bir_lowering=False, num_devices=1)
    arrays, dram = {}, {}
    for n, v in host.items():
        arrays["in_" + n] = np.ascontiguousarray(v)
        dram[n] = nc.dram_tensor("in_" + n, v.shape, mybir.dt.from_np(v.dtype), kind="ExternalInput").ap()
    for n, shape, dt in (("rows0", (NP, 2 * D), F32), ("rows0d", (NP, D), F32), ("msg", (EW, D), F32), ("am", (EW,), F32),
                         ("adj", (NW, BM, NB * WN), BF16), ("deg", (NP,), F32), ("grows1", (NP, D), F32), ("grows2", (NP, 2 * D), F32),
                         ("lrows0", (NP, D), F32), ("lrows1", (NP, 2 * D), F32), ("lrows2", (NP, 2 * D), F32),
                         ("qt", (NW, D, 2, WH), F32), ("qs", (NW, KS, WH), BF16), ("geoS", (KS, EW), BF16), ("agx", (NW, D, WH), F32), ("agr", (NW, WH, D + GK), F32)):
        dram[n] = nc.dram_tensor("s_" + n, shape, dt).ap()
    out = nc.dram_tensor("out_T", (D, NP), F32, kind="ExternalOutput").ap()
    gnn_kernel(nc, dram, out)
    got = run(nc, [arrays], core_ids=[0]).results[0]["out_T"]
    return np.ascontiguousarray(got[:, :N].T)
```
